# Optimizing a Trainium2 kernel written in Bass

```python
import numpy as np
import jax
import jax.numpy as jnp

def _softmax(x, axis=-1):
    return jax.nn.softmax(x, axis=axis)

def _gelu(x):
    return jax.nn.gelu(x, approximate=True)

def _silu(x):
    return jax.nn.silu(x)

def _sigmoid(x):
    return jax.nn.sigmoid(x)

def _layernorm(x, axis=-1, eps=1e-05):
    m = jnp.mean(x, axis=axis, keepdims=True)
    v = jnp.var(x, axis=axis, keepdims=True)
    return (x - m) / jnp.sqrt(v + eps)

def _scatter_add(tgt, idx, src, axis=0):
    return tgt.at[idx].add(src)

def _segment_sum(src, seg, n):
    return jax.ops.segment_sum(src, seg, n)
kernel_name = 'mk_prb_d1_jaxref_r4_90f3e0'

def setup_inputs(seed: int=0):
    np.random.seed(seed)
    _w = jnp.asarray

    def _L0_attn_setup():
        import jax, jax.numpy as jnp
        import numpy as np
        B, L, C, H = (8, 512, 256, 16)
        HID = 4 * C

        def _rope(x):
            b, n, c = x.shape
            k_max = c // 2
            theta = 1.0 / 10000.0 ** (jnp.arange(k_max, dtype=jnp.float32) / k_max)
            cos_t, sin_t = (jnp.cos(theta), jnp.sin(theta))
            xr = x.reshape(b, n, k_max, 2)
            re = xr[..., 0] * cos_t - xr[..., 1] * sin_t
            im = xr[..., 0] * sin_t + xr[..., 1] * cos_t
            return jnp.stack((re, im), axis=-1).reshape(b, n, c)

        def _dwconv(x_bcl, w, bias):
            y = jax.lax.conv_general_dilated(x_bcl, w, (1,), [(1, 1)], dimension_numbers=('NCH', 'OIH', 'NCH'), feature_group_count=x_bcl.shape[1])
            return y + bias[None, :, None]

        def _ln(x, g, b, eps=1e-05):
            mu = x.mean(-1, keepdims=True)
            var = ((x - mu) ** 2).mean(-1, keepdims=True)
            return (x - mu) * jax.lax.rsqrt(var + eps) * g + b

        def _mlla_forward(x, cpe1_w, cpe1_b, norm1_g, norm1_b, in_w, in_b, actp_w, actp_b, dwc_w, dwc_b, qk_w, qk_b, lepe_w, lepe_b, out_w, out_b, cpe2_w, cpe2_b, norm2_g, norm2_b, fc1_w, fc1_b, fc2_w, fc2_b):
            b, n, c = x.shape
            h, d = (H, c // H)
            x = x + _dwconv(x.transpose(0, 2, 1), cpe1_w, cpe1_b).transpose(0, 2, 1)
            shortcut = x
            xn = _ln(x, norm1_g, norm1_b)
            act_res = jax.nn.silu(xn @ actp_w + actp_b)
            xi = xn @ in_w + in_b
            xi = jax.nn.silu(_dwconv(xi.transpose(0, 2, 1), dwc_w, dwc_b)).transpose(0, 2, 1)
            qk = xi @ qk_w + qk_b
            q = jax.nn.elu(qk[..., :c]) + 1.0
            k = jax.nn.elu(qk[..., c:]) + 1.0
            q_rope = _rope(q).reshape(b, n, h, d).transpose(0, 2, 1, 3)
            k_rope = _rope(k).reshape(b, n, h, d).transpose(0, 2, 1, 3)
            qh = q.reshape(b, n, h, d).transpose(0, 2, 1, 3)
            kh = k.reshape(b, n, h, d).transpose(0, 2, 1, 3)
            vh = xi.reshape(b, n, h, d).transpose(0, 2, 1, 3)
            k_mean = kh.mean(axis=2, keepdims=True)
            z = 1.0 / (jnp.einsum('bhnd,bhmd->bhnm', qh, k_mean) + 1e-06)
            kv = jnp.einsum('bhnd,bhne->bhde', k_rope, vh) * (1.0 / n)
            attn = jnp.einsum('bhnd,bhde->bhne', q_rope, kv) * z
            attn = attn.transpose(0, 2, 1, 3).reshape(b, n, c)
            v_bcl = vh.transpose(0, 2, 1, 3).reshape(b, n, c).transpose(0, 2, 1)
            attn = attn + _dwconv(v_bcl, lepe_w, lepe_b).transpose(0, 2, 1)
            x = shortcut + attn * act_res @ out_w + out_b
            x = x + _dwconv(x.transpose(0, 2, 1), cpe2_w, cpe2_b).transpose(0, 2, 1)
            xn2 = _ln(x, norm2_g, norm2_b)
            mlp = jax.nn.gelu(xn2 @ fc1_w + fc1_b, approximate=False) @ fc2_w + fc2_b
            return x + mlp
        key = jax.random.key(seed)
        ks = jax.random.split(key, 12)

        def nrm(k, shape, scale=0.02):
            return jax.random.normal(k, shape, jnp.float32) * scale
        return {'x': jax.random.normal(ks[0], (B, L, C), jnp.float32), 'cpe1_w': nrm(ks[1], (C, 1, 3), 0.1), 'cpe1_b': jnp.zeros((C,), jnp.float32), 'norm1_g': jnp.ones((C,), jnp.float32), 'norm1_b': jnp.zeros((C,), jnp.float32), 'in_w': nrm(ks[2], (C, C)), 'in_b': jnp.zeros((C,), jnp.float32), 'actp_w': nrm(ks[3], (C, C)), 'actp_b': jnp.zeros((C,), jnp.float32), 'dwc_w': nrm(ks[4], (C, 1, 3), 0.1), 'dwc_b': jnp.zeros((C,), jnp.float32), 'qk_w': nrm(ks[5], (C, 2 * C)), 'qk_b': jnp.zeros((2 * C,), jnp.float32), 'lepe_w': nrm(ks[6], (C, 1, 3), 0.1), 'lepe_b': jnp.zeros((C,), jnp.float32), 'out_w': nrm(ks[7], (C, C)), 'out_b': jnp.zeros((C,), jnp.float32), 'cpe2_w': nrm(ks[8], (C, 1, 3), 0.1), 'cpe2_b': jnp.zeros((C,), jnp.float32), 'norm2_g': jnp.ones((C,), jnp.float32), 'norm2_b': jnp.zeros((C,), jnp.float32), 'fc1_w': nrm(ks[9], (C, HID)), 'fc1_b': jnp.zeros((HID,), jnp.float32), 'fc2_w': nrm(ks[10], (HID, C)), 'fc2_b': jnp.zeros((C,), jnp.float32)}
    _L0_attn_in = _L0_attn_setup()

    def _L0_ffn_setup():
        import jax, jax.numpy as jnp
        import numpy as np
        D_IN, D_HID = (256, 1024)

        def _ternary(key, shape):
            return jax.random.randint(key, shape, -1, 2).astype(jnp.float32)

        def _tlin(x, w, s):
            return jnp.einsum('bsi,oi->bso', x, w) * s
        key = jax.random.key(seed)
        ks = jax.random.split(key, 12)
        inv = lambda fan: 1.0 / np.sqrt(fan).astype(np.float32)
        return {'x': jax.random.normal(ks[0], (4, 512, D_IN), dtype=jnp.float32), 'w1_w': _ternary(ks[1], (D_HID, D_IN)), 'w1_s': jax.random.uniform(ks[2], (D_HID,), dtype=jnp.float32) * inv(D_IN), 'w2_w': _ternary(ks[3], (D_HID, D_IN)), 'w2_s': jax.random.uniform(ks[4], (D_HID,), dtype=jnp.float32) * inv(D_IN), 'h1_w': _ternary(ks[5], (D_HID, D_HID)), 'h1_s': jax.random.uniform(ks[6], (D_HID,), dtype=jnp.float32) * inv(D_HID), 'h2_w': _ternary(ks[7], (D_HID, D_HID)), 'h2_s': jax.random.uniform(ks[8], (D_HID,), dtype=jnp.float32) * inv(D_HID), 'w3_w': _ternary(ks[9], (D_IN, D_HID)), 'w3_s': jax.random.uniform(ks[10], (D_IN,), dtype=jnp.float32) * inv(D_HID)}
    _L0_ffn_in = _L0_ffn_setup()
    _d = {'L0_attn_x': _L0_attn_in['x'], 'L0_attn_cpe1_w': _L0_attn_in['cpe1_w'], 'L0_attn_cpe1_b': _L0_attn_in['cpe1_b'], 'L0_attn_norm1_g': _L0_attn_in['norm1_g'], 'L0_attn_norm1_b': _L0_attn_in['norm1_b'], 'L0_attn_in_w': _L0_attn_in['in_w'], 'L0_attn_in_b': _L0_attn_in['in_b'], 'L0_attn_actp_w': _L0_attn_in['actp_w'], 'L0_attn_actp_b': _L0_attn_in['actp_b'], 'L0_attn_dwc_w': _L0_attn_in['dwc_w'], 'L0_attn_dwc_b': _L0_attn_in['dwc_b'], 'L0_attn_qk_w': _L0_attn_in['qk_w'], 'L0_attn_qk_b': _L0_attn_in['qk_b'], 'L0_attn_lepe_w': _L0_attn_in['lepe_w'], 'L0_attn_lepe_b': _L0_attn_in['lepe_b'], 'L0_attn_out_w': _L0_attn_in['out_w'], 'L0_attn_out_b': _L0_attn_in['out_b'], 'L0_attn_cpe2_w': _L0_attn_in['cpe2_w'], 'L0_attn_cpe2_b': _L0_attn_in['cpe2_b'], 'L0_attn_norm2_g': _L0_attn_in['norm2_g'], 'L0_attn_norm2_b': _L0_attn_in['norm2_b'], 'L0_attn_fc1_w': _L0_attn_in['fc1_w'], 'L0_attn_fc1_b': _L0_attn_in['fc1_b'], 'L0_attn_fc2_w': _L0_attn_in['fc2_w'], 'L0_attn_fc2_b': _L0_attn_in['fc2_b'], 'L0_ffn_w1_w': _L0_ffn_in['w1_w'], 'L0_ffn_w1_s': _L0_ffn_in['w1_s'], 'L0_ffn_w2_w': _L0_ffn_in['w2_w'], 'L0_ffn_w2_s': _L0_ffn_in['w2_s'], 'L0_ffn_h1_w': _L0_ffn_in['h1_w'], 'L0_ffn_h1_s': _L0_ffn_in['h1_s'], 'L0_ffn_h2_w': _L0_ffn_in['h2_w'], 'L0_ffn_h2_s': _L0_ffn_in['h2_s'], 'L0_ffn_w3_w': _L0_ffn_in['w3_w'], 'L0_ffn_w3_s': _L0_ffn_in['w3_s']}
    _x0 = _d['L0_attn_x']
    _d['L0_attn_x'] = jax.random.normal(jax.random.fold_in(jax.random.key(seed), 1), (2, 2048, 256), dtype=_x0.dtype)
    del _x0
    return _d

def reference(L0_attn_x, L0_attn_cpe1_w, L0_attn_cpe1_b, L0_attn_norm1_g, L0_attn_norm1_b, L0_attn_in_w, L0_attn_in_b, L0_attn_actp_w, L0_attn_actp_b, L0_attn_dwc_w, L0_attn_dwc_b, L0_attn_qk_w, L0_attn_qk_b, L0_attn_lepe_w, L0_attn_lepe_b, L0_attn_out_w, L0_attn_out_b, L0_attn_cpe2_w, L0_attn_cpe2_b, L0_attn_norm2_g, L0_attn_norm2_b, L0_attn_fc1_w, L0_attn_fc1_b, L0_attn_fc2_w, L0_attn_fc2_b, L0_ffn_w1_w, L0_ffn_w1_s, L0_ffn_w2_w, L0_ffn_w2_s, L0_ffn_h1_w, L0_ffn_h1_s, L0_ffn_h2_w, L0_ffn_h2_s, L0_ffn_w3_w, L0_ffn_w3_s):

    def _L0_attn_ref(x, cpe1_w, cpe1_b, norm1_g, norm1_b, in_w, in_b, actp_w, actp_b, dwc_w, dwc_b, qk_w, qk_b, lepe_w, lepe_b, out_w, out_b, cpe2_w, cpe2_b, norm2_g, norm2_b, fc1_w, fc1_b, fc2_w, fc2_b):
        import jax, jax.numpy as jnp
        import numpy as np
        B, L, C, H = (8, 512, 256, 16)
        HID = 4 * C

        def _rope(x):
            b, n, c = x.shape
            k_max = c // 2
            theta = 1.0 / 10000.0 ** (jnp.arange(k_max, dtype=jnp.float32) / k_max)
            cos_t, sin_t = (jnp.cos(theta), jnp.sin(theta))
            xr = x.reshape(b, n, k_max, 2)
            re = xr[..., 0] * cos_t - xr[..., 1] * sin_t
            im = xr[..., 0] * sin_t + xr[..., 1] * cos_t
            return jnp.stack((re, im), axis=-1).reshape(b, n, c)

        def _dwconv(x_bcl, w, bias):
            y = jax.lax.conv_general_dilated(x_bcl, w, (1,), [(1, 1)], dimension_numbers=('NCH', 'OIH', 'NCH'), feature_group_count=x_bcl.shape[1])
            return y + bias[None, :, None]

        def _ln(x, g, b, eps=1e-05):
            mu = x.mean(-1, keepdims=True)
            var = ((x - mu) ** 2).mean(-1, keepdims=True)
            return (x - mu) * jax.lax.rsqrt(var + eps) * g + b

        def _mlla_forward(x, cpe1_w, cpe1_b, norm1_g, norm1_b, in_w, in_b, actp_w, actp_b, dwc_w, dwc_b, qk_w, qk_b, lepe_w, lepe_b, out_w, out_b, cpe2_w, cpe2_b, norm2_g, norm2_b, fc1_w, fc1_b, fc2_w, fc2_b):
            b, n, c = x.shape
            h, d = (H, c // H)
            x = x + _dwconv(x.transpose(0, 2, 1), cpe1_w, cpe1_b).transpose(0, 2, 1)
            shortcut = x
            xn = _ln(x, norm1_g, norm1_b)
            act_res = jax.nn.silu(xn @ actp_w + actp_b)
            xi = xn @ in_w + in_b
            xi = jax.nn.silu(_dwconv(xi.transpose(0, 2, 1), dwc_w, dwc_b)).transpose(0, 2, 1)
            qk = xi @ qk_w + qk_b
            q = jax.nn.elu(qk[..., :c]) + 1.0
            k = jax.nn.elu(qk[..., c:]) + 1.0
            q_rope = _rope(q).reshape(b, n, h, d).transpose(0, 2, 1, 3)
            k_rope = _rope(k).reshape(b, n, h, d).transpose(0, 2, 1, 3)
            qh = q.reshape(b, n, h, d).transpose(0, 2, 1, 3)
            kh = k.reshape(b, n, h, d).transpose(0, 2, 1, 3)
            vh = xi.reshape(b, n, h, d).transpose(0, 2, 1, 3)
            k_mean = kh.mean(axis=2, keepdims=True)
            z = 1.0 / (jnp.einsum('bhnd,bhmd->bhnm', qh, k_mean) + 1e-06)
            kv = jnp.einsum('bhnd,bhne->bhde', k_rope, vh) * (1.0 / n)
            attn = jnp.einsum('bhnd,bhde->bhne', q_rope, kv) * z
            attn = attn.transpose(0, 2, 1, 3).reshape(b, n, c)
            v_bcl = vh.transpose(0, 2, 1, 3).reshape(b, n, c).transpose(0, 2, 1)
            attn = attn + _dwconv(v_bcl, lepe_w, lepe_b).transpose(0, 2, 1)
            x = shortcut + attn * act_res @ out_w + out_b
            x = x + _dwconv(x.transpose(0, 2, 1), cpe2_w, cpe2_b).transpose(0, 2, 1)
            xn2 = _ln(x, norm2_g, norm2_b)
            mlp = jax.nn.gelu(xn2 @ fc1_w + fc1_b, approximate=False) @ fc2_w + fc2_b
            return x + mlp
        return _mlla_forward(x, cpe1_w, cpe1_b, norm1_g, norm1_b, in_w, in_b, actp_w, actp_b, dwc_w, dwc_b, qk_w, qk_b, lepe_w, lepe_b, out_w, out_b, cpe2_w, cpe2_b, norm2_g, norm2_b, fc1_w, fc1_b, fc2_w, fc2_b)

    def _L0_ffn_ref(x, w1_w, w1_s, w2_w, w2_s, h1_w, h1_s, h2_w, h2_s, w3_w, w3_s):
        import jax, jax.numpy as jnp
        import numpy as np
        D_IN, D_HID = (256, 1024)

        def _ternary(key, shape):
            return jax.random.randint(key, shape, -1, 2).astype(jnp.float32)

        def _tlin(x, w, s):
            return jnp.einsum('bsi,oi->bso', x, w) * s
        h = jax.nn.silu(_tlin(x, w1_w, w1_s)) * _tlin(x, w2_w, w2_s)
        h = jax.nn.gelu(_tlin(h, h1_w, h1_s), approximate=False)
        h = jax.nn.gelu(_tlin(h, h2_w, h2_s), approximate=False)
        return _tlin(h, w3_w, w3_s)
    x = L0_attn_x
    xn = _layernorm(x, axis=-1)
    x = x + _L0_attn_ref(xn, L0_attn_cpe1_w, L0_attn_cpe1_b, L0_attn_norm1_g, L0_attn_norm1_b, L0_attn_in_w, L0_attn_in_b, L0_attn_actp_w, L0_attn_actp_b, L0_attn_dwc_w, L0_attn_dwc_b, L0_attn_qk_w, L0_attn_qk_b, L0_attn_lepe_w, L0_attn_lepe_b, L0_attn_out_w, L0_attn_out_b, L0_attn_cpe2_w, L0_attn_cpe2_b, L0_attn_norm2_g, L0_attn_norm2_b, L0_attn_fc1_w, L0_attn_fc1_b, L0_attn_fc2_w, L0_attn_fc2_b) + _L0_ffn_ref(xn, L0_ffn_w1_w, L0_ffn_w1_s, L0_ffn_w2_w, L0_ffn_w2_s, L0_ffn_h1_w, L0_ffn_h1_s, L0_ffn_h2_w, L0_ffn_h2_s, L0_ffn_w3_w, L0_ffn_w3_s)
    return x

_drawn_inputs = setup_inputs


def setup_inputs(seed=0):
    import zlib

    import numpy as np

    out = dict(_drawn_inputs(seed))
    spreads = {'L0_attn_cpe1_b': (0.0, 0.1),
     'L0_attn_norm1_g': (1.0, 0.2),
     'L0_attn_norm1_b': (0.0, 0.1),
     'L0_attn_in_b': (0.0, 0.1),
     'L0_attn_actp_b': (0.0, 0.1),
     'L0_attn_dwc_b': (0.0, 0.1),
     'L0_attn_qk_b': (0.0, 0.1),
     'L0_attn_lepe_b': (0.0, 0.1),
     'L0_attn_out_b': (0.0, 0.1),
     'L0_attn_cpe2_b': (0.0, 0.1),
     'L0_attn_norm2_g': (1.0, 0.2),
     'L0_attn_norm2_b': (0.0, 0.1),
     'L0_attn_fc1_b': (0.0, 0.1),
     'L0_attn_fc2_b': (0.0, 0.1)}
    factors = {}
    for name, (base, spread) in spreads.items():
        noise = np.random.default_rng([zlib.crc32(name.encode()), seed]).standard_normal(out[name].shape)
        drawn = base * np.exp(spread * noise) if base else spread * noise
        out[name] = jnp.asarray(drawn.astype(out[name].dtype))
    for name, factor in factors.items():
        out[name] = (out[name] * factor).astype(out[name].dtype)
    return out
```

```python
from contextlib import ExitStack

import numpy as np

import concourse.bass as bass
from concourse import mybir

F32 = mybir.dt.float32
F32R = mybir.dt.float32r
I32 = mybir.dt.int32
ALU = mybir.AluOpType
ACT = mybir.ActivationFunctionType
AX_X = mybir.AxisListType.X

P = 128
BATCHES, N, C = 2, 2048, 256
KC = C // P
HEADS = 16
D = C // HEADS
HID = 4 * C
KH = HID // P
TOK = 512
SUB = TOK // P
NT = N // TOK
TILES = BATCHES * NT
HQ = 32
EPS = 1e-5
Z_EPS = 1e-6

PARAMS = {}
for _name, _width in (
    ("cpe1_w0", KC), ("cpe1_w1", KC), ("cpe1_w2", KC), ("cpe1_b", KC),
    ("norm1_g", KC), ("norm1_b", KC), ("in_b", KC), ("actp_b", KC),
    ("dwc_w0", KC), ("dwc_w1", KC), ("dwc_w2", KC), ("dwc_b", KC), ("q_b", KC),
    ("lepe_w0", KC), ("lepe_w1", KC), ("lepe_w2", KC), ("lepe_b", KC), ("out_b", KC),
    ("cpe2_w0", KC), ("cpe2_w1", KC), ("cpe2_w2", KC), ("cpe2_b", KC),
    ("norm2_g", KC), ("norm2_b", KC), ("fc1_b", KH), ("fc2_b", KC),
    ("w1_s", KH), ("w2_s", KH), ("h1_s", KH), ("h2_s", KH), ("w3_s", KC),
):
    PARAMS[_name] = (sum(w for _, w in PARAMS.values()), _width)
N_PARAMS = sum(w for _, w in PARAMS.values())

A_COLS = {"actp": 0, "in": C, "q": 2 * C, "k": 3 * C, "out": 4 * C}
A_WIDTH = 5 * C


def constants():
    identity = np.eye(P, dtype=np.float32)
    head_of = np.arange(C) // D
    same_head = np.equal.outer(np.arange(P) // D, np.arange(P) // D).astype(np.float32)
    head_rows = np.zeros((P, KC, HQ), np.float32)
    expand = np.zeros((P, KC, P), np.float32)
    for c in range(C):
        head_rows[c % P, c // P, head_of[c]] = 1.0
        for q in range(P // HQ):
            expand[q * HQ + head_of[c], c // P, c % P] = 1.0
    pairs = C // 2
    theta = 1.0 / np.float32(10000.0) ** (np.arange(pairs, dtype=np.float32) / np.float32(pairs))
    cos, sin = np.cos(theta), np.sin(theta)
    rope = np.zeros((P, 2, KC, P), np.float32)
    for j in range(pairs):
        e, chunk = (2 * j) % P, (2 * j) // P
        rot = np.array([[cos[j], -sin[j]], [sin[j], cos[j]]], np.float32)
        rope[e:e + 2, 1, chunk, e:e + 2] = rot
        rope[e:e + 2, 0, chunk, e:e + 2] = rot.T
    return np.concatenate([identity, same_head, head_rows.reshape(P, -1), expand.reshape(P, -1),
                           rope.reshape(P, -1)], axis=1)


CONST_COLS = {"identity": (0, P), "same_head": (P, P), "head_rows": (2 * P, KC * HQ),
              "expand": (2 * P + KC * HQ, KC * P), "rope": (2 * P + KC * HQ + KC * P, 2 * KC * P)}
N_CONST = 2 * P + KC * HQ + 3 * KC * P


def attention_part(nc, x, params, consts, k_bias, w_attn, w_fc1, w_fc2, xn_scratch, y_scratch):
    with ExitStack() as ctx:
        def sb(name, shape, dt=F32):
            return ctx.enter_context(nc.sbuf_tensor(name, shape, dt))

        def sem(name):
            return ctx.enter_context(nc.semaphore(name))

        pairs = [ctx.enter_context(nc.psum_tensor(f"banks{i}", [P, 2, TOK], F32)) for i in range(4)]

        def as_tokens(pair):
            return pair[:].rearrange("p a b -> p (a b)").rearrange("p (s c) -> p s c", s=SUB)

        xh = sb("xh", [P, KC, N + 2])
        x0 = sb("x0", [P, KC, N])
        act = sb("act", [P, KC, N])
        ph = sb("ph", [P, KC, N + 2])
        vh = sb("vh", [P, KC, N + 2])
        wa_hi, wa_lo = sb("wa_hi", [P, KC, A_WIDTH], F32R), sb("wa_lo", [P, KC, A_WIDTH], F32R)
        wf1_hi, wf1_lo = sb("wf1_hi", [P, KC, HID], F32R), sb("wf1_lo", [P, KC, HID], F32R)
        wf2_hi, wf2_lo = sb("wf2_hi", [P, KH, C], F32R), sb("wf2_lo", [P, KH, C], F32R)
        prm = sb("prm", [P, N_PARAMS])
        cst = sb("cst", [P, N_CONST])
        kb = sb("kb", [P, C])
        w1p = sb("w1p", [P, 2, KC])
        small = sb("small", [P, 4, SUB])
        xt = sb("xt", [P, 2, SUB, C])
        xnt = sb("xnt", [P, SUB, C])
        xnf = sb("xnf", [P, KC, TOK])
        p_hi, p_lo = sb("p_hi", [P, KC, TOK], F32R), sb("p_lo", [P, KC, TOK], F32R)
        h_hi, h_lo = sb("h_hi", [P, KH, TOK], F32R), sb("h_lo", [P, KH, TOK], F32R)
        conv = sb("conv", [P, KC, TOK])
        kt = sb("kt", [P, SUB, C])
        vt = sb("vt", [P, SUB, KC, P + 1])
        st = {x: sb(f"st_{x}", [P, SUB, 6]) for x in "abh"}
        mv = {x: sb(f"mv_{x}", [P, SUB, 2]) for x in "abh"}
        rs = {x: sb(f"rs_{x}", [P, SUB]) for x in "abh"}
        nb = {x: sb(f"nb_{x}", [P, SUB]) for x in "bh"}
        kve = sb("kve", [P, KC, P])
        kden = sb("kden", [P, KC, HQ])
        xnt_flat = xnt[:].rearrange("p s c -> p (s c)")
        zi = xnt_flat[:, 0:TOK]
        kvs = xnt_flat[:, TOK:TOK + KC * P].rearrange("p (k n) -> p k n", k=KC)
        kvr = xnt_flat[:, TOK + KC * P:TOK + 2 * KC * P].rearrange("p (k n) -> p k n", k=KC)
        zs = xt[:, 0].rearrange("p s c -> p (s c)").rearrange("p (k n) -> p k n", k=KC)
        hf = xt[:, 1].rearrange("p s c -> p (s c)").rearrange("p (k n) -> p k n", k=2)
        at = kt[:].rearrange("p s c -> p (s c)").rearrange("p (k n) -> p k n", k=KC)
        y_sb = conv
        wa_raw = vh[:].rearrange("p k n -> p (k n)")[:, 0:KC * A_WIDTH].rearrange("p (k n) -> p k n", k=KC)
        act_flat = act[:].rearrange("p k n -> p (k n)")
        wf1_raw = act_flat[:, 0:KC * HID].rearrange("p (k n) -> p k n", k=KC)
        wf2_raw = act_flat[:, KC * HID:KC * HID + KH * C].rearrange("p (k n) -> p k n", k=KH)

        def par(name, i):
            at_, width = PARAMS[name]
            assert i < width
            return prm[:, at_ + i:at_ + i + 1]

        def const(name):
            at_, width = CONST_COLS[name]
            return cst[:, at_:at_ + width]

        ident = const("identity")
        head_rows = const("head_rows").rearrange("p (k h) -> p k h", k=KC)
        expand = const("expand").rearrange("p (k n) -> p k n", k=KC)
        rope = const("rope").rearrange("p (w k n) -> p w k n", w=2, k=KC)

        once = ("params_in", "wa_in", "wf_in", "zeroed", "centre_taps", "wa_hi_done", "wa_lo_done",
                "wf_hi_done", "wf_lo_done",
                "e_masked", "e_rot1", "e_kvr", "e_rot2", "e_kve", "e_den", "e_den_eps", "e_z")
        per_tile = {
            "sync": ("xn_saved", "y_saved"),
            "gpsimd": ("a_var", "a_rstd", "a_applied", "b_var", "b_rstd", "b_mean", "b_scaled", "b_lo", "d_lo",
                       "f_gated", "f_lo", "h_var", "h_rstd", "h_mean", "h_scaled", "h_lo"),
            "scalar": ("xh_written", "b_centre", "b_applied", "b_hi", "c_out", "d_centre", "d_silu", "d_kexp",
                       "d_qparts", "f_centre", "f_z", "f_hi", "h_centre", "h_applied", "h_hi", "i_gelu"),
            "vector": ("a_stats", "a_moments", "b_left", "b_taps", "b_stats", "b_moments", "d_left", "d_taps",
                       "d_hi", "d_vcopied", "d_kz", "d_kmin", "d_k", "d_q", "f_left", "f_taps", "f_a", "f_sum",
                       "g_x1", "h_left", "h_taps", "h_stats", "h_moments", "i_lo", "i_y"),
            "tensor": ("a_transposed", "b_tokens", "b_back", "c_product", "d_vtokens", "d_kproduct",
                       "d_qproduct", "e_kv", "f_num", "f_zrows", "g_product", "h_tokens", "h_back", "i_fc1",
                       "i_fc2"),
        }
        s = {name: sem(name) for name in once + sum(per_tile.values(), ())}

        def start_at_one(e, engine):
            for name in per_tile[engine]:
                e.sem_inc(s[name], 1)

        x_in = [sem("x_in0"), sem("x_in1")]

        def done(b, t, per_tile=1):
            return b * (NT * per_tile) + ((t + 1) * per_tile + 1)

        def before(b, per_tile=1):
            return b * (NT * per_tile) + 1

        def earlier(b, t, per_tile=1, more=0):
            return b * (NT * per_tile) + (t * per_tile + more + 1)

        def wait_apart(e, semaphore, value):
            count = e.compute_val(value)
            e.wait_ge(s["params_in"], 48)
            e.wait_ge(semaphore, count)

        def centre(buf, k, t, shift=0):
            return buf[:, k, 1 + shift + t * TOK:1 + shift + (t + 1) * TOK]

        def tile_of(buf, k, t):
            return buf[:, k, t * TOK:(t + 1) * TOK]

        block = ctx.enter_context(nc.Block())

        @block.sync
        def _(sp):
            start_at_one(sp, "sync")
            sp.dma_start(prm[:], params).then_inc(s["params_in"], 16)
            sp.dma_start(cst[:], consts).then_inc(s["params_in"], 16)
            sp.dma_start(kb[:], k_bias).then_inc(s["params_in"], 16)

            def load_x(b, t):
                if t >= 2:
                    wait_apart(sp, s["a_transposed"], done(b, t - 2))
                else:
                    wait_apart(sp, s["a_transposed"], before(b))
                    wait_apart(sp, s["f_a"], before(b))
                    wait_apart(sp, s["i_lo"], before(b, KH))
                sp.dma_start(xt[:, t % 2], x[b * NT + t]).then_inc(x_in[t % 2], 16)

            with sp.Fori(0, BATCHES) as b:
                load_x(b, 0)
                load_x(b, 1)
                with sp.If(b < 1):
                    sp.dma_start(wa_raw, w_attn).then_inc(s["wa_in"], 16)
                    sp.dma_start(wf1_raw, w_fc1).then_inc(s["wf_in"], 16)
                    sp.dma_start(wf2_raw, w_fc2).then_inc(s["wf_in"], 16)
                for t in range(2, NT):
                    load_x(b, t)
                for t in range(NT):
                    wait_apart(sp, s["xh_written"], done(b, t))
                    sp.dma_start(xn_scratch[b * NT + t], xh[:, :, 1 + t * TOK:1 + (t + 1) * TOK]) \
                        .then_inc(s["xn_saved"], 16)
                for t in range(NT):
                    wait_apart(sp, s["i_y"], done(b, t, KC))
                    sp.dma_start(y_scratch[b * NT + t], y_sb[:]).then_inc(s["y_saved"], 16)
            sp.wait_ge(s["xn_saved"], 16 * TILES + 1)
            sp.wait_ge(s["y_saved"], 16 * TILES + 1)

        @block.gpsimd
        def _(pool):
            start_at_one(pool, "gpsimd")
            pool.memset(small[:, 0, :], EPS)
            pool.memset(small[:, 1, :], -0.5)
            pool.memset(small[:, 2, :], -1.0)
            pool.memset(vt[:, :, :, P:P + 1], 1.0)
            for buf in (xh, ph):
                pool.memset(buf[:, :, 0:1], 0.0)
                last = pool.memset(buf[:, :, N + 1:N + 2], 0.0)
            last.then_inc(s["zeroed"], 1)
            pool.wait_ge(s["wa_hi_done"], 1)
            pool.tensor_tensor(wa_lo[:], wa_raw, wa_hi[:].bitcast(F32), ALU.subtract).then_inc(s["wa_lo_done"], 1)
            pool.wait_ge(s["wa_lo_done"], 1)
            pool.memset(vh[:, :, 0:1], 0.0)
            pool.memset(vh[:, :, N + 1:N + 2], 0.0).then_inc(s["zeroed"], 1)
            pool.wait_ge(s["wf_hi_done"], 1)
            pool.tensor_tensor(wf1_lo[:], wf1_raw, wf1_hi[:].bitcast(F32), ALU.subtract)
            pool.tensor_tensor(wf2_lo[:], wf2_raw, wf2_hi[:].bitcast(F32), ALU.subtract).then_inc(s["wf_lo_done"], 1)

            def inverse_deviation(b, t, x, applied):
                pool.wait_ge(s[applied], earlier(b, t))
                pool.wait_ge(s[f"{x}_moments"], done(b, t))
                pool.tensor_tensor(rs[x][:], mv[x][:, :, 1], small[:, 0, :], ALU.add).then_inc(s[f"{x}_var"], 1)
                pool.wait_ge(s[f"{x}_var"], done(b, t))
                pool.tensor_tensor(rs[x][:], rs[x][:], small[:, 1, :], ALU.pow).then_inc(s[f"{x}_rstd"], 1)

            def norm_x(b, t):
                inverse_deviation(b, t, "a", "a_applied")
                wait_apart(pool, s["a_rstd"], done(b, t))
                for i in range(SUB):
                    last = pool.tensor_scalar(xt[:, t % 2, i], xt[:, t % 2, i], mv["a"][:, i, 0:1], rs["a"][:, i:i + 1],
                                              ALU.subtract, ALU.mult)
                last.then_inc(s["a_applied"], 1)

            def norm_scalars(b, t, x):
                inverse_deviation(b, t, x, f"{x}_applied")
                pool.wait_ge(s[f"{x}_rstd"], done(b, t))
                pool.tensor_tensor(nb[x][:], mv[x][:, :, 0], rs[x][:], ALU.mult).then_inc(s[f"{x}_mean"], 1)
                pool.wait_ge(s[f"{x}_mean"], done(b, t))
                pool.tensor_tensor(nb[x][:], nb[x][:], small[:, 2, :], ALU.mult).then_inc(s[f"{x}_scaled"], 1)

            def low_part(b, t, hi, lo, source):
                pool.wait_ge(s[hi], done(b, t))
                pool.tensor_tensor(p_lo[:], source, p_hi[:].bitcast(F32), ALU.subtract).then_inc(s[lo], 1)

            with pool.Fori(0, BATCHES) as b:
                for step in range(NT + 3):
                    if 0 <= step - 2 < NT:
                        low_part(b, step - 2, "b_hi", "b_lo", xnf[:])
                    if step < NT:
                        norm_x(b, step)
                    if 0 <= step - 1 < NT:
                        norm_scalars(b, step - 1, "b")
                for t in range(NT):
                    low_part(b, t, "d_hi", "d_lo", vh[:, :, 1 + t * TOK:1 + (t + 1) * TOK])
                for t in range(NT):
                    pool.wait_ge(s["f_sum"], done(b, t))
                    gated = act[:, :, t * TOK:(t + 1) * TOK]
                    pool.tensor_tensor(gated, gated, at, ALU.mult).then_inc(s["f_gated"], 1)
                    low_part(b, t, "f_hi", "f_lo", gated)
                for step in range(NT + 1):
                    if step >= 1:
                        low_part(b, step - 1, "h_hi", "h_lo", xnf[:])
                    if step < NT:
                        norm_scalars(b, step, "h")

        @block.scalar
        def _(e):
            start_at_one(e, "scalar")
            e.wait_ge(s["params_in"], 48)
            e.wait_ge(s["centre_taps"], 1)
            e.wait_ge(s["zeroed"], 1)

            def affine(out, in_, scale, bias, func=ACT.Identity):
                return e.activation(out, in_, func, bias=bias, scale=scale)

            def copy_xn(b, t):
                if t == 0:
                    e.wait_ge(s["h_taps"], before(b))
                e.wait_ge(s["a_transposed"], done(b, t))
                for k in range(KC):
                    last = e.copy(centre(xh, k, t), pairs[0][:, k, :])
                last.then_inc(s["xh_written"], 1)

            def conv1_centre(b, t):
                e.wait_ge(s["xh_written"], done(b, min(t + 1, NT - 1)))
                if t == 0:
                    e.wait_ge(s["i_y"], before(b, KC))
                for k in range(KC):
                    last = affine(tile_of(x0, k, t), centre(xh, k, t), w1p[:, 0, k:k + 1], par("cpe1_b", k))
                last.then_inc(s["b_centre"], 1)

            def apply_norm(b, t, x, bank):
                e.wait_ge(s[f"{x}_scaled"], done(b, t))
                e.wait_ge(s[f"{x}_back"], earlier(b, t))
                for i in range(SUB):
                    last = affine(xnt[:, i, :], as_tokens(bank)[:, i, :], rs[x][:, i:i + 1], nb[x][:, i:i + 1])
                last.then_inc(s[f"{x}_applied"], 1)

            def gain_and_split(b, t, x, bank, gain, bias, users, users_count):
                e.wait_ge(s[f"{x}_back"], done(b, t))
                e.wait_ge(s[f"{x}_lo"], earlier(b, t))
                e.wait_ge(s[users], users_count)
                for k in range(KC):
                    affine(xnf[:, k, :], bank[:, k, :], par(gain, k), par(bias, k))
                for k in range(KC):
                    last = affine(p_hi[:, k, :], bank[:, k, :], par(gain, k), par(bias, k))
                last.then_inc(s[f"{x}_hi"], 1)

            def projections_out(b, t):
                if t == 0:
                    e.wait_ge(s["wf_lo_done"], 1)
                    e.wait_ge(s["f_lo"], before(b))
                    e.wait_ge(s["f_num"], before(b))
                for j in range(2 * KC):
                    e.wait_ge(s["c_product"], earlier(b, t, 2 * KC, j + 1))
                    k = j % KC
                    if j < KC:
                        last = e.activation(tile_of(act, k, t), pairs[3][:, j % 2, :], ACT.Silu,
                                            bias=par("actp_b", k))
                    else:
                        last = e.activation(centre(ph, k, t), pairs[3][:, j % 2, :], ACT.Identity,
                                            bias=par("in_b", k))
                    last.then_inc(s["c_out"], 1)

            def conv2_centre(b, t):
                e.wait_ge(s["c_out"], done(b, min(t + 1, NT - 1), 2 * KC))
                e.wait_ge(s["d_silu"], earlier(b, t))
                if t == 0:
                    e.wait_ge(s["y_saved"], before(b, 16))
                for k in range(KC):
                    last = affine(conv[:, k, :], centre(ph, k, t), par("dwc_w1", k), par("dwc_b", k))
                last.then_inc(s["d_centre"], 1)

            def silu_v(b, t):
                e.wait_ge(s["d_taps"], done(b, t))
                if t == 0:
                    e.wait_ge(s["zeroed"], 2)
                    e.wait_ge(s["f_taps"], before(b))
                last = e.activation(vh[:, :, 1 + t * TOK:1 + (t + 1) * TOK], conv[:], ACT.Silu)
                last.then_inc(s["d_silu"], 1)

            def exps(b, t):
                e.wait_ge(s["d_kz"], done(b, t))
                e.wait_ge(s["d_k"], earlier(b, t))
                if t == 0:
                    e.wait_ge(s["b_back"], done(b, NT - 1))
                e.activation(xnt[:], kt[:], ACT.Exp).then_inc(s["d_kexp"], 1)
                e.wait_ge(s["d_qproduct"], done(b, t))
                e.wait_ge(s["d_q"], earlier(b, t))
                if t == 0:
                    e.wait_ge(s["b_lo"], done(b, NT - 1))
                e.wait_ge(s["d_taps"], done(b, min(t + 1, NT - 1)))
                for k in range(KC):
                    e.activation(xnf[:, k, :], pairs[2][:, k, :], ACT.Exp, bias=par("q_b", k))
                for k in range(KC):
                    last = e.activation(centre(ph, k, t), pairs[2][:, k, :], ACT.Relu, bias=par("q_b", k))
                last.then_inc(s["d_qparts"], 1)

            def lepe_centre(b, t):
                e.wait_ge(s["f_sum"], earlier(b, t))
                if t == 0:
                    e.wait_ge(s["d_silu"], done(b, NT - 1))
                for k in range(KC):
                    last = affine(conv[:, k, :], centre(vh, k, t), par("lepe_w1", k), par("lepe_b", k))
                last.then_inc(s["f_centre"], 1)

            def copy_z(b, t):
                e.wait_ge(s["f_zrows"], done(b, t))
                e.wait_ge(s["f_a"], earlier(b, t))
                if t == 0:
                    e.wait_ge(s["a_transposed"], done(b, NT - 1))
                e.copy(zs, pairs[1][:]).then_inc(s["f_z"], 1)

            def gated_high(b, t):
                e.wait_ge(s["f_gated"], done(b, t))
                if t == 0:
                    e.wait_ge(s["d_kproduct"], done(b, NT - 1))
                    e.wait_ge(s["d_qproduct"], done(b, NT - 1))
                else:
                    e.wait_ge(s["g_product"], done(b, t - 1))
                e.copy(p_hi[:], act[:, :, t * TOK:(t + 1) * TOK]).then_inc(s["f_hi"], 1)

            def conv3_centre(b, t):
                e.wait_ge(s["g_x1"], done(b, min(t + 1, NT - 1)))
                for k in range(KC):
                    last = affine(tile_of(x0, k, t), centre(xh, k, t), w1p[:, 1, k:k + 1], par("cpe2_b", k))
                last.then_inc(s["h_centre"], 1)

            def gelus(b, t):
                if t == 0:
                    e.wait_ge(s["f_a"], done(b, NT - 1))
                    e.wait_ge(s["a_transposed"], done(b, NT - 1))
                e.wait_ge(s["i_fc2"], earlier(b, t, KC))
                for m in range(KH):
                    e.wait_ge(s["i_fc1"], earlier(b, t, KH, m + 1))
                    if m >= 2:
                        e.wait_ge(s["i_lo"], earlier(b, t, KH, m - 1))
                    else:
                        e.wait_ge(s["i_lo"], earlier(b, t, KH))
                    e.activation(hf[:, m % 2, :], pairs[2][:, m % 2, :], ACT.Gelu, bias=par("fc1_b", m))
                    e.activation(h_hi[:, m, :], pairs[2][:, m % 2, :], ACT.Gelu, bias=par("fc1_b", m)) \
                        .then_inc(s["i_gelu"], 1)

            with e.Fori(0, BATCHES) as b:
                for step in range(NT + 3):
                    if step >= 3:
                        projections_out(b, step - 3)
                    if 0 <= step - 2 < NT:
                        apply_norm(b, step - 2, "b", pairs[1])
                        gain_and_split(b, step - 2, "b", pairs[2], "norm1_g", "norm1_b", "c_product",
                                       earlier(b, step - 2, 2 * KC))
                    if step < NT:
                        copy_xn(b, step)
                    if 0 <= step - 1 < NT:
                        conv1_centre(b, step - 1)
                for step in range(NT + 1):
                    if step >= 1:
                        exps(b, step - 1) if step == NT else None
                    if step < NT:
                        conv2_centre(b, step)
                        silu_v(b, step)
                    if 1 <= step < NT:
                        exps(b, step - 1)
                for t in range(NT):
                    lepe_centre(b, t)
                    copy_z(b, t)
                    gated_high(b, t)
                for step in range(NT + 2):
                    if 0 <= step - 1 < NT:
                        apply_norm(b, step - 1, "h", pairs[0])
                        gain_and_split(b, step - 1, "h", pairs[1], "norm2_g", "norm2_b", "i_fc1",
                                       earlier(b, step - 1, KH))
                    if step < NT:
                        conv3_centre(b, step)
                    if 0 <= step - 1 < NT:
                        gelus(b, step - 1)

        @block.vector
        def _(e):
            start_at_one(e, "vector")
            e.wait_ge(s["params_in"], 48)
            for i, name in enumerate(("cpe1_w1", "cpe2_w1")):
                at_ = PARAMS[name][0]
                last = e.tensor_scalar(w1p[:, i, :], prm[:, at_:at_ + KC], 1.0, None, ALU.add)
            last.then_inc(s["centre_taps"], 1)

            def moments(b, t, x, source, ready, count, applied):
                e.wait_ge(ready, count)
                e.wait_ge(s[f"{x}_moments"], earlier(b, t))
                for i in range(SUB):
                    last = e.bn_stats(st[x][:, i, :], source(i))
                last.then_inc(s[f"{x}_stats"], 1)
                wait_apart(e, s[f"{x}_stats"], done(b, t))
                wait_apart(e, s[applied], earlier(b, t))
                for i in range(SUB):
                    last = e.bn_aggr(mv[x][:, i, :], st[x][:, i, :])
                last.then_inc(s[f"{x}_moments"], 1)

            def side_taps(b, t, x, source, out, taps):
                e.wait_ge(s[f"{x}_centre"], done(b, t))
                for k in range(KC):
                    last = e.scalar_tensor_tensor(out=out(k), in0=centre(source, k, t, -1), scalar=par(taps + "_w0", k),
                                                  in1=out(k), op0=ALU.mult, op1=ALU.add)
                last.then_inc(s[f"{x}_left"], 1)
                e.wait_ge(s[f"{x}_left"], done(b, t))
                for k in range(KC):
                    last = e.scalar_tensor_tensor(out=out(k), in0=centre(source, k, t, 1), scalar=par(taps + "_w2", k),
                                                  in1=out(k), op0=ALU.mult, op1=ALU.add)
                last.then_inc(s[f"{x}_taps"], 1)

            def split_attn_weights():
                e.wait_ge(s["wa_in"], 16)
                e.tensor_copy(wa_hi[:], wa_raw).then_inc(s["wa_hi_done"], 1)

            def split_mlp_weights():
                e.wait_ge(s["wf_in"], 32)
                e.tensor_copy(wf1_hi[:], wf1_raw)
                e.tensor_copy(wf2_hi[:], wf2_raw).then_inc(s["wf_hi_done"], 1)

            def v_high(b, t):
                e.wait_ge(s["d_silu"], done(b, t))
                if t == 0:
                    e.wait_ge(s["c_product"], done(b, NT - 1, 2 * KC))
                else:
                    e.wait_ge(s["d_kproduct"], done(b, t - 1))
                    e.wait_ge(s["d_qproduct"], done(b, t - 1))
                e.tensor_copy(p_hi[:], vh[:, :, 1 + t * TOK:1 + (t + 1) * TOK]).then_inc(s["d_hi"], 1)

            def v_and_k(b, t):
                e.wait_ge(s["d_vtokens"], done(b, t))
                e.wait_ge(s["e_kv"], earlier(b, t))
                e.tensor_copy(vt[:, :, :, 0:P], as_tokens(pairs[0]).rearrange("p s (k n) -> p s k n", k=KC)) \
                    .then_inc(s["d_vcopied"], 1)
                e.wait_ge(s["d_kproduct"], done(b, t))
                e.tensor_tensor(kt[:], as_tokens(pairs[1]), kb[:].unsqueeze(1).to_broadcast([P, SUB, C]), ALU.add) \
                    .then_inc(s["d_kz"], 1)

            def k_and_q(b, t):
                e.wait_ge(s["d_kexp"], done(b, t))
                e.tensor_scalar(xnt[:], xnt[:], 1.0, None, ALU.min).then_inc(s["d_kmin"], 1)
                e.wait_ge(s["d_kmin"], done(b, t))
                e.scalar_tensor_tensor(out=kt[:], in0=kt[:], scalar=0.0, in1=xnt[:], op0=ALU.max, op1=ALU.add) \
                    .then_inc(s["d_k"], 1)
                e.wait_ge(s["d_qparts"], done(b, t))
                q = ph[:, :, 1 + t * TOK:1 + (t + 1) * TOK]
                e.scalar_tensor_tensor(out=q, in0=xnf[:], scalar=1.0, in1=q, op0=ALU.min, op1=ALU.add) \
                    .then_inc(s["d_q"], 1)

            def mean_kv(b):
                e.wait_ge(s["e_kv"], done(b, NT - 1))
                kvp = pairs[3][:, 0, 0:KC * (P + 1)].rearrange("p (k n) -> p k n", k=KC)
                for k in range(KC):
                    e.scalar_tensor_tensor(out=kvs[:, k, :], in0=kvp[:, k, 0:P], scalar=1.0 / N,
                                           in1=const("same_head"), op0=ALU.mult, op1=ALU.mult)
                    last = e.tensor_scalar(kden[:, k, :], head_rows[:, k, :], kvp[:, k, P:P + 1], 1.0 / N,
                                           ALU.mult, ALU.mult)
                last.then_inc(s["e_masked"], 1)
                rotated = pairs[3][:, 1, 0:KC * P].rearrange("p (k n) -> p k n", k=KC)
                e.wait_ge(s["e_rot1"], b + 1)
                e.tensor_copy(kvr, rotated).then_inc(s["e_kvr"], 1)
                e.wait_ge(s["e_rot2"], b + 1)
                e.tensor_copy(kve[:], rotated).then_inc(s["e_kve"], 1)
                e.wait_ge(s["e_den"], b + 1)
                e.tensor_scalar(zi, pairs[3][:, 0, :], Z_EPS, None, ALU.add).then_inc(s["e_den_eps"], 1)
                e.wait_ge(s["e_den_eps"], b + 1)
                e.reciprocal(zi, zi).then_inc(s["e_z"], 1)

            def attention_out(b, t):
                e.wait_ge(s["f_z"], done(b, t))
                e.wait_ge(s["f_num"], done(b, t))
                e.wait_ge(s["f_gated"], earlier(b, t))
                if t == 0:
                    e.wait_ge(s["e_kv"], done(b, NT - 1))
                e.tensor_tensor(at, pairs[0][:], zs, ALU.mult).then_inc(s["f_a"], 1)
                e.wait_ge(s["f_a"], done(b, t))
                e.wait_ge(s["f_taps"], done(b, t))
                e.tensor_tensor(at, at, conv[:], ALU.add).then_inc(s["f_sum"], 1)

            def x1(b, t):
                e.wait_ge(s["g_product"], done(b, t))
                if t == 0:
                    e.wait_ge(s["xn_saved"], done(b, NT - 1, 16))
                    e.wait_ge(s["b_taps"], done(b, NT - 1))
                for k in range(KC):
                    last = e.scalar_tensor_tensor(out=centre(xh, k, t), in0=pairs[2][:, k, :], scalar=par("out_b", k),
                                                  in1=tile_of(x0, k, t), op0=ALU.add, op1=ALU.add)
                last.then_inc(s["g_x1"], 1)

            def mlp_low(b, t):
                e.wait_ge(s["i_fc2"], earlier(b, t, KC))
                for m in range(KH):
                    e.wait_ge(s["i_gelu"], earlier(b, t, KH, m + 1))
                    e.tensor_tensor(h_lo[:, m, :], hf[:, m % 2, :], h_hi[:, m, :].bitcast(F32), ALU.subtract) \
                        .then_inc(s["i_lo"], 1)

            def mlp_out(b, t):
                e.wait_ge(s["y_saved"], earlier(b, t, 16))
                if t == 0:
                    e.wait_ge(s["f_sum"], done(b, NT - 1))
                for k in range(KC):
                    e.wait_ge(s["i_fc2"], earlier(b, t, KC, k + 1))
                    e.scalar_tensor_tensor(out=y_sb[:, k, :], in0=pairs[3][:, k, :], scalar=par("fc2_b", k),
                                           in1=tile_of(x0, k, t), op0=ALU.add, op1=ALU.add).then_inc(s["i_y"], 1)

            split_attn_weights()
            split_mlp_weights()
            with e.Fori(0, BATCHES) as b:
                for step in range(NT + 3):
                    if step < NT:
                        moments(b, step, "a", lambda i, t=step: xt[:, t % 2, i, :], x_in[step % 2],
                                b * (16 * NT // 2) + 16 * (step // 2 + 1), "a_applied")
                    if 0 <= step - 1 < NT:
                        t = step - 1
                        side_taps(b, t, "b", xh, lambda k, t=t: tile_of(x0, k, t), "cpe1")
                        moments(b, t, "b", lambda i: as_tokens(pairs[1])[:, i, :], s["b_tokens"], done(b, t),
                                "b_applied")
                for step in range(NT + 1):
                    if step < NT:
                        side_taps(b, step, "d", ph, lambda k: conv[:, k, :], "dwc")
                    if step >= 1:
                        v_and_k(b, step - 1)
                    if step < NT:
                        v_high(b, step)
                    if step >= 1:
                        k_and_q(b, step - 1)
                mean_kv(b)
                for step in range(NT + 1):
                    if step < NT:
                        side_taps(b, step, "f", vh, lambda k: conv[:, k, :], "lepe")
                        attention_out(b, step)
                    if step >= 1:
                        x1(b, step - 1)
                for step in range(NT + 2):
                    if step < NT:
                        side_taps(b, step, "h", xh, lambda k, t=step: tile_of(x0, k, t), "cpe2")
                        moments(b, step, "h", lambda i: as_tokens(pairs[0])[:, i, :], s["h_tokens"],
                                done(b, step), "h_applied")
                    if 0 <= step - 1 < NT:
                        mlp_low(b, step - 1)
                        mlp_out(b, step - 1)

        @block.tensor
        def _(e):
            start_at_one(e, "tensor")
            e.wait_ge(s["params_in"], 48)

            def to_channels(bank, source):
                for i in range(SUB):
                    for k in range(KC):
                        last = e.transpose(bank[:, k, i * P:(i + 1) * P], source(i)[:, k * P:(k + 1) * P], ident)
                return last

            def to_tokens(bank, source):
                for i in range(SUB):
                    for k in range(KC):
                        last = e.transpose(as_tokens(bank)[:, i, k * P:(k + 1) * P],
                                           source(k)[:, i * P:(i + 1) * P], ident)
                return last

            def split_product(out, w_hi, w_lo, x_hi, x_lo, chunks):
                for k in chunks:
                    for n, (w, v) in enumerate(((w_hi, x_hi), (w_hi, x_lo), (w_lo, x_hi))):
                        last = e.matmul(out, w(k), v(k), start=(k == 0 and n == 0),
                                        stop=(k == chunks[-1] and n == 2))
                return last

            def attn_w(w, name, m):
                at_ = A_COLS[name] + m * P
                return lambda k: w[:, k, at_:at_ + P]

            def part(buf):
                return lambda k: buf[:, k, :]

            def a_channels(b, t):
                e.wait_ge(s["a_applied"], done(b, t))
                e.wait_ge(s["xh_written"], earlier(b, t))
                to_channels(pairs[0], lambda i: xt[:, t % 2, i, :]).then_inc(s["a_transposed"], 1)

            def norm_tokens(b, t, x, bank):
                e.wait_ge(s[f"{x}_taps"], done(b, t))
                e.wait_ge(s[f"{x}_applied"], earlier(b, t))
                to_tokens(bank, lambda k: tile_of(x0, k, t)).then_inc(s[f"{x}_tokens"], 1)

            def norm_back(b, t, x, bank):
                e.wait_ge(s[f"{x}_applied"], done(b, t))
                e.wait_ge(s[f"{x}_hi"], earlier(b, t))
                to_channels(bank, lambda i: xnt[:, i, :]).then_inc(s[f"{x}_back"], 1)

            def projections(b, t):
                if t == 0:
                    e.wait_ge(s["wa_lo_done"], 1)
                e.wait_ge(s["b_lo"], done(b, t))
                for j in range(2 * KC):
                    m, name = j % KC, "actp" if j < KC else "in"
                    if j >= 2:
                        e.wait_ge(s["c_out"], earlier(b, t, 2 * KC, j - 1))
                    else:
                        e.wait_ge(s["c_out"], earlier(b, t, 2 * KC))
                    split_product(pairs[3][:, j % 2, :], attn_w(wa_hi, name, m), attn_w(wa_lo, name, m),
                                  part(p_hi), part(p_lo), range(KC)).then_inc(s["c_product"], 1)

            def k_and_q(b, t):
                e.wait_ge(s["d_silu"], done(b, t))
                e.wait_ge(s["d_vcopied"], earlier(b, t))
                to_tokens(pairs[0], lambda k: centre(vh, k, t)).then_inc(s["d_vtokens"], 1)
                e.wait_ge(s["d_lo"], done(b, t))
                e.wait_ge(s["d_kz"], earlier(b, t))
                kc = A_COLS["k"]
                for i in range(SUB):
                    cols = slice(i * P, (i + 1) * P)
                    last = split_product(as_tokens(pairs[1])[:, i, :],
                                         lambda k: p_hi[:, k, cols], lambda k: p_lo[:, k, cols],
                                         lambda k: wa_hi[:, k, kc:kc + C], lambda k: wa_lo[:, k, kc:kc + C], range(KC))
                last.then_inc(s["d_kproduct"], 1)
                e.wait_ge(s["d_qparts"], earlier(b, t))
                for m in range(KC):
                    last = split_product(pairs[2][:, m, :], attn_w(wa_hi, "q", m), attn_w(wa_lo, "q", m),
                                         part(p_hi), part(p_lo), range(KC))
                last.then_inc(s["d_qproduct"], 1)

            def add_kv(b, t):
                e.wait_ge(s["d_k"], done(b, t))
                e.wait_ge(s["d_vcopied"], done(b, t))
                kvp = pairs[3][:, 0, 0:KC * (P + 1)].rearrange("p (k n) -> p k n", k=KC)
                for i in range(SUB):
                    for k in range(KC):
                        last = e.matmul(kvp[:, k, :], kt[:, i, k * P:(k + 1) * P], vt[:, i, k, :],
                                        start=(t == 0 and i == 0 and k == 0), stop=(t == NT - 1 and i == SUB - 1),
                                        skip_group_check=True)
                last.then_inc(s["e_kv"], 1)

            def rotate_kv(b):
                rotated = pairs[3][:, 1, 0:KC * P].rearrange("p (k n) -> p k n", k=KC)
                for n, (before_, source, after) in enumerate((("e_masked", kvs, "e_rot1"), ("e_kvr", kvr, "e_rot2"))):
                    e.wait_ge(s[before_], b + 1)
                    for k in range(KC):
                        last = e.matmul(rotated[:, k, :], rope[:, n, k, :], source[:, k, :], start=True, stop=True)
                    last.then_inc(s[after], 1)

            def denominators(b):
                e.wait_ge(s["d_q"], done(b, NT - 1))
                for t in range(NT):
                    for k in range(KC):
                        last = e.matmul(pairs[3][t * HQ:(t + 1) * HQ, 0, :], kden[:, k, :], centre(ph, k, t),
                                        start=(k == 0), stop=(k == KC - 1))
                last.then_inc(s["e_den"], 1)

            def attention(b, t):
                e.wait_ge(s["e_kve"], b + 1)
                e.wait_ge(s["f_a"], earlier(b, t))
                for k in range(KC):
                    last = e.matmul(pairs[0][:, k, :], kve[:, k, :], centre(ph, k, t), start=True, stop=True)
                last.then_inc(s["f_num"], 1)
                e.wait_ge(s["e_z"], b + 1)
                e.wait_ge(s["f_z"], earlier(b, t))
                rows = slice(t * HQ, (t + 1) * HQ)
                for k in range(KC):
                    last = e.matmul(pairs[1][:, k, :], expand[rows, k, :], zi[rows, :], start=True, stop=True)
                last.then_inc(s["f_zrows"], 1)

            def out_proj(b, t):
                e.wait_ge(s["f_lo"], done(b, t))
                e.wait_ge(s["g_x1"], earlier(b, t))
                for m in range(KC):
                    last = split_product(pairs[2][:, m, :], attn_w(wa_hi, "out", m), attn_w(wa_lo, "out", m),
                                         part(p_hi), part(p_lo), range(KC))
                last.then_inc(s["g_product"], 1)

            def mlp(b, t):
                if t == 0:
                    e.wait_ge(s["wf_lo_done"], 1)
                e.wait_ge(s["h_lo"], done(b, t))
                for m in range(KH):
                    if m >= 2:
                        e.wait_ge(s["i_gelu"], earlier(b, t, KH, m - 1))
                    else:
                        e.wait_ge(s["i_gelu"], earlier(b, t, KH))
                    cols = slice(m * P, (m + 1) * P)
                    split_product(pairs[2][:, m % 2, :], lambda k: wf1_hi[:, k, cols], lambda k: wf1_lo[:, k, cols],
                                  part(p_hi), part(p_lo), range(KC)).then_inc(s["i_fc1"], 1)
                e.wait_ge(s["i_y"], earlier(b, t, KC))
                for m in range(KC):
                    cols = slice(m * P, (m + 1) * P)
                    for k in range(KH):
                        if m == 0:
                            e.wait_ge(s["i_lo"], earlier(b, t, KH, k + 1))
                        for n, (w, v) in enumerate(((wf2_hi, h_hi), (wf2_hi, h_lo), (wf2_lo, h_hi))):
                            last = e.matmul(pairs[3][:, m, :], w[:, k, cols], v[:, k, :],
                                            start=(k == 0 and n == 0), stop=(k == KH - 1 and n == 2))
                    last.then_inc(s["i_fc2"], 1)

            with e.Fori(0, BATCHES) as b:
                e.wait_ge(s["h_hi"], before(b))
                e.wait_ge(s["i_gelu"], before(b, KH))
                e.wait_ge(s["i_y"], before(b, KC))
                for step in range(NT + 3):
                    if step >= 3:
                        projections(b, step - 3)
                    if 0 <= step - 2 < NT:
                        norm_back(b, step - 2, "b", pairs[2])
                    if step < NT:
                        a_channels(b, step)
                    if 0 <= step - 1 < NT:
                        norm_tokens(b, step - 1, "b", pairs[1])
                e.wait_ge(s["xh_written"], done(b, NT - 1))
                e.wait_ge(s["b_hi"], done(b, NT - 1))
                e.wait_ge(s["c_out"], done(b, NT - 1, 2 * KC))
                for step in range(NT + 1):
                    if step < NT:
                        k_and_q(b, step)
                    if step >= 1:
                        add_kv(b, step - 1)
                rotate_kv(b)
                denominators(b)
                e.wait_ge(s["d_vcopied"], done(b, NT - 1))
                e.wait_ge(s["d_kz"], done(b, NT - 1))
                e.wait_ge(s["d_qparts"], done(b, NT - 1))
                for step in range(NT + 1):
                    if step < NT:
                        attention(b, step)
                    if step >= 1:
                        out_proj(b, step - 1)
                e.wait_ge(s["f_a"], done(b, NT - 1))
                e.wait_ge(s["f_z"], done(b, NT - 1))
                e.wait_ge(s["g_x1"], done(b, NT - 1))
                for step in range(NT + 2):
                    if 0 <= step - 1 < NT:
                        norm_back(b, step - 1, "h", pairs[1])
                    if step < NT:
                        norm_tokens(b, step, "h", pairs[0])
                    if 0 <= step - 1 < NT:
                        mlp(b, step - 1)


def gated_part(nc, x, params, consts, w_gate, w_up, w_h1, w_h2, w_down, xn_scratch, y_scratch, out):
    with ExitStack() as ctx:
        def sb(name, shape, dt=F32):
            return ctx.enter_context(nc.sbuf_tensor(name, shape, dt))

        def sem(name):
            return ctx.enter_context(nc.semaphore(name))

        banks = [ctx.enter_context(nc.psum_tensor(f"g_banks{i}", [P, 2, TOK], F32)) for i in range(4)]
        gate_banks, up_banks, layer_banks, out_banks = banks
        out_tokens = out_banks[:].rearrange("p a b -> p (a b)").rearrange("p (s c) -> p s c", s=SUB)

        LAYERS = (("gate", w_gate, KC, HID), ("up", w_up, KC, HID), ("h1", w_h1, KH, HID),
                  ("h2", w_h2, KH, HID), ("down", w_down, KH, C))
        W = {name: sb(f"{name}_weights", [P, k, n], F32R) for name, _, k, n in LAYERS}
        STAGE = 2 * HID
        stage = sb("stage", [P, 2, STAGE])
        prm = sb("g_prm", [P, N_PARAMS])
        ident = sb("g_ident", [P, P])
        ones = sb("g_ones", [P, 1])
        xn = sb("g_xn", [P, KC, TOK])
        x_hi, x_lo = sb("x_hi", [P, KC, TOK], F32R), sb("x_lo", [P, KC, TOK], F32R)
        a_hi, a_lo = sb("a_hi", [P, KH, TOK], F32R), sb("a_lo", [P, KH, TOK], F32R)
        b_hi, b_lo = sb("b_hi", [P, KH, TOK], F32R), sb("b_lo", [P, KH, TOK], F32R)
        silu = sb("g_silu", [P, 2, TOK])
        full = sb("full", [P, 2, TOK])
        y = sb("y", [P, KC, TOK])
        xt = sb("g_xt", [P, SUB, C])
        ot = sb("g_ot", [P, SUB, C])
        PIECE = SUB * C
        bits = sb("bits", [P, sum(k * n for _, _, k, n in LAYERS) // PIECE])
        flags = sb("flags", [1, len(LAYERS)], I32)

        once = ("w_staged0", "w_staged1", "w_in0", "w_in1", "prm_in", "ones_set", "bits_low", "bits_max",
                "bits_sum", "flag_set")
        per_tile = {
            "sync": ("xn_in", "y_in", "xt_in", "out_stored"),
            "gpsimd": ("x_split",),
            "scalar": ("x_hi_done", "silu_done", "u_hi", "h1_gelu", "h2_gelu"),
            "vector": ("gated", "u_lo", "h1_lo", "h2_lo", "y_sum", "out_sum"),
            "tensor": ("gate_mm", "up_mm", "h1_mm", "h2_mm", "down_mm", "y_turned"),
        }
        s = {name: sem(f"g_{name}") for name in once + sum(per_tile.values(), ())}

        def start_at_one(e, engine):
            for name in per_tile[engine]:
                e.sem_inc(s[name], 1)

        def count(g, per_tile, more=0):
            return g * per_tile + (more + 1)

        def par(name, i):
            at_, width = PARAMS[name]
            assert i < width
            return prm[:, at_ + i:at_ + i + 1]

        pieces = []
        for n, (name, src, k, width) in enumerate(LAYERS):
            flat_src, flat = src.rearrange("p k n -> p (k n)"), W[name][:].rearrange("p k n -> p (k n)")
            for c in range(0, k * width, STAGE):
                pieces.append((n, flat_src[:, c:c + STAGE], flat[:, c:c + STAGE].bitcast(F32)))
        last_piece = {n: max(i for i, piece in enumerate(pieces) if piece[0] == n) for n in range(len(LAYERS))}

        def piece_columns(layer):
            ends = [sum(k * n for _, _, k, n in LAYERS[:i]) // PIECE for i in range(len(LAYERS) + 1)]
            return range(0 if layer == 1 else ends[layer], ends[layer + 1])

        def wait_weights(e, layer):
            count = last_piece[layer] + 1
            e.wait_ge(s["w_in0"], 16 * ((count + 1) // 2))
            if count >= 2:
                e.wait_ge(s["w_in1"], 16 * (count // 2))

        def wait_apart(e, semaphore, value):
            count = e.compute_val(value)
            e.wait_ge(s["prm_in"], 32)
            e.wait_ge(semaphore, count)

        block = ctx.enter_context(nc.Block())

        @block.sync
        def _(sp):
            start_at_one(sp, "sync")
            sp.dma_start(prm[:], params).then_inc(s["prm_in"], 16)
            sp.dma_start(ident[:], consts[:, 0:P]).then_inc(s["prm_in"], 16)
            with sp.Fori(0, TILES) as g:
                wait_apart(sp, s["x_split"], count(g, 1))
                sp.dma_start(xn[:], xn_scratch[g]).then_inc(s["xn_in"], 16)
                wait_apart(sp, s["y_turned"], count(g, 1))
                sp.dma_start(y[:], y_scratch[g]).then_inc(s["y_in"], 16)
                wait_apart(sp, s["out_sum"], count(g, 1))
                sp.dma_start(xt[:], x[g]).then_inc(s["xt_in"], 16)
                wait_apart(sp, s["out_sum"], count(g, 1, 1))
                sp.dma_start(out[g], ot[:]).then_inc(s["out_stored"], 16)
            sp.wait_ge(s["out_stored"], 16 * TILES + 1)

        @block.gpsimd
        def _(pool):
            start_at_one(pool, "gpsimd")
            pool.memset(ones[:], 1.0).then_inc(s["ones_set"], 1)
            for i, (_, src, dst) in enumerate(pieces):
                if i >= 2:
                    pool.wait_ge(s[f"w_in{i % 2}"], 16 * (i // 2))
                pool.dma_start(stage[:, i % 2, :], src).then_inc(s[f"w_staged{i % 2}"], 16)
                if i >= 1:
                    j = i - 1
                    pool.wait_ge(s[f"w_staged{j % 2}"], 16 * (j // 2 + 1))
                    pool.dma_start(pieces[j][2], stage[:, j % 2, :]).then_inc(s[f"w_in{j % 2}"], 16)
            j = len(pieces) - 1
            pool.wait_ge(s[f"w_staged{j % 2}"], 16 * (j // 2 + 1))
            pool.dma_start(pieces[j][2], stage[:, j % 2, :]).then_inc(s[f"w_in{j % 2}"], 16)

            with pool.Fori(0, TILES) as g:
                pool.wait_ge(s["x_hi_done"], count(g, 1, 1))
                pool.tensor_tensor(x_lo[:], xn[:], x_hi[:].bitcast(F32), ALU.subtract).then_inc(s["x_split"], 1)

        @block.scalar
        def _(e):
            start_at_one(e, "scalar")
            e.wait_ge(s["prm_in"], 32)

            def gelu_layer(g, mm, gelu, low, out_hi, scale, users):
                for m in range(KH):
                    e.wait_ge(s[mm], count(g, KH, m + 1))
                    e.wait_ge(s[low], count(g, KH, max(m - 1, 0)))
                    if m == 0:
                        for name, used in users:
                            e.wait_ge(s[name], used)
                    e.activation(full[:, m % 2, :], layer_banks[:, m % 2, :], ACT.Gelu, scale=par(scale, m))
                    e.activation(out_hi[:, m, :], layer_banks[:, m % 2, :], ACT.Gelu, scale=par(scale, m)) \
                        .then_inc(s[gelu], 1)

            def high_of_gated(g, m):
                e.wait_ge(s["gated"], count(g, KH, m + 1))
                if m == 0:
                    e.wait_ge(s["down_mm"], count(g, KC))
                e.copy(a_hi[:, m, :], full[:, m % 2, :]).then_inc(s["u_hi"], 1)

            with e.Fori(0, TILES) as g:
                e.wait_ge(s["xn_in"], count(g, 16, 16))
                e.wait_ge(s["up_mm"], count(g, KH))
                e.copy(x_hi[:], xn[:]).then_inc(s["x_hi_done"], 1)
                for m in range(KH):
                    e.wait_ge(s["gate_mm"], count(g, KH, m + 1))
                    e.wait_ge(s["gated"], count(g, KH, max(m - 1, 0)))
                    e.activation(silu[:, m % 2, :], gate_banks[:, m % 2, :], ACT.Silu, scale=par("w1_s", m)) \
                        .then_inc(s["silu_done"], 1)
                    if m >= 1:
                        high_of_gated(g, m - 1)
                high_of_gated(g, KH - 1)
                gelu_layer(g, "h1_mm", "h1_gelu", "h1_lo", b_hi, "h1_s",
                           (("h2_mm", count(g, KH)), ("u_lo", count(g, KH, KH))))
                gelu_layer(g, "h2_mm", "h2_gelu", "h2_lo", a_hi, "h2_s",
                           (("h1_mm", count(g, KH, KH)), ("h1_lo", count(g, KH, KH))))

        @block.vector
        def _(e):
            start_at_one(e, "vector")
            at_piece = 0
            low_bits = ot[:].rearrange("p s c -> p (s c)").bitcast(I32)
            for n, (name, _, k, width) in enumerate(LAYERS):
                wait_weights(e, n)
                flat = W[name][:].rearrange("p k n -> p (k n)").bitcast(I32)
                for c in range(0, k * width, PIECE):
                    if at_piece:
                        e.wait_ge(s["bits_max"], at_piece)
                    e.tensor_scalar(low_bits, flat[:, c:c + PIECE], 0xFFF, None, ALU.bitwise_and) \
                        .then_inc(s["bits_low"], 1)
                    e.wait_ge(s["bits_low"], at_piece + 1)
                    e.tensor_reduce(bits[:, at_piece:at_piece + 1], low_bits, AX_X, ALU.max).then_inc(s["bits_max"], 1)
                    at_piece += 1
                e.wait_ge(s["bits_sum"], n + 1)
                n_pieces = len(piece_columns(n))
                e.tensor_reduce(flags[0:1, n:n + 1], out_banks[0:1, 0, 0:n_pieces], AX_X, ALU.max).then_inc(s["flag_set"], 1)

            def low(g, m, out_lo, out_hi, ready, after):
                e.wait_ge(s[ready], count(g, KH, m + 1))
                e.tensor_tensor(out_lo[:, m, :], full[:, m % 2, :], out_hi[:, m, :].bitcast(F32), ALU.subtract) \
                    .then_inc(s[after], 1)

            e.wait_ge(s["prm_in"], 32)
            with e.Fori(0, TILES) as g:
                for m in range(KH):
                    e.wait_ge(s["up_mm"], count(g, KH, m + 1))
                    e.wait_ge(s["silu_done"], count(g, KH, m + 1))
                    if m == 0:
                        e.wait_ge(s["h2_lo"], count(g, KH))
                        e.wait_ge(s["down_mm"], count(g, KC))
                    else:
                        e.wait_ge(s["u_lo"], count(g, KH, max(m - 1, 0)))
                        e.wait_ge(s["u_hi"], count(g, KH, max(m - 1, 0)))
                    e.scalar_tensor_tensor(out=full[:, m % 2, :], in0=up_banks[:, m % 2, :], scalar=par("w2_s", m),
                                           in1=silu[:, m % 2, :], op0=ALU.mult, op1=ALU.mult).then_inc(s["gated"], 1)
                    if m >= 1:
                        low(g, m - 1, a_lo, a_hi, "u_hi", "u_lo")
                low(g, KH - 1, a_lo, a_hi, "u_hi", "u_lo")
                e.wait_ge(s["h2_mm"], count(g, KH))
                for m in range(KH):
                    low(g, m, b_lo, b_hi, "h1_gelu", "h1_lo")
                for m in range(KH):
                    low(g, m, a_lo, a_hi, "h2_gelu", "h2_lo")
                e.wait_ge(s["y_in"], count(g, 16, 16))
                for k in range(KC):
                    e.wait_ge(s["down_mm"], count(g, KC, k + 1))
                    e.scalar_tensor_tensor(out=y[:, k, :], in0=layer_banks[:, k, :], scalar=par("w3_s", k),
                                           in1=y[:, k, :], op0=ALU.mult, op1=ALU.add).then_inc(s["y_sum"], 1)
                e.wait_ge(s["xt_in"], count(g, 16, 16))
                e.wait_ge(s["out_stored"], count(g, 16))
                e.wait_ge(s["y_turned"], count(g, 1, 1))
                e.tensor_tensor(ot[:], out_tokens, xt[:], ALU.add).then_inc(s["out_sum"], 1)

        @block.tensor
        def _(e):
            start_at_one(e, "tensor")
            e.wait_ge(s["prm_in"], 32)
            e.wait_ge(s["ones_set"], 1)
            for n in range(len(LAYERS)):
                columns_ = piece_columns(n)
                e.wait_ge(s["bits_max"], columns_[-1] + 1)
                if n >= 1:
                    e.wait_ge(s["flag_set"], n)
                e.matmul(out_banks[0:1, 0, 0:len(columns_)], ones[:], bits[:, columns_[0]:columns_[-1] + 1],
                         start=True, stop=True).then_inc(s["bits_sum"], 1)

            def product(bank, w, x_hi_, x_lo_, m, chunks, wide, ready=None):
                dt = F32 if wide else F32R
                for k in range(chunks):
                    if ready:
                        ready(k)
                    for n, x_part in enumerate((x_hi_, x_lo_)):
                        last = e.matmul(bank, w[:, k, m * P:(m + 1) * P].bitcast(dt), x_part[:, k, :].bitcast(dt),
                                        start=(k == 0 and n == 0), stop=(k == chunks - 1 and n == 1))
                return last

            def first_layer(g, wide):
                e.wait_ge(s["x_split"], count(g, 1, 1))
                for m in range(KH):
                    e.wait_ge(s["silu_done"], count(g, KH, max(m - 1, 0)))
                    product(gate_banks[:, m % 2, :], W["gate"], x_hi, x_lo, m, KC, wide).then_inc(s["gate_mm"], 1)
                    e.wait_ge(s["gated"], count(g, KH, max(m - 1, 0)))
                    product(up_banks[:, m % 2, :], W["up"], x_hi, x_lo, m, KC, wide).then_inc(s["up_mm"], 1)

            def hidden_layer(g, wide, w, hi, lo, inputs, outputs, mm, read_before):
                for m in range(KH):
                    if m >= 2:
                        e.wait_ge(s[outputs], count(g, KH, m - 1))
                    else:
                        e.wait_ge(s[read_before[0]], read_before[1])
                        e.wait_ge(s[outputs], count(g, KH))

                    def ready(k):
                        if m == 0:
                            e.wait_ge(s[inputs], count(g, KH, k + 1))

                    product(layer_banks[:, m % 2, :], w, hi, lo, m, KH, wide, ready).then_inc(s[mm], 1)

            def last_layer(g, wide):
                for m in range(KC):
                    if m == 0:
                        e.wait_ge(s["h2_gelu"], count(g, KH, KH))

                    def ready(k):
                        if m == 0:
                            e.wait_ge(s["h2_lo"], count(g, KH, k + 1))

                    product(layer_banks[:, m, :], W["down"], a_hi, a_lo, m, KH, wide, ready).then_inc(s["down_mm"], 1)

            def either(layer, run):
                e.wait_ge(s["flag_set"], layer + 1)
                flag = e.value_load(flags[0:1, layer:layer + 1])
                with e.If(flag > 0):
                    run(True)
                with e.Else():
                    run(False)

            with e.Fori(0, TILES) as g:
                either(1, lambda wide: first_layer(g, wide))
                either(2, lambda wide: hidden_layer(g, wide, W["h1"], a_hi, a_lo, "u_lo", "h1_gelu", "h1_mm",
                                                       ("y_sum", count(g, KC))))
                either(3, lambda wide: hidden_layer(g, wide, W["h2"], b_hi, b_lo, "h1_lo", "h2_gelu", "h2_mm",
                                                       ("h1_gelu", count(g, KH, KH))))
                either(4, lambda wide: last_layer(g, wide))
                e.wait_ge(s["out_sum"], count(g, 1))
                for i in range(SUB):
                    for k in range(KC):
                        if i == 0:
                            e.wait_ge(s["y_sum"], count(g, KC, k + 1))
                        last = e.transpose(out_tokens[:, i, k * P:(k + 1) * P], y[:, k, i * P:(i + 1) * P], ident[:])
                last.then_inc(s["y_turned"], 1)


def build(nc, t):
    x = t["x"].rearrange("g (s p) c -> g p s c", p=P)
    out = t["out"].rearrange("g (s p) c -> g p s c", p=P)
    xn_scratch = nc.dram_tensor("xn_scratch", (TILES, P, KC, TOK), F32, kind="Internal").ap()
    y_scratch = nc.dram_tensor("y_scratch", (TILES, P, KC, TOK), F32, kind="Internal").ap()
    attention_part(nc, x, t["params"], t["consts"], t["k_bias"], t["w_attn"], t["w_fc1"], t["w_fc2"],
                   xn_scratch, y_scratch)
    gated_part(nc, x, t["params"], t["consts"], t["w_gate"], t["w_up"], t["w_h1"], t["w_h2"], t["w_down"],
               xn_scratch, y_scratch, out)


def chunked(w):
    w = np.asarray(w)
    return np.ascontiguousarray(w.reshape(w.shape[0] // P, P, w.shape[1]).transpose(1, 0, 2))


def columns(v):
    v = np.asarray(v)
    return v.reshape(-1, P).T


def kernel(**inputs):
    import concourse.bacc as bacc
    from concourse.bass_utils import run_bass_kernel_spmd as run

    a = {k.removeprefix("L0_attn_"): np.asarray(v) for k, v in inputs.items() if k.startswith("L0_attn_")}
    f = {k.removeprefix("L0_ffn_"): np.asarray(v) for k, v in inputs.items() if k.startswith("L0_ffn_")}
    vectors = {}
    for conv in ("cpe1", "dwc", "lepe", "cpe2"):
        for tap in range(3):
            vectors[f"{conv}_w{tap}"] = a[f"{conv}_w"][:, 0, tap]
        vectors[f"{conv}_b"] = a[f"{conv}_b"]
    for name in ("norm1_g", "norm1_b", "in_b", "actp_b", "out_b", "norm2_g", "norm2_b", "fc1_b", "fc2_b"):
        vectors[name] = a[name]
    vectors["q_b"] = a["qk_b"][:C]
    for name in ("w1_s", "w2_s", "h1_s", "h2_s", "w3_s"):
        vectors[name] = f[name]
    arrays = {
        "x": a["x"].reshape(TILES, TOK, C),
        "params": np.concatenate([columns(vectors[name]) for name in PARAMS], axis=1),
        "consts": constants(),
        "k_bias": np.tile(a["qk_b"][None, C:], (P, 1)),
        "w_attn": chunked(np.concatenate([a["actp_w"], a["in_w"], a["qk_w"], a["out_w"]], axis=1)),
        "w_fc1": chunked(a["fc1_w"]),
        "w_fc2": chunked(a["fc2_w"]),
        "w_gate": chunked(f["w1_w"].T),
        "w_up": chunked(f["w2_w"].T),
        "w_h1": chunked(f["h1_w"].T),
        "w_h2": chunked(f["h2_w"].T),
        "w_down": chunked(f["w3_w"].T),
    }
    arrays = {k: np.ascontiguousarray(v) for k, v in arrays.items()}
    nc = bacc.Bacc("TRN2", target_bir_lowering=False, num_devices=1)
    t = {k: nc.dram_tensor(k, v.shape, mybir.dt.from_np(v.dtype), kind="ExternalInput").ap()
         for k, v in arrays.items()}
    t["out"] = nc.dram_tensor("out", (TILES, TOK, C), F32, kind="ExternalOutput").ap()
    build(nc, t)
    r = run(nc, [arrays], core_ids=[0])
    return r.results[0]["out"].reshape(BATCHES, N, C)
```

```python
from contextlib import ExitStack

import numpy as np

import concourse.bass as bass
from concourse import mybir

F32 = mybir.dt.float32
F32R = mybir.dt.float32r
I32 = mybir.dt.int32
ALU = mybir.AluOpType
ACT = mybir.ActivationFunctionType
AX_X = mybir.AxisListType.X

P = 128
BATCHES, N, C = 2, 2048, 256
KC = C // P
HEADS = 16
D = C // HEADS
HID = 4 * C
KH = HID // P
TOK = 512
SUB = TOK // P
NT = N // TOK
TILES = BATCHES * NT
HQ = 32
EPS = 1e-5
Z_EPS = 1e-6

GATED_LAYERS = (("gate", KC, HID), ("up", KC, HID), ("h1", KH, HID), ("h2", KH, HID), ("down", KH, C))
PIECE = sum(k * n for _, k, n in GATED_LAYERS) // TILES

PARAMS = {}
for _name, _width in (
    ("cpe1_w0", KC), ("cpe1_w1", KC), ("cpe1_w2", KC), ("cpe1_b", KC),
    ("norm1_g", KC), ("norm1_b", KC), ("in_b", KC), ("actp_b", KC),
    ("dwc_w0", KC), ("dwc_w1", KC), ("dwc_w2", KC), ("dwc_b", KC), ("q_b", KC),
    ("lepe_w0", KC), ("lepe_w1", KC), ("lepe_w2", KC), ("lepe_b", KC), ("out_b", KC),
    ("cpe2_w0", KC), ("cpe2_w1", KC), ("cpe2_w2", KC), ("cpe2_b", KC),
    ("norm2_g", KC), ("norm2_b", KC), ("fc1_b", KH),
    ("w1_s", KH), ("w2_s", KH), ("h1_s", KH), ("h2_s", KH),
):
    PARAMS[_name] = (sum(w for _, w in PARAMS.values()), _width)
N_PARAMS = sum(w for _, w in PARAMS.values())

A_COLS = {"actp": 0, "in": C, "q": 2 * C, "k": 3 * C, "out": 4 * C}
A_WIDTH = 5 * C


def constants():
    identity = np.eye(P, dtype=np.float32)
    head_of = np.arange(C) // D
    same_head = np.equal.outer(np.arange(P) // D, np.arange(P) // D).astype(np.float32)
    head_rows = np.zeros((P, KC, HQ), np.float32)
    expand = np.zeros((P, KC, P), np.float32)
    for c in range(C):
        head_rows[c % P, c // P, head_of[c]] = 1.0
        for q in range(P // HQ):
            expand[q * HQ + head_of[c], c // P, c % P] = 1.0
    pairs = C // 2
    theta = 1.0 / np.float32(10000.0) ** (np.arange(pairs, dtype=np.float32) / np.float32(pairs))
    cos, sin = np.cos(theta), np.sin(theta)
    rope = np.zeros((P, 2, KC, P), np.float32)
    for j in range(pairs):
        e, chunk = (2 * j) % P, (2 * j) // P
        rot = np.array([[cos[j], -sin[j]], [sin[j], cos[j]]], np.float32)
        rope[e:e + 2, 1, chunk, e:e + 2] = rot
        rope[e:e + 2, 0, chunk, e:e + 2] = rot.T
    return np.concatenate([identity, same_head, head_rows.reshape(P, -1), expand.reshape(P, -1),
                           rope.reshape(P, -1)], axis=1)


CONST_COLS = {"identity": (0, P), "same_head": (P, P), "head_rows": (2 * P, KC * HQ),
              "expand": (2 * P + KC * HQ, KC * P), "rope": (2 * P + KC * HQ + KC * P, 2 * KC * P)}
N_CONST = 2 * P + KC * HQ + 3 * KC * P


def as_tokens(pair):
    return pair[:].rearrange("p a b -> p (a b)").rearrange("p (s c) -> p s c", s=SUB)


def to_channels(e, bank, source, ident):
    for i in range(SUB):
        for k in range(KC):
            last = e.transpose(bank[:, k, i * P:(i + 1) * P], source(i)[:, k * P:(k + 1) * P], ident)
    return last


def to_tokens(e, bank, source, ident):
    for i in range(SUB):
        for k in range(KC):
            last = e.transpose(as_tokens(bank)[:, i, k * P:(k + 1) * P], source(k)[:, i * P:(i + 1) * P], ident)
    return last


def split_product(e, out, w_hi, w_lo, x_hi, x_lo, chunks):
    for k in range(chunks):
        for n, (w, v) in enumerate(((w_hi, x_hi), (w_hi, x_lo), (w_lo, x_hi))):
            last = e.matmul(out, w(k), v(k), start=(k == 0 and n == 0), stop=(k == chunks - 1 and n == 2))
    return last


def attention_part(nc, x, params, consts, rows, w_attn, xn_scratch, x1_scratch):
    with ExitStack() as ctx:
        def sb(name, shape, dt=F32):
            return ctx.enter_context(nc.sbuf_tensor(name, shape, dt))

        def sem(name):
            return ctx.enter_context(nc.semaphore(name))

        pairs = [ctx.enter_context(nc.psum_tensor(f"banks{i}", [P, 2, TOK], F32)) for i in range(4)]

        xh = sb("xh", [P, KC, N + 2])
        x0_framed = sb("x0", [P, KC, N + 2])
        x0 = x0_framed[:, :, 1:N + 1]
        act = sb("act", [P, KC, N])
        ph = sb("ph", [P, KC, N + 2])
        vh = sb("vh", [P, KC, N + 2])
        wa_hi, wa_lo = sb("wa_hi", [P, KC, A_WIDTH], F32R), sb("wa_lo", [P, KC, A_WIDTH], F32R)
        prm = sb("prm", [P, N_PARAMS])
        cst = sb("cst", [P, N_CONST])
        kb = sb("kb", [P, C])
        w1p = sb("w1p", [P, KC])
        small = sb("small", [P, 3, SUB])
        xt = sb("xt", [P, 2, SUB, C])
        xnt = sb("xnt", [P, 2, SUB, C])
        xnf = sb("xnf", [P, 2, KC, TOK])
        p_hi, p_lo = sb("p_hi", [P, 2, KC, TOK], F32R), sb("p_lo", [P, 2, KC, TOK], F32R)
        conv = sb("conv", [P, 2, KC, TOK])
        kt = sb("kt", [P, 2, SUB, C])
        vt = sb("vt", [P, 2, SUB, KC, P + 1])
        st = {x: sb(f"st_{x}", [P, SUB, 6]) for x in "ab"}
        mv = {x: sb(f"mv_{x}", [P, NT, SUB, 2]) for x in "ab"}
        rs = {x: sb(f"rs_{x}", [P, NT, SUB]) for x in "ab"}
        nb = sb("nb", [P, NT, SUB])
        kvs = sb("kvs", [P, KC, P])
        kvr = sb("kvr", [P, KC, P])
        kve = sb("kve", [P, KC, P])
        kden = sb("kden", [P, KC, HQ])
        zi = sb("zi", [P, TOK])
        at = kt[:, 0].rearrange("p s c -> p (s c)").rearrange("p (k n) -> p k n", k=KC)
        zs = kt[:, 1].rearrange("p s c -> p (s c)").rearrange("p (k n) -> p k n", k=KC)
        wa_raw = vh[:].rearrange("p k n -> p (k n)")[:, 0:KC * A_WIDTH].rearrange("p (k n) -> p k n", k=KC)

        def par(name, i):
            at_, width = PARAMS[name]
            assert i < width
            return prm[:, at_ + i:at_ + i + 1]

        def const(name):
            at_, width = CONST_COLS[name]
            return cst[:, at_:at_ + width]

        ident = const("identity")
        head_rows = const("head_rows").rearrange("p (k h) -> p k h", k=KC)
        expand = const("expand").rearrange("p (k n) -> p k n", k=KC)
        rope = const("rope").rearrange("p (w k n) -> p w k n", w=2, k=KC)

        once = ("params_in", "wa_in", "zeroed", "centre_taps", "wa_hi_done", "wa_lo_done",
                "e_masked", "e_rot1", "e_kvr", "e_rot2", "e_kve", "e_den", "e_den_eps", "e_z")
        per_tile = {
            "sync": ("xn_saved", "x1_saved"),
            "gpsimd": ("a_var", "a_rstd", "b_var", "b_rstd", "b_mean", "b_scaled", "b_lo", "d_lo", "f_gated", "f_lo"),
            "scalar": ("xh_written", "b_centre", "b_applied", "b_hi", "c_out", "d_centre", "d_silu", "d_kexp",
                       "d_qparts", "f_centre", "f_z", "f_hi"),
            "vector": ("a_stats", "a_moments", "a_applied", "b_left", "b_taps", "b_stats", "b_moments", "d_left",
                       "d_taps", "d_hi", "d_vcopied", "d_kz", "d_kmin", "d_k", "d_q", "f_left", "f_taps", "f_a",
                       "f_sum", "g_x1"),
            "tensor": ("a_transposed", "b_tokens", "b_back", "c_product", "d_vtokens", "d_kproduct",
                       "d_qproduct", "e_kv", "f_num", "f_zrows", "g_product"),
        }
        s = {name: sem(name) for name in once + sum(per_tile.values(), ())}

        def start_at_one(e, engine):
            for name in per_tile[engine]:
                e.sem_inc(s[name], 1)

        x_in = [sem("x_in0"), sem("x_in1")]

        def done(b, t, per_tile=1):
            return b * (NT * per_tile) + ((t + 1) * per_tile + 1)

        def earlier(b, t, per_tile=1, more=0):
            return b * (NT * per_tile) + (t * per_tile + more + 1)

        def slot_free(b, t, per_tile=1):
            return b * (NT * per_tile) + (max(t - 1, 0) * per_tile + 1)

        def before(b, per_tile=1):
            return b * (NT * per_tile) + 1

        def wait_apart(e, semaphore, value):
            count = e.compute_val(value)
            e.wait_ge(s["params_in"], 48)
            e.wait_ge(semaphore, count)

        def centre(buf, k, t, shift=0):
            return buf[:, k, 1 + shift + t * TOK:1 + shift + (t + 1) * TOK]

        def centres(buf, t):
            return buf[:, :, 1 + t * TOK:1 + (t + 1) * TOK]

        def tile_of(buf, k, t):
            return buf[:, k, t * TOK:(t + 1) * TOK]

        block = ctx.enter_context(nc.Block())

        @block.sync
        def _(sp):
            sp.dma_start(prm[:], params).then_inc(s["params_in"], 16)
            sp.dma_start(cst[:], consts).then_inc(s["params_in"], 16)
            sp.dma_start(kb[:], rows[:, 0:C]).then_inc(s["params_in"], 16)
            start_at_one(sp, "sync")

            def load_x(b, t):
                wait_apart(sp, s["a_transposed"], slot_free(b, t))
                sp.dma_start(xt[:, t % 2], x[b * NT + t]).then_inc(x_in[t % 2], 16)

            with sp.Fori(0, BATCHES) as b:
                load_x(b, 0)
                load_x(b, 1)
                with sp.If(b < 1):
                    sp.dma_start(wa_raw, w_attn).then_inc(s["wa_in"], 16)
                for t in range(2, NT):
                    load_x(b, t)
                for t in range(NT):
                    wait_apart(sp, s["xh_written"], done(b, t))
                    sp.dma_start(xn_scratch[b * NT + t], centres(xh, t)).then_inc(s["xn_saved"], 16)
                for t in range(NT):
                    wait_apart(sp, s["g_x1"], done(b, t))
                    cols = slice(1 + t * TOK - (t == 0), 1 + (t + 1) * TOK + (t == NT - 1))
                    sp.dma_start(x1_scratch[b][:, :, cols], x0_framed[:, :, cols]) \
                        .then_inc(s["x1_saved"], 16)
            sp.wait_ge(s["xn_saved"], 16 * TILES + 1)
            sp.wait_ge(s["x1_saved"], 16 * TILES + 1)

        @block.gpsimd
        def _(pool):
            start_at_one(pool, "gpsimd")
            pool.memset(small[:, 0, :], EPS)
            pool.memset(small[:, 1, :], -0.5)
            pool.memset(small[:, 2, :], -1.0)
            for i in range(2):
                pool.memset(vt[:, i, :, :, P:P + 1], 1.0)
            for buf in (x0_framed, xh, ph):
                pool.memset(buf[:, :, 0:1], 0.0)
                last = pool.memset(buf[:, :, N + 1:N + 2], 0.0)
            last.then_inc(s["zeroed"], 1)

            def inverse_deviation(b, t, x):
                pool.wait_ge(s[f"{x}_applied"], before(b))
                pool.wait_ge(s[f"{x}_moments"], done(b, t))
                pool.tensor_tensor(rs[x][:, t], mv[x][:, t, :, 1], small[:, 0, :], ALU.add).then_inc(s[f"{x}_var"], 1)
                pool.wait_ge(s[f"{x}_var"], done(b, t))
                pool.tensor_tensor(rs[x][:, t], rs[x][:, t], small[:, 1, :], ALU.pow).then_inc(s[f"{x}_rstd"], 1)

            def norm_scalars(b, t):
                inverse_deviation(b, t, "b")
                pool.wait_ge(s["b_rstd"], done(b, t))
                pool.tensor_tensor(nb[:, t], mv["b"][:, t, :, 0], rs["b"][:, t], ALU.mult).then_inc(s["b_mean"], 1)
                pool.wait_ge(s["b_mean"], done(b, t))
                pool.tensor_tensor(nb[:, t], nb[:, t], small[:, 2, :], ALU.mult).then_inc(s["b_scaled"], 1)

            def low_part(b, t, hi, lo, source):
                pool.wait_ge(s[hi], done(b, t))
                pool.tensor_tensor(p_lo[:, t % 2], source, p_hi[:, t % 2].bitcast(F32), ALU.subtract) \
                    .then_inc(s[lo], 1)

            def split_attn_weights():
                pool.wait_ge(s["wa_hi_done"], 1)
                pool.tensor_tensor(wa_lo[:], wa_raw, wa_hi[:].bitcast(F32), ALU.subtract) \
                    .then_inc(s["wa_lo_done"], 1)
                pool.wait_ge(s["wa_lo_done"], 1)
                pool.memset(vh[:, :, 0:1], 0.0)
                pool.memset(vh[:, :, N + 1:N + 2], 0.0).then_inc(s["zeroed"], 1)

            pool.wait_ge(s["zeroed"], 1)
            with pool.Fori(0, BATCHES) as b:
                for t in range(NT):
                    inverse_deviation(b, t, "a")
                with pool.If(b < 1):
                    split_attn_weights()
                for step in range(NT + 1):
                    if step >= 1:
                        low_part(b, step - 1, "b_hi", "b_lo", xnf[:, (step - 1) % 2])
                    if step < NT:
                        norm_scalars(b, step)
                for t in range(NT):
                    low_part(b, t, "d_hi", "d_lo", centres(vh, t))
                for t in range(NT):
                    pool.wait_ge(s["f_sum"], done(b, t))
                    gated = act[:, :, t * TOK:(t + 1) * TOK]
                    pool.tensor_tensor(gated, gated, at, ALU.mult).then_inc(s["f_gated"], 1)
                    low_part(b, t, "f_hi", "f_lo", gated)

        @block.scalar
        def _(e):
            start_at_one(e, "scalar")
            e.wait_ge(s["params_in"], 48)
            e.wait_ge(s["centre_taps"], 1)
            e.wait_ge(s["zeroed"], 1)

            def affine(out, in_, scale, bias, func=ACT.Identity):
                return e.activation(out, in_, func, bias=bias, scale=scale)

            def copy_xn(b, t):
                if t == 0:
                    e.wait_ge(s["b_taps"], before(b))
                    e.wait_ge(s["xn_saved"], before(b, 16))
                e.wait_ge(s["a_transposed"], done(b, t))
                e.copy(centres(xh, t), pairs[t % 2][:]).then_inc(s["xh_written"], 1)

            def conv1_centre(b, t):
                e.wait_ge(s["xh_written"], done(b, min(t + 1, NT - 1)))
                if t == 0:
                    e.wait_ge(s["x1_saved"], before(b, 16))
                for k in range(KC):
                    last = affine(tile_of(x0, k, t), centre(xh, k, t), w1p[:, k:k + 1], par("cpe1_b", k))
                last.then_inc(s["b_centre"], 1)

            def apply_norm(b, t):
                e.wait_ge(s["b_scaled"], done(b, t))
                if t == 0:
                    e.wait_ge(s["d_k"], before(b))
                e.wait_ge(s["b_back"], slot_free(b, t))
                for i in range(SUB):
                    last = affine(xnt[:, t % 2, i, :], as_tokens(pairs[t % 2])[:, i, :], rs["b"][:, t, i:i + 1],
                                  nb[:, t, i:i + 1])
                last.then_inc(s["b_applied"], 1)

            def gain_and_split(b, t):
                e.wait_ge(s["b_back"], done(b, t))
                e.wait_ge(s["b_lo"], slot_free(b, t))
                e.wait_ge(s["c_product"], slot_free(b, t, 2 * KC))
                if t == 0:
                    e.wait_ge(s["g_product"], before(b))
                    e.wait_ge(s["d_q"], before(b))
                for k in range(KC):
                    affine(xnf[:, t % 2, k, :], pairs[2][:, k, :], par("norm1_g", k), par("norm1_b", k))
                for k in range(KC):
                    last = affine(p_hi[:, t % 2, k, :], pairs[2][:, k, :], par("norm1_g", k), par("norm1_b", k))
                last.then_inc(s["b_hi"], 1)

            def projections_out(b, t, js):
                if t == 0:
                    e.wait_ge(s["f_lo"], before(b))
                    e.wait_ge(s["f_num"], before(b))
                for j in js:
                    e.wait_ge(s["c_product"], earlier(b, t, 2 * KC, j + 1))
                    k = j % KC
                    if j < KC:
                        last = e.activation(tile_of(act, k, t), pairs[3][:, j % 2, :], ACT.Silu,
                                            bias=par("actp_b", k))
                    else:
                        last = e.activation(centre(ph, k, t), pairs[3][:, j % 2, :], ACT.Identity,
                                            bias=par("in_b", k))
                    last.then_inc(s["c_out"], 1)

            def conv2_centre(b, t):
                e.wait_ge(s["c_out"], done(b, min(t + 1, NT - 1), 2 * KC))
                e.wait_ge(s["d_silu"], slot_free(b, t))
                if t == 0:
                    e.wait_ge(s["f_sum"], before(b))
                for k in range(KC):
                    last = affine(conv[:, t % 2, k, :], centre(ph, k, t), par("dwc_w1", k), par("dwc_b", k))
                last.then_inc(s["d_centre"], 1)

            def silu_v(b, t):
                e.wait_ge(s["d_taps"], done(b, t))
                if t == 0:
                    e.wait_ge(s["zeroed"], 2)
                    e.wait_ge(s["f_taps"], before(b))
                e.activation(centres(vh, t), conv[:, t % 2], ACT.Silu).then_inc(s["d_silu"], 1)

            def exp_k(b, t):
                e.wait_ge(s["d_kz"], done(b, t))
                e.wait_ge(s["d_k"], slot_free(b, t))
                if t == 0:
                    e.wait_ge(s["b_back"], done(b, NT - 1))
                e.activation(xnt[:, t % 2], kt[:, t % 2], ACT.Exp).then_inc(s["d_kexp"], 1)

            def exp_q(b, t):
                e.wait_ge(s["d_qproduct"], done(b, t))
                e.wait_ge(s["d_q"], slot_free(b, t))
                if t == 0:
                    e.wait_ge(s["b_lo"], done(b, NT - 1))
                e.wait_ge(s["d_taps"], done(b, min(t + 1, NT - 1)))
                for k in range(KC):
                    e.activation(xnf[:, t % 2, k, :], pairs[2][:, k, :], ACT.Exp, bias=par("q_b", k))
                for k in range(KC):
                    last = e.activation(centre(ph, k, t), pairs[2][:, k, :], ACT.Relu, bias=par("q_b", k))
                last.then_inc(s["d_qparts"], 1)

            def lepe_centre(b, t):
                e.wait_ge(s["f_sum"], slot_free(b, t))
                if t == 0:
                    e.wait_ge(s["d_silu"], done(b, NT - 1))
                for k in range(KC):
                    last = affine(conv[:, t % 2, k, :], centre(vh, k, t), par("lepe_w1", k), par("lepe_b", k))
                last.then_inc(s["f_centre"], 1)

            def copy_z(b, t):
                e.wait_ge(s["f_zrows"], done(b, t))
                e.wait_ge(s["f_a"], earlier(b, t))
                e.copy(zs, pairs[1][:]).then_inc(s["f_z"], 1)

            def gated_high(b, t):
                e.wait_ge(s["f_gated"], done(b, t))
                if t < 2:
                    e.wait_ge(s["d_qproduct"], done(b, NT - 1))
                else:
                    e.wait_ge(s["g_product"], slot_free(b, t))
                e.copy(p_hi[:, t % 2], act[:, :, t * TOK:(t + 1) * TOK]).then_inc(s["f_hi"], 1)

            with e.Fori(0, BATCHES) as b:
                for t in range(NT):
                    copy_xn(b, t)
                for step in range(NT + 2):
                    if step < NT:
                        conv1_centre(b, step)
                    if 0 <= step - 1 < NT:
                        apply_norm(b, step - 1)
                    if step >= 2:
                        projections_out(b, step - 2, range(0, KC))
                    if 0 <= step - 1 < NT:
                        gain_and_split(b, step - 1)
                    if step >= 2:
                        projections_out(b, step - 2, range(KC, 2 * KC))
                for step in range(NT + 1):
                    if step < NT:
                        conv2_centre(b, step)
                    if step >= 1:
                        exp_k(b, step - 1)
                        if step < NT:
                            exp_q(b, step - 1)
                    if step < NT:
                        silu_v(b, step)
                exp_q(b, NT - 1)
                lepe_centre(b, 0)
                lepe_centre(b, 1)
                for t in range(NT):
                    copy_z(b, t)
                    gated_high(b, t)
                    if t + 2 < NT:
                        lepe_centre(b, t + 2)

        @block.vector
        def _(e):
            start_at_one(e, "vector")
            e.wait_ge(s["params_in"], 48)
            at_ = PARAMS["cpe1_w1"][0]
            e.tensor_scalar(w1p[:], prm[:, at_:at_ + KC], 1.0, None, ALU.add).then_inc(s["centre_taps"], 1)

            def moments(b, t, x, source, ready, count):
                wait_apart(e, s[f"{x}_applied"], before(b))
                e.wait_ge(ready, count)
                e.wait_ge(s[f"{x}_moments"], earlier(b, t))
                for i in range(SUB):
                    last = e.bn_stats(st[x][:, i, :], source(i))
                last.then_inc(s[f"{x}_stats"], 1)
                wait_apart(e, s[f"{x}_stats"], done(b, t))
                for i in range(SUB):
                    last = e.bn_aggr(mv[x][:, t, i, :], st[x][:, i, :])
                last.then_inc(s[f"{x}_moments"], 1)

            def apply_xn(b, t):
                e.wait_ge(s["a_rstd"], done(b, t))
                for i in range(SUB):
                    last = e.tensor_scalar(xt[:, t % 2, i], xt[:, t % 2, i], mv["a"][:, t, i, 0:1],
                                           rs["a"][:, t, i:i + 1], ALU.subtract, ALU.mult)
                last.then_inc(s["a_applied"], 1)

            def side_taps(b, t, x, source, out, taps):
                e.wait_ge(s[f"{x}_centre"], done(b, t))
                for k in range(KC):
                    last = e.scalar_tensor_tensor(out=out(k), in0=centre(source, k, t, -1), scalar=par(taps + "_w0", k),
                                                  in1=out(k), op0=ALU.mult, op1=ALU.add)
                last.then_inc(s[f"{x}_left"], 1)
                e.wait_ge(s[f"{x}_left"], done(b, t))
                for k in range(KC):
                    last = e.scalar_tensor_tensor(out=out(k), in0=centre(source, k, t, 1), scalar=par(taps + "_w2", k),
                                                  in1=out(k), op0=ALU.mult, op1=ALU.add)
                last.then_inc(s[f"{x}_taps"], 1)

            def v_high(b, t):
                e.wait_ge(s["d_silu"], done(b, t))
                if t < 2:
                    e.wait_ge(s["c_product"], done(b, NT - 1, 2 * KC))
                else:
                    e.wait_ge(s["d_qproduct"], slot_free(b, t))
                e.tensor_copy(p_hi[:, t % 2], centres(vh, t)).then_inc(s["d_hi"], 1)

            def v_and_k(b, t):
                e.wait_ge(s["d_vtokens"], done(b, t))
                e.wait_ge(s["e_kv"], slot_free(b, t))
                if t == 0:
                    e.wait_ge(s["f_gated"], before(b))
                e.tensor_copy(vt[:, t % 2, :, :, 0:P], as_tokens(pairs[0]).rearrange("p s (k n) -> p s k n", k=KC)) \
                    .then_inc(s["d_vcopied"], 1)
                e.wait_ge(s["d_kproduct"], done(b, t))
                e.tensor_tensor(kt[:, t % 2], as_tokens(pairs[1]), kb[:].unsqueeze(1).to_broadcast([P, SUB, C]),
                                ALU.add).then_inc(s["d_kz"], 1)

            def elu_k(b, t):
                e.wait_ge(s["d_kexp"], done(b, t))
                e.tensor_scalar(xnt[:, t % 2], xnt[:, t % 2], 1.0, None, ALU.min).then_inc(s["d_kmin"], 1)
                e.wait_ge(s["d_kmin"], done(b, t))
                e.scalar_tensor_tensor(out=kt[:, t % 2], in0=kt[:, t % 2], scalar=0.0, in1=xnt[:, t % 2],
                                       op0=ALU.max, op1=ALU.add).then_inc(s["d_k"], 1)

            def elu_q(b, t):
                e.wait_ge(s["d_qparts"], done(b, t))
                q = centres(ph, t)
                e.scalar_tensor_tensor(out=q, in0=xnf[:, t % 2], scalar=1.0, in1=q, op0=ALU.min, op1=ALU.add) \
                    .then_inc(s["d_q"], 1)

            def mean_kv(b):
                e.wait_ge(s["e_kv"], done(b, NT - 1))
                kvp = pairs[3][:, 0, 0:KC * (P + 1)].rearrange("p (k n) -> p k n", k=KC)
                for k in range(KC):
                    e.scalar_tensor_tensor(out=kvs[:, k, :], in0=kvp[:, k, 0:P], scalar=1.0 / N,
                                           in1=const("same_head"), op0=ALU.mult, op1=ALU.mult)
                    last = e.tensor_scalar(kden[:, k, :], head_rows[:, k, :], kvp[:, k, P:P + 1], 1.0 / N,
                                           ALU.mult, ALU.mult)
                last.then_inc(s["e_masked"], 1)
                rotated = pairs[3][:, 1, 0:KC * P].rearrange("p (k n) -> p k n", k=KC)
                e.wait_ge(s["e_rot1"], b + 1)
                e.tensor_copy(kvr[:], rotated).then_inc(s["e_kvr"], 1)
                e.wait_ge(s["e_rot2"], b + 1)
                e.tensor_copy(kve[:], rotated).then_inc(s["e_kve"], 1)
                e.wait_ge(s["e_den"], b + 1)
                e.tensor_scalar(zi[:], pairs[3][:, 0, :], Z_EPS, None, ALU.add).then_inc(s["e_den_eps"], 1)
                e.wait_ge(s["e_den_eps"], b + 1)
                e.reciprocal(zi[:], zi[:]).then_inc(s["e_z"], 1)

            def lepe(b, t):
                side_taps(b, t, "f", vh, lambda k: conv[:, t % 2, k, :], "lepe")

            def attention_out(b, t):
                e.wait_ge(s["f_z"], done(b, t))
                e.wait_ge(s["f_num"], done(b, t))
                e.wait_ge(s["f_gated"], earlier(b, t))
                e.tensor_tensor(at, pairs[0][:], zs, ALU.mult).then_inc(s["f_a"], 1)
                e.wait_ge(s["f_a"], done(b, t))
                e.wait_ge(s["f_taps"], done(b, t))
                e.tensor_tensor(at, at, conv[:, t % 2], ALU.add).then_inc(s["f_sum"], 1)

            def x1(b, t):
                e.wait_ge(s["g_product"], done(b, t))
                for k in range(KC):
                    last = e.scalar_tensor_tensor(out=tile_of(x0, k, t), in0=pairs[2][:, k, :], scalar=par("out_b", k),
                                                  in1=tile_of(x0, k, t), op0=ALU.add, op1=ALU.add)
                last.then_inc(s["g_x1"], 1)

            with e.Fori(0, BATCHES) as b:
                for step in range(NT + 1):
                    if step < NT:
                        moments(b, step, "a", lambda i, t=step: xt[:, t % 2, i, :], x_in[step % 2],
                                b * (16 * NT // 2) + 16 * (step // 2 + 1))
                    if step >= 1:
                        apply_xn(b, step - 1)
                with e.If(b < 1):
                    e.wait_ge(s["wa_in"], 16)
                    e.tensor_copy(wa_hi[:], wa_raw).then_inc(s["wa_hi_done"], 1)
                for t in range(NT):
                    side_taps(b, t, "b", xh, lambda k, t=t: tile_of(x0, k, t), "cpe1")
                    moments(b, t, "b", lambda i: as_tokens(pairs[t % 2])[:, i, :], s["b_tokens"], done(b, t))
                for step in range(NT + 1):
                    if step < NT:
                        side_taps(b, step, "d", ph, lambda k: conv[:, step % 2, k, :], "dwc")
                    if step >= 1:
                        v_and_k(b, step - 1)
                        elu_k(b, step - 1)
                    if step < NT:
                        v_high(b, step)
                    if step >= 1:
                        elu_q(b, step - 1)
                mean_kv(b)
                lepe(b, 0)
                lepe(b, 1)
                for step in range(NT + 1):
                    if step < NT:
                        attention_out(b, step)
                    if step >= 1:
                        x1(b, step - 1)
                    if step + 2 < NT:
                        lepe(b, step + 2)

        @block.tensor
        def _(e):
            start_at_one(e, "tensor")
            e.wait_ge(s["params_in"], 48)

            def attn_w(w, name, m):
                at_ = A_COLS[name] + m * P
                return lambda k: w[:, k, at_:at_ + P]

            def part(buf, t):
                return lambda k: buf[:, t % 2, k, :]

            def a_channels(b, t):
                e.wait_ge(s["a_applied"], done(b, t))
                e.wait_ge(s["xh_written"], slot_free(b, t))
                to_channels(e, pairs[t % 2], lambda i: xt[:, t % 2, i, :], ident).then_inc(s["a_transposed"], 1)

            def norm_tokens(b, t):
                e.wait_ge(s["b_taps"], done(b, t))
                if t < 2:
                    e.wait_ge(s["xh_written"], done(b, NT - 1))
                else:
                    e.wait_ge(s["b_applied"], slot_free(b, t))
                to_tokens(e, pairs[t % 2], lambda k: tile_of(x0, k, t), ident).then_inc(s["b_tokens"], 1)

            def norm_back(b, t):
                e.wait_ge(s["b_applied"], done(b, t))
                e.wait_ge(s["b_hi"], earlier(b, t))
                to_channels(e, pairs[2], lambda i: xnt[:, t % 2, i, :], ident).then_inc(s["b_back"], 1)

            def projections(b, t, js):
                if t == 0:
                    e.wait_ge(s["wa_lo_done"], 1)
                e.wait_ge(s["b_lo"], done(b, t))
                for j in js:
                    m, name = j % KC, "actp" if j < KC else "in"
                    e.wait_ge(s["c_out"], earlier(b, t, 2 * KC, max(j - 1, 0)))
                    split_product(e, pairs[3][:, j % 2, :], attn_w(wa_hi, name, m), attn_w(wa_lo, name, m),
                                  part(p_hi, t), part(p_lo, t), KC).then_inc(s["c_product"], 1)

            def v_tokens(b, t):
                e.wait_ge(s["d_silu"], done(b, t))
                e.wait_ge(s["d_vcopied"], earlier(b, t))
                to_tokens(e, pairs[0], lambda k: centre(vh, k, t), ident).then_inc(s["d_vtokens"], 1)

            def k_and_q(b, t):
                e.wait_ge(s["d_lo"], done(b, t))
                e.wait_ge(s["d_kz"], earlier(b, t))
                kc = A_COLS["k"]
                for i in range(SUB):
                    cols = slice(i * P, (i + 1) * P)
                    last = split_product(e, as_tokens(pairs[1])[:, i, :],
                                         lambda k: p_hi[:, t % 2, k, cols], lambda k: p_lo[:, t % 2, k, cols],
                                         lambda k: wa_hi[:, k, kc:kc + C], lambda k: wa_lo[:, k, kc:kc + C], KC)
                last.then_inc(s["d_kproduct"], 1)
                e.wait_ge(s["d_qparts"], earlier(b, t))
                for m in range(KC):
                    last = split_product(e, pairs[2][:, m, :], attn_w(wa_hi, "q", m), attn_w(wa_lo, "q", m),
                                         part(p_hi, t), part(p_lo, t), KC)
                last.then_inc(s["d_qproduct"], 1)

            def add_kv(b, t):
                e.wait_ge(s["d_k"], done(b, t))
                e.wait_ge(s["d_vcopied"], done(b, t))
                kvp = pairs[3][:, 0, 0:KC * (P + 1)].rearrange("p (k n) -> p k n", k=KC)
                for i in range(SUB):
                    for k in range(KC):
                        last = e.matmul(kvp[:, k, :], kt[:, t % 2, i, k * P:(k + 1) * P], vt[:, t % 2, i, k, :],
                                        start=(t == 0 and i == 0 and k == 0), stop=(t == NT - 1 and i == SUB - 1),
                                        skip_group_check=True)
                last.then_inc(s["e_kv"], 1)

            def rotate_kv(b):
                rotated = pairs[3][:, 1, 0:KC * P].rearrange("p (k n) -> p k n", k=KC)
                for n, (before_, source, after) in enumerate((("e_masked", kvs, "e_rot1"), ("e_kvr", kvr, "e_rot2"))):
                    e.wait_ge(s[before_], b + 1)
                    for k in range(KC):
                        last = e.matmul(rotated[:, k, :], rope[:, n, k, :], source[:, k, :], start=True, stop=True)
                    last.then_inc(s[after], 1)

            def denominators(b):
                e.wait_ge(s["d_q"], done(b, NT - 1))
                for t in range(NT):
                    for k in range(KC):
                        last = e.matmul(pairs[3][t * HQ:(t + 1) * HQ, 0, :], kden[:, k, :], centre(ph, k, t),
                                        start=(k == 0), stop=(k == KC - 1))
                last.then_inc(s["e_den"], 1)

            def numerators(b, t):
                e.wait_ge(s["e_kve"], b + 1)
                if t == 0:
                    e.wait_ge(s["d_vcopied"], done(b, NT - 1))
                e.wait_ge(s["f_a"], earlier(b, t))
                for k in range(KC):
                    last = e.matmul(pairs[0][:, k, :], kve[:, k, :], centre(ph, k, t), start=True, stop=True)
                last.then_inc(s["f_num"], 1)

            def spread_z(b, t):
                e.wait_ge(s["e_z"], b + 1)
                if t == 0:
                    e.wait_ge(s["d_kz"], done(b, NT - 1))
                e.wait_ge(s["f_z"], earlier(b, t))
                rows = slice(t * HQ, (t + 1) * HQ)
                for k in range(KC):
                    last = e.matmul(pairs[1][:, k, :], expand[rows, k, :], zi[rows, :], start=True, stop=True)
                last.then_inc(s["f_zrows"], 1)

            def out_proj(b, t):
                e.wait_ge(s["f_lo"], done(b, t))
                if t == 0:
                    e.wait_ge(s["d_qparts"], done(b, NT - 1))
                e.wait_ge(s["g_x1"], earlier(b, t))
                for m in range(KC):
                    last = split_product(e, pairs[2][:, m, :], attn_w(wa_hi, "out", m), attn_w(wa_lo, "out", m),
                                         part(p_hi, t), part(p_lo, t), KC)
                last.then_inc(s["g_product"], 1)

            with e.Fori(0, BATCHES) as b:
                e.wait_ge(s["f_a"], before(b))
                e.wait_ge(s["f_z"], before(b))
                for t in range(NT):
                    a_channels(b, t)
                e.wait_ge(s["g_x1"], before(b))
                for step in range(NT + 2):
                    if step >= 2:
                        projections(b, step - 2, range(0, KC))
                    if 0 <= step - 1 < NT:
                        norm_back(b, step - 1)
                    if step >= 2:
                        projections(b, step - 2, range(KC, 2 * KC))
                    if step < NT:
                        norm_tokens(b, step)
                e.wait_ge(s["b_hi"], done(b, NT - 1))
                e.wait_ge(s["c_out"], done(b, NT - 1, 2 * KC))
                for step in range(NT + 1):
                    if step < NT:
                        v_tokens(b, step)
                        k_and_q(b, step)
                    if step >= 1:
                        add_kv(b, step - 1)
                rotate_kv(b)
                denominators(b)
                for step in range(NT + 1):
                    if step < NT:
                        numerators(b, step)
                        spread_z(b, step)
                    if step >= 1:
                        out_proj(b, step - 1)


def mlp_part(nc, x, params, consts, rows, w_fc1, w_fc2, w_gated, x1_scratch, y_scratch, weights, wide_flag):
    with ExitStack() as ctx:
        def sb(name, shape, dt=F32):
            return ctx.enter_context(nc.sbuf_tensor(name, shape, dt))

        def sem(name):
            return ctx.enter_context(nc.semaphore(name))

        token_banks, back_banks, fc1_banks, fc2_banks = (
            ctx.enter_context(nc.psum_tensor(f"m_banks{i}", [P, 2, TOK], F32)) for i in range(4))

        wf1_hi, wf1_lo = sb("wf1_hi", [P, KC, HID], F32R), sb("wf1_lo", [P, KC, HID], F32R)
        wf2_hi, wf2_lo = sb("wf2_hi", [P, KH, C], F32R), sb("wf2_lo", [P, KH, C], F32R)
        stage = sb("stage", [P, PIECE])
        low_bits = sb("low_bits", [P, PIECE // 2], I32)
        prm = sb("m_prm", [P, N_PARAMS])
        ident = sb("m_ident", [P, P])
        ones = sb("m_ones", [P, 1])
        small = sb("m_small", [P, 3, SUB])
        w1p = sb("m_w1p", [P, KC])
        xw = sb("xw", [P, KC, TOK + 2])
        x2 = sb("x2", [P, KC, TOK])
        y = sb("m_y", [P, 2, SUB, C])
        fc2_bias = sb("fc2_bias", [P, C])
        xnt = sb("m_xnt", [P, SUB, C])
        xnf = sb("m_xnf", [P, KC, TOK])
        p_hi, p_lo = sb("m_p_hi", [P, KC, TOK], F32R), sb("m_p_lo", [P, KC, TOK], F32R)
        hf = sb("hf", [P, 2, TOK])
        h_hi, h_lo = sb("h_hi", [P, KH, TOK], F32R), sb("h_lo", [P, KH, TOK], F32R)
        st = sb("m_st", [P, SUB, 6])
        mv = sb("m_mv", [P, SUB, 2])
        rs = sb("m_rs", [P, SUB])
        nb = sb("m_nb", [P, SUB])
        bits = sb("bits", [P, 1])
        wf1_raw = y[:].rearrange("p a s c -> p (a s c)").rearrange("p (k n) -> p k n", k=KC)
        wf2_raw = stage[:, 0:KH * C].rearrange("p (k n) -> p k n", k=KH)

        once = ("prm_in", "bias_in", "wf1_in", "wf2_in", "wf1_hi_done", "wf1_lo_done", "wf2_hi_done", "wf2_lo_done",
                "ones_set", "centre_taps", "bits_zeroed", "bits_max", "bits_sum", "flag_set")
        per_tile = {
            "sync": ("xw_in", "x_in", "w_staged", "w_in", "y_saved"),
            "gpsimd": ("h_var", "h_rstd", "h_mean", "h_scaled", "h_split", "x_biased"),
            "scalar": ("h_centre", "h_applied", "h_hi", "i_gelu"),
            "vector": ("h_left", "h_taps", "h_stats", "h_moments", "h_x2", "i_lo", "i_y", "w_checked"),
            "tensor": ("h_tokens", "h_back", "i_fc1", "i_fc2"),
        }
        s = {name: sem(f"m_{name}") for name in once + sum(per_tile.values(), ())}

        def start_at_one(e, engine):
            for name in per_tile[engine]:
                e.sem_inc(s[name], 1)

        def par(name, i):
            at_, width = PARAMS[name]
            assert i < width
            return prm[:, at_ + i:at_ + i + 1]

        def count(b, t, per_tile=1, more=0):
            return b * (NT * per_tile) + (t * per_tile + more + 1)

        def wait_apart(e, semaphore, value):
            value = e.compute_val(value)
            e.wait_ge(s["prm_in"], 32)
            e.wait_ge(semaphore, value)

        block = ctx.enter_context(nc.Block())

        @block.sync
        def _(sp):
            sp.dma_start(prm[:], params).then_inc(s["prm_in"], 16)
            sp.dma_start(ident[:], consts[:, 0:P]).then_inc(s["prm_in"], 16)
            start_at_one(sp, "sync")

            def load_window(b, t):
                sp.dma_start(xw[:], x1_scratch[b][:, :, t * TOK:(t + 1) * TOK + 2]).then_inc(s["xw_in"], 16)

            def following(b, step, records):
                return nc.s_assert_within(b + step, 0, records - 1,
                                          skip_runtime_bounds_check_because="the branch excludes the last batch")

            def load_x(g, slot):
                sp.dma_start(y[:, slot], x[g]).then_inc(s["x_in"], 16)

            load_window(0, 0)
            sp.dma_start(wf1_raw, w_fc1).then_inc(s["wf1_in"], 16)
            sp.dma_start(wf2_raw, w_fc2).then_inc(s["wf2_in"], 16)
            sp.dma_start(fc2_bias[:], rows[:, C:2 * C]).then_inc(s["bias_in"], 16)
            sp.wait_ge(s["h_taps"], 2)
            load_window(0, 1)
            sp.wait_ge(s["wf1_lo_done"], 1)
            load_x(0, 0)
            sp.wait_ge(s["wf2_lo_done"], 1)
            sp.dma_start(stage[:], w_gated[0]).then_inc(s["w_staged"], 16)

            with sp.Fori(0, BATCHES) as b:
                for t in range(NT):
                    wait_apart(sp, s["x_biased"], count(b, t + 1))
                    wait_apart(sp, s["y_saved"], count(b, t, 16))
                    if t + 1 < NT:
                        load_x(b * NT + (t + 1), (t + 1) % 2)
                    else:
                        with sp.If(b < BATCHES - 1):
                            load_x(following(b * NT, NT, TILES), 0)
                        with sp.Else():
                            load_x(0, 0)
                    wait_apart(sp, s["h_taps"], count(b, t + 2))
                    if t + 2 < NT:
                        load_window(b, t + 2)
                    else:
                        with sp.If(b < BATCHES - 1):
                            load_window(following(b, 1, BATCHES), t + 2 - NT)
                        if t + 2 == NT:
                            with sp.Else():
                                load_window(0, 0)
                    wait_apart(sp, s["w_staged"], count(b, t, 16, 16))
                    sp.dma_start(weights[:, b * NT + t, :].bitcast(F32), stage[:]).then_inc(s["w_in"], 16)
                    wait_apart(sp, s["w_in"], count(b, t, 16, 16))
                    if t + 1 < NT:
                        sp.dma_start(stage[:], w_gated[b * NT + (t + 1)]).then_inc(s["w_staged"], 16)
                    else:
                        with sp.If(b < BATCHES - 1):
                            sp.dma_start(stage[:], w_gated[following(b * NT, NT, TILES)]).then_inc(s["w_staged"], 16)
                    wait_apart(sp, s["i_y"], count(b, t + 1))
                    sp.dma_start(y_scratch[b * NT + t], y[:, t % 2]).then_inc(s["y_saved"], 16)
            sp.wait_ge(s["xw_in"], 16 * (TILES + 1) + 1)
            sp.wait_ge(s["y_saved"], 16 * TILES + 1)

        @block.gpsimd
        def _(pool):
            start_at_one(pool, "gpsimd")
            pool.memset(small[:, 0, :], EPS)
            pool.memset(small[:, 1, :], -0.5)
            pool.memset(small[:, 2, :], -1.0)
            pool.memset(ones[:], 1.0).then_inc(s["ones_set"], 1)
            pool.wait_ge(s["wf1_hi_done"], 1)
            pool.tensor_tensor(wf1_lo[:], wf1_raw, wf1_hi[:].bitcast(F32), ALU.subtract).then_inc(s["wf1_lo_done"], 1)

            def norm(n):
                pool.wait_ge(s["ones_set"], 1)
                pool.wait_ge(s["h_moments"], n)
                pool.wait_ge(s["h_applied"], n - 1)
                pool.tensor_tensor(rs[:], mv[:, :, 1], small[:, 0, :], ALU.add).then_inc(s["h_var"], 1)
                pool.wait_ge(s["h_var"], n)
                pool.tensor_tensor(rs[:], rs[:], small[:, 1, :], ALU.pow).then_inc(s["h_rstd"], 1)
                pool.wait_ge(s["h_rstd"], n)
                pool.tensor_tensor(nb[:], mv[:, :, 0], rs[:], ALU.mult).then_inc(s["h_mean"], 1)
                pool.wait_ge(s["h_mean"], n)
                pool.tensor_tensor(nb[:], nb[:], small[:, 2, :], ALU.mult).then_inc(s["h_scaled"], 1)
                pool.wait_ge(s["h_hi"], n)
                pool.tensor_tensor(p_lo[:], xnf[:], p_hi[:].bitcast(F32), ALU.subtract).then_inc(s["h_split"], 1)

            def bias(n, slot):
                pool.wait_ge(s["bias_in"], 16)
                pool.wait_ge(s["x_in"], n * 16 - 15)
                pool.tensor_tensor(y[:, slot], y[:, slot], fc2_bias[:].unsqueeze(1).to_broadcast([P, SUB, C]),
                                   ALU.add).then_inc(s["x_biased"], 1)

            bias(2, 0)
            norm(2)
            with pool.Fori(0, BATCHES) as b:
                for t in range(NT):
                    bias(count(b, t + 2), (t + 1) % 2)
                    norm(count(b, t + 2))

        @block.scalar
        def _(e):
            start_at_one(e, "scalar")
            e.wait_ge(s["prm_in"], 32)
            e.wait_ge(s["centre_taps"], 1)

            def centre(n):
                e.wait_ge(s["xw_in"], n * 16 - 15)
                e.wait_ge(s["h_tokens"], n - 1)
                for k in range(KC):
                    last = e.activation(x2[:, k, :], xw[:, k, 1:TOK + 1], ACT.Identity,
                                        bias=par("cpe2_b", k), scale=w1p[:, k:k + 1])
                last.then_inc(s["h_centre"], 1)

            def apply_norm(n):
                e.wait_ge(s["h_scaled"], n)
                e.wait_ge(s["h_x2"], n)
                e.wait_ge(s["h_back"], n - 1)
                tokens = as_tokens(token_banks)
                for i in range(SUB):
                    last = e.activation(xnt[:, i, :], tokens[:, i, :], ACT.Identity, bias=nb[:, i:i + 1],
                                        scale=rs[:, i:i + 1])
                last.then_inc(s["h_applied"], 1)

            def gain_and_split(n):
                e.wait_ge(s["h_back"], n)
                e.wait_ge(s["h_split"], n - 1)
                for buf in (xnf, p_hi):
                    for k in range(KC):
                        last = e.activation(buf[:, k, :], back_banks[:, k, :], ACT.Identity,
                                            bias=par("norm2_b", k), scale=par("norm2_g", k))
                last.then_inc(s["h_hi"], 1)

            def gelu(b, t, m):
                e.wait_ge(s["i_fc1"], count(b, t, KH, m + 1))
                e.wait_ge(s["i_lo"], count(b, t, KH, max(m - 1, 0)))
                if m == 0:
                    e.wait_ge(s["i_fc2"], count(b, t))
                for out in (hf[:, m % 2, :], h_hi[:, m, :]):
                    last = e.activation(out, fc1_banks[:, m % 2, :], ACT.Gelu, bias=par("fc1_b", m))
                last.then_inc(s["i_gelu"], 1)

            centre(2)
            e.wait_ge(s["wf2_in"], 16)
            e.copy(wf2_hi[:], wf2_raw).then_inc(s["wf2_hi_done"], 1)
            apply_norm(2)
            gain_and_split(2)
            with e.Fori(0, BATCHES) as b:
                for t in range(NT):
                    for m in range(KH):
                        gelu(b, t, m)
                        if m == 1:
                            centre(count(b, t + 2))
                    apply_norm(count(b, t + 2))
                    gain_and_split(count(b, t + 2))

        @block.vector
        def _(e):
            start_at_one(e, "vector")
            e.wait_ge(s["prm_in"], 32)
            at_ = PARAMS["cpe2_w1"][0]
            e.tensor_scalar(w1p[:], prm[:, at_:at_ + KC], 1.0, None, ALU.add).then_inc(s["centre_taps"], 1)
            e.memset(low_bits[:], 0).then_inc(s["bits_zeroed"], 1)
            e.wait_ge(s["wf1_in"], 16)
            e.tensor_copy(wf1_hi[:], wf1_raw).then_inc(s["wf1_hi_done"], 1)
            e.wait_ge(s["wf2_hi_done"], 1)
            e.tensor_tensor(wf2_lo[:], wf2_raw, wf2_hi[:].bitcast(F32), ALU.subtract).then_inc(s["wf2_lo_done"], 1)

            def side_taps(n):
                e.wait_ge(s["h_centre"], n)
                for tap, name, signal in ((0, "cpe2_w0", "h_left"), (2, "cpe2_w2", "h_taps")):
                    for k in range(KC):
                        last = e.scalar_tensor_tensor(out=x2[:, k, :], in0=xw[:, k, tap:tap + TOK],
                                                      scalar=par(name, k), in1=x2[:, k, :],
                                                      op0=ALU.mult, op1=ALU.add)
                    last.then_inc(s[signal], 1)
                    e.wait_ge(s[signal], n)

            def moments(n, slot):
                wait_apart(e, s["h_tokens"], n)
                e.wait_ge(s["h_moments"], n - 1)
                for i in range(SUB):
                    last = e.bn_stats(st[:, i, :], as_tokens(token_banks)[:, i, :])
                last.then_inc(s["h_stats"], 1)
                wait_apart(e, s["h_scaled"], n - 1)
                e.wait_ge(s["h_stats"], n)
                for i in range(SUB):
                    last = e.bn_aggr(mv[:, i, :], st[:, i, :])
                last.then_inc(s["h_moments"], 1)
                e.wait_ge(s["x_biased"], n)
                e.tensor_tensor(y[:, slot], as_tokens(token_banks), y[:, slot], ALU.add).then_inc(s["h_x2"], 1)

            def check(piece, n):
                e.wait_ge(s["w_in"], n * 16 + 1)
                for half in range(2):
                    columns_ = weights[:, piece, half * (PIECE // 2):(half + 1) * (PIECE // 2)].bitcast(I32)
                    e.wait_ge(s["w_checked"], n * 2 + (half - 1))
                    e.scalar_tensor_tensor(out=low_bits[:], in0=columns_, scalar=0xFFF, in1=low_bits[:],
                                           op0=ALU.bitwise_and, op1=ALU.bitwise_or).then_inc(s["w_checked"], 1)

            side_taps(2)
            moments(2, 0)
            with e.Fori(0, BATCHES) as b:
                for t in range(NT):
                    for m in range(KH):
                        e.wait_ge(s["i_gelu"], count(b, t, KH, m + 1))
                        if m == 0:
                            e.wait_ge(s["i_fc2"], count(b, t))
                        e.tensor_tensor(h_lo[:, m, :], hf[:, m % 2, :], h_hi[:, m, :].bitcast(F32), ALU.subtract) \
                            .then_inc(s["i_lo"], 1)
                        if m == 1:
                            side_taps(count(b, t + 2))
                        if m == 5:
                            moments(count(b, t + 2), (t + 1) % 2)
                    check(b * NT + t, b * NT + (t + 1))
                    e.wait_ge(s["i_fc2"], count(b, t + 1))
                    e.wait_ge(s["h_x2"], count(b, t + 1))
                    e.tensor_tensor(y[:, t % 2], as_tokens(fc2_banks), y[:, t % 2], ALU.add).then_inc(s["i_y"], 1)
            e.wait_ge(s["w_checked"], 2 * TILES + 1)
            e.tensor_reduce(bits[:], low_bits[:], AX_X, ALU.max).then_inc(s["bits_max"], 1)
            e.wait_ge(s["bits_sum"], 1)
            e.tensor_reduce(wide_flag[:], token_banks[0:1, 0, 0:1], AX_X, ALU.max).then_inc(s["flag_set"], 1)

        @block.tensor
        def _(e):
            start_at_one(e, "tensor")
            e.wait_ge(s["prm_in"], 32)

            def norm_tokens(n):
                e.wait_ge(s["h_taps"], n)
                e.wait_ge(s["h_applied"], n - 1)
                e.wait_ge(s["h_x2"], n - 1)
                to_tokens(e, token_banks, lambda k: x2[:, k, :], ident[:]).then_inc(s["h_tokens"], 1)

            def norm_back(n):
                e.wait_ge(s["h_applied"], n)
                e.wait_ge(s["h_hi"], n - 1)
                to_channels(e, back_banks, lambda i: xnt[:, i, :], ident[:]).then_inc(s["h_back"], 1)

            norm_tokens(2)
            norm_back(2)
            e.wait_ge(s["wf1_lo_done"], 1)
            e.wait_ge(s["wf2_lo_done"], 1)
            with e.Fori(0, BATCHES) as b:
                for t in range(NT):
                    e.wait_ge(s["h_split"], count(b, t + 1))
                    for m in range(KH):
                        e.wait_ge(s["i_gelu"], count(b, t, KH, max(m - 1, 0)))
                        split_product(e, fc1_banks[:, m % 2, :], lambda k: wf1_hi[:, k, m * P:(m + 1) * P],
                                      lambda k: wf1_lo[:, k, m * P:(m + 1) * P], lambda k: p_hi[:, k, :],
                                      lambda k: p_lo[:, k, :], KC).then_inc(s["i_fc1"], 1)
                        if m == 4:
                            norm_tokens(count(b, t + 2))
                    e.wait_ge(s["i_y"], count(b, t))
                    for i in range(SUB):
                        cols = slice(i * P, (i + 1) * P)
                        for k in range(KH):
                            if i == 0:
                                e.wait_ge(s["i_lo"], count(b, t, KH, k + 1))
                            for n, (v, w) in enumerate(((h_hi, wf2_hi), (h_lo, wf2_hi), (h_hi, wf2_lo))):
                                last = e.matmul(as_tokens(fc2_banks)[:, i, :], v[:, k, cols], w[:, k, :],
                                                start=(k == 0 and n == 0), stop=(k == KH - 1 and n == 2))
                        if i == 1:
                            norm_back(count(b, t + 2))
                    last.then_inc(s["i_fc2"], 1)
            e.wait_ge(s["h_applied"], TILES + 2)
            e.wait_ge(s["h_x2"], TILES + 2)
            e.wait_ge(s["bits_max"], 1)
            e.matmul(token_banks[0:1, 0, 0:1], ones[:], bits[:], start=True, stop=True).then_inc(s["bits_sum"], 1)


def gated_part(nc, params, rows, weights, wide_flag, xn_scratch, y_scratch, out):
    with ExitStack() as ctx:
        def sb(name, shape, dt=F32):
            return ctx.enter_context(nc.sbuf_tensor(name, shape, dt))

        def sem(name):
            return ctx.enter_context(nc.semaphore(name))

        banks = [ctx.enter_context(nc.psum_tensor(f"g_banks{i}", [P, 2, TOK], F32)) for i in range(4)]
        gate_banks, up_banks, layer_banks, down_banks = banks
        hidden_banks = [layer_banks[:, 0, :], layer_banks[:, 1, :], gate_banks[:, 0, :], gate_banks[:, 1, :]]

        flat = weights[:].rearrange("p t n -> p (t n)")
        W, at_column = {}, 0
        for name, k, width in GATED_LAYERS:
            W[name] = flat[:, at_column:at_column + k * width].rearrange("p (k n) -> p k n", k=k)
            at_column += k * width
        prm = sb("g_prm", [P, N_PARAMS])
        down_scale = sb("down_scale", [P, C])
        xn = sb("g_xn", [P, KC, TOK])
        x_hi, x_lo = sb("x_hi", [P, KC, TOK], F32R), sb("x_lo", [P, KC, TOK], F32R)
        a_hi, a_lo = sb("a_hi", [P, KH, TOK], F32R), sb("a_lo", [P, KH, TOK], F32R)
        b_hi, b_lo = sb("b_hi", [P, KH, TOK], F32R), sb("b_lo", [P, KH, TOK], F32R)
        silu = sb("g_silu", [P, 2, TOK])
        full = sb("full", [P, 2, TOK])
        y = sb("y", [P, SUB, C])
        ot = sb("g_ot", [P, SUB, C])

        once = ("prm_in",)
        per_tile = {
            "sync": ("xn_in", "y_in", "out_stored"),
            "gpsimd": ("x_split",),
            "scalar": ("x_hi_done", "silu_done", "u_hi", "h1_gelu", "h2_gelu"),
            "vector": ("gated", "u_lo", "h1_lo", "h2_lo", "scaled", "out_sum"),
            "tensor": ("gate_mm", "up_mm", "h1_mm", "h2_mm", "down_mm"),
        }
        s = {name: sem(f"g_{name}") for name in once + sum(per_tile.values(), ())}

        def start_at_one(e, engine):
            for name in per_tile[engine]:
                e.sem_inc(s[name], 1)

        def count(g, per_tile, more=0):
            return g * per_tile + (more + 1)

        def par(name, i):
            at_, width = PARAMS[name]
            assert i < width
            return prm[:, at_ + i:at_ + i + 1]

        def wait_apart(e, semaphore, value):
            count = e.compute_val(value)
            e.wait_ge(s["prm_in"], 32)
            e.wait_ge(semaphore, count)

        block = ctx.enter_context(nc.Block())

        @block.sync
        def _(sp):
            start_at_one(sp, "sync")
            sp.dma_start(xn[:], xn_scratch[0]).then_inc(s["xn_in"], 16)
            sp.dma_start(prm[:], params).then_inc(s["prm_in"], 16)
            sp.dma_start(down_scale[:], rows[:, 2 * C:3 * C]).then_inc(s["prm_in"], 16)
            with sp.Fori(0, TILES) as g:
                wait_apart(sp, s["x_split"], count(g, 1, 1))
                with sp.If(g < TILES - 1):
                    next_ = nc.s_assert_within(g + 1, 0, TILES - 1,
                                               skip_runtime_bounds_check_because="the branch excludes the last tile")
                    sp.dma_start(xn[:], xn_scratch[next_]).then_inc(s["xn_in"], 16)
                with sp.Else():
                    sp.dma_start(xn[:], xn_scratch[0]).then_inc(s["xn_in"], 16)
                wait_apart(sp, s["out_sum"], count(g, 1))
                sp.dma_start(y[:], y_scratch[g]).then_inc(s["y_in"], 16)
                wait_apart(sp, s["out_sum"], count(g, 1, 1))
                sp.dma_start(out[g], ot[:]).then_inc(s["out_stored"], 16)
            sp.wait_ge(s["xn_in"], 16 * (TILES + 1) + 1)
            sp.wait_ge(s["out_stored"], 16 * TILES + 1)

        @block.gpsimd
        def _(pool):
            start_at_one(pool, "gpsimd")

            def low_of_x(n):
                pool.wait_ge(s["x_hi_done"], n)
                pool.tensor_tensor(x_lo[:], xn[:], x_hi[:].bitcast(F32), ALU.subtract).then_inc(s["x_split"], 1)

            low_of_x(2)
            with pool.Fori(0, TILES) as g:
                low_of_x(g + 3)

        @block.scalar
        def _(e):
            start_at_one(e, "scalar")
            e.wait_ge(s["prm_in"], 32)

            def high_of_x(n):
                e.wait_ge(s["xn_in"], n * 16 - 15)
                e.wait_ge(s["up_mm"], n * KH - (2 * KH - 1))
                e.copy(x_hi[:], xn[:]).then_inc(s["x_hi_done"], 1)

            def gelu(g, m, mm, done, low, out_hi, scale):
                e.wait_ge(s[mm], count(g, KH, m + 1))
                e.wait_ge(s[low], count(g, KH, max(m - 1, 0)))
                for out_ in (full[:, m % 2, :], out_hi[:, m, :]):
                    last = e.activation(out_, hidden_banks[m % 4], ACT.Gelu, scale=par(scale, m))
                last.then_inc(s[done], 1)

            def high_of_gated(g, m):
                e.wait_ge(s["gated"], count(g, KH, m + 1))
                if m == 0:
                    e.wait_ge(s["down_mm"], count(g, 1))
                e.copy(a_hi[:, m, :], full[:, m % 2, :]).then_inc(s["u_hi"], 1)

            high_of_x(2)
            with e.Fori(0, TILES) as g:
                for m in range(KH):
                    e.wait_ge(s["gate_mm"], count(g, KH, m + 1))
                    e.wait_ge(s["gated"], count(g, KH, max(m - 1, 0)))
                    e.activation(silu[:, m % 2, :], gate_banks[:, m % 2, :], ACT.Silu, scale=par("w1_s", m)) \
                        .then_inc(s["silu_done"], 1)
                    if m >= 1:
                        high_of_gated(g, m - 1)
                high_of_gated(g, KH - 1)
                e.wait_ge(s["h2_mm"], count(g, KH))
                e.wait_ge(s["u_lo"], count(g, KH, KH))
                for m in range(KH):
                    gelu(g, m, "h1_mm", "h1_gelu", "h1_lo", b_hi, "h1_s")
                    if m == 3:
                        high_of_x(g + 3)
                e.wait_ge(s["h1_mm"], count(g, KH, KH))
                e.wait_ge(s["h1_lo"], count(g, KH, KH))
                for m in range(KH):
                    gelu(g, m, "h2_mm", "h2_gelu", "h2_lo", a_hi, "h2_s")

        @block.vector
        def _(e):
            start_at_one(e, "vector")
            def low(g, m, out_lo, out_hi, ready, after):
                e.wait_ge(s[ready], count(g, KH, m + 1))
                e.tensor_tensor(out_lo[:, m, :], full[:, m % 2, :], out_hi[:, m, :].bitcast(F32), ALU.subtract) \
                    .then_inc(s[after], 1)

            e.wait_ge(s["prm_in"], 32)
            with e.Fori(0, TILES) as g:
                for m in range(KH):
                    e.wait_ge(s["up_mm"], count(g, KH, m + 1))
                    e.wait_ge(s["silu_done"], count(g, KH, m + 1))
                    if m == 0:
                        e.wait_ge(s["h2_lo"], count(g, KH))
                        e.wait_ge(s["down_mm"], count(g, 1))
                    else:
                        e.wait_ge(s["u_lo"], count(g, KH, max(m - 1, 0)))
                        e.wait_ge(s["u_hi"], count(g, KH, max(m - 1, 0)))
                    e.scalar_tensor_tensor(out=full[:, m % 2, :], in0=up_banks[:, m % 2, :], scalar=par("w2_s", m),
                                           in1=silu[:, m % 2, :], op0=ALU.mult, op1=ALU.mult).then_inc(s["gated"], 1)
                    if m >= 1:
                        low(g, m - 1, a_lo, a_hi, "u_hi", "u_lo")
                low(g, KH - 1, a_lo, a_hi, "u_hi", "u_lo")
                e.wait_ge(s["h2_mm"], count(g, KH))
                for m in range(KH):
                    low(g, m, b_lo, b_hi, "h1_gelu", "h1_lo")
                for m in range(KH):
                    low(g, m, a_lo, a_hi, "h2_gelu", "h2_lo")
                e.wait_ge(s["out_stored"], count(g, 16))
                e.wait_ge(s["down_mm"], count(g, 1, 1))
                e.tensor_tensor(ot[:], as_tokens(down_banks), down_scale[:].unsqueeze(1).to_broadcast([P, SUB, C]),
                                ALU.mult).then_inc(s["scaled"], 1)
                e.wait_ge(s["y_in"], count(g, 16, 16))
                e.wait_ge(s["scaled"], count(g, 1, 1))
                e.tensor_tensor(ot[:], ot[:], y[:], ALU.add).then_inc(s["out_sum"], 1)

        @block.tensor
        def _(e):
            start_at_one(e, "tensor")
            e.wait_ge(s["prm_in"], 32)

            def add(bank, w, v, wide, first, last):
                dt = F32 if wide else F32R
                return e.matmul(bank, w.bitcast(dt), v.bitcast(dt), start=first, stop=last)

            def first_layer(g, wide):
                e.wait_ge(s["x_split"], count(g, 1, 1))
                e.wait_ge(s["h2_gelu"], count(g, KH))
                for m in range(KH):
                    cols = slice(m * P, (m + 1) * P)
                    for name, bank, reader, signal in (("gate", gate_banks, "silu_done", "gate_mm"),
                                                       ("up", up_banks, "gated", "up_mm")):
                        e.wait_ge(s[reader], count(g, KH, max(m - 1, 0)))
                        for k in range(KC):
                            for n, v in enumerate((x_hi, x_lo)):
                                last = add(bank[:, m % 2, :], W[name][:, k, cols], v[:, k, :], wide,
                                           k == 0 and n == 0, k == KC - 1 and n == 1)
                        last.then_inc(s[signal], 1)

            def hidden_layer(g, wide, w, hi, lo, inputs, gelu, mm):
                for ms in [(0, 1)] + [(m,) for m in range(2, KH)]:
                    e.wait_ge(s[gelu], count(g, KH, max(ms[-1] - 3, 0)))
                    for k in range(KH):
                        if ms[0] == 0:
                            e.wait_ge(s[inputs], count(g, KH, k + 1))
                        for m in ms:
                            for n, v in enumerate((hi, lo)):
                                last = add(hidden_banks[m % 4], w[:, k, m * P:(m + 1) * P], v[:, k, :], wide,
                                           k == 0 and n == 0, k == KH - 1 and n == 1)
                            if k == KH - 1:
                                last.then_inc(s[mm], 1)

            def last_layer(g, wide):
                e.wait_ge(s["scaled"], count(g, 1))
                for groups in ((0, 2), (1, 3)):
                    for k in range(KH):
                        if groups[0] == 0:
                            e.wait_ge(s["h2_lo"], count(g, KH, k + 1))
                        for i in groups:
                            for n, v in enumerate((a_hi, a_lo)):
                                last = add(as_tokens(down_banks)[:, i, :], v[:, k, i * P:(i + 1) * P], W["down"][:, k, :],
                                           wide, k == 0 and n == 0, k == KH - 1 and n == 1)
                last.then_inc(s["down_mm"], 1)

            def all_tiles(wide):
                with e.Fori(0, TILES) as g:
                    first_layer(g, wide)
                    e.wait_ge(s["silu_done"], count(g, KH, KH))
                    hidden_layer(g, wide, W["h1"], a_hi, a_lo, "u_lo", "h1_gelu", "h1_mm")
                    e.wait_ge(s["h1_gelu"], count(g, KH, KH - 2))
                    hidden_layer(g, wide, W["h2"], b_hi, b_lo, "h1_lo", "h2_gelu", "h2_mm")
                    last_layer(g, wide)

            flag = e.value_load(wide_flag[0:1, 0:1])
            with e.If(flag > 0):
                all_tiles(True)
            with e.Else():
                all_tiles(False)


def build(nc, t):
    x = t["x"].rearrange("g (s p) c -> g p s c", p=P)
    out = t["out"].rearrange("g (s p) c -> g p s c", p=P)
    xn_scratch = nc.dram_tensor("xn_scratch", (TILES, P, KC, TOK), F32, kind="Internal").ap()
    x1_scratch = nc.dram_tensor("x1_scratch", (BATCHES, P, KC, N + 2), F32, kind="Internal").ap()
    y_scratch = nc.dram_tensor("y_scratch", (TILES, P, SUB, C), F32, kind="Internal").ap()
    attention_part(nc, x, t["params"], t["consts"], t["rows"], t["w_attn"], xn_scratch, x1_scratch)
    with nc.sbuf_tensor("gated_weights", [P, TILES, PIECE], F32R) as weights, \
            nc.sbuf_tensor("wide_flag", [1, 1], I32) as wide_flag:
        mlp_part(nc, x, t["params"], t["consts"], t["rows"], t["w_fc1"], t["w_fc2"], t["w_gated"], x1_scratch,
                 y_scratch, weights, wide_flag)
        gated_part(nc, t["params"], t["rows"], weights, wide_flag, xn_scratch, y_scratch, out)


def chunked(w):
    w = np.asarray(w)
    return np.ascontiguousarray(w.reshape(w.shape[0] // P, P, w.shape[1]).transpose(1, 0, 2))


def columns(v):
    v = np.asarray(v)
    return v.reshape(-1, P).T


def kernel(**inputs):
    import concourse.bacc as bacc
    from concourse.bass_utils import run_bass_kernel_spmd as run

    a = {k.removeprefix("L0_attn_"): np.asarray(v) for k, v in inputs.items() if k.startswith("L0_attn_")}
    f = {k.removeprefix("L0_ffn_"): np.asarray(v) for k, v in inputs.items() if k.startswith("L0_ffn_")}
    vectors = {}
    for conv in ("cpe1", "dwc", "lepe", "cpe2"):
        for tap in range(3):
            vectors[f"{conv}_w{tap}"] = a[f"{conv}_w"][:, 0, tap]
        vectors[f"{conv}_b"] = a[f"{conv}_b"]
    for name in ("norm1_g", "norm1_b", "in_b", "actp_b", "out_b", "norm2_g", "norm2_b", "fc1_b"):
        vectors[name] = a[name]
    vectors["q_b"] = a["qk_b"][:C]
    for name in ("w1_s", "w2_s", "h1_s", "h2_s"):
        vectors[name] = f[name]
    arrays = {
        "x": a["x"].reshape(TILES, TOK, C),
        "params": np.concatenate([columns(vectors[name]) for name in PARAMS], axis=1),
        "consts": constants(),
        "rows": np.concatenate([np.tile(v[None, :], (P, 1)) for v in (a["qk_b"][C:], a["fc2_b"], f["w3_s"])], axis=1),
        "w_attn": chunked(np.concatenate([a["actp_w"], a["in_w"], a["qk_w"], a["out_w"]], axis=1)),
        "w_fc1": chunked(a["fc1_w"]),
        "w_fc2": chunked(a["fc2_w"]),
        "w_gated": np.concatenate(
            [chunked(f[f"{w}_w"].T).reshape(P, -1) for w in ("w1", "w2", "h1", "h2", "w3")], axis=1)
        .reshape(P, TILES, PIECE).transpose(1, 0, 2),
    }
    arrays = {k: np.ascontiguousarray(v) for k, v in arrays.items()}
    nc = bacc.Bacc("TRN2", target_bir_lowering=False, num_devices=1)
    t = {k: nc.dram_tensor(k, v.shape, mybir.dt.from_np(v.dtype), kind="ExternalInput").ap()
         for k, v in arrays.items()}
    t["out"] = nc.dram_tensor("out", (TILES, TOK, C), F32, kind="ExternalOutput").ap()
    build(nc, t)
    r = run(nc, [arrays], core_ids=[0])
    return r.results[0]["out"].reshape(BATCHES, N, C)
```

```python
from contextlib import ExitStack

import numpy as np

import concourse.bass as bass
from concourse import mybir

F32 = mybir.dt.float32
F32R = mybir.dt.float32r
I32 = mybir.dt.int32
ALU = mybir.AluOpType
ACT = mybir.ActivationFunctionType
AX_X = mybir.AxisListType.X

P = 128
BATCHES, N, C = 2, 2048, 256
KC = C // P
HEADS = 16
D = C // HEADS
HID = 4 * C
KH = HID // P
TOK = 512
SUB = TOK // P
NT = N // TOK
TILES = BATCHES * NT
HQ = 32
EPS = 1e-5
Z_EPS = 1e-6

GATED_LAYERS = (("gate", KC, HID), ("up", KC, HID), ("h1", KH, HID), ("h2", KH, HID), ("down", KH, C))
PIECE = sum(k * n for _, k, n in GATED_LAYERS) // TILES

PARAMS = {}
for _name, _width in (
    ("cpe1_w0", KC), ("cpe1_w1", KC), ("cpe1_w2", KC), ("cpe1_b", KC),
    ("norm1_g", KC), ("norm1_b", KC), ("in_b", KC), ("actp_b", KC),
    ("dwc_w0", KC), ("dwc_w1", KC), ("dwc_w2", KC), ("dwc_b", KC), ("q_b", KC),
    ("lepe_w0", KC), ("lepe_w1", KC), ("lepe_w2", KC), ("lepe_b", KC), ("out_b", KC),
    ("cpe2_w0", KC), ("cpe2_w1", KC), ("cpe2_w2", KC), ("cpe2_b", KC),
    ("norm2_g", KC), ("norm2_b", KC), ("fc1_b", KH),
    ("w1_s", KH), ("w2_s", KH), ("h1_s", KH), ("h2_s", KH),
):
    PARAMS[_name] = (sum(w for _, w in PARAMS.values()), _width)
N_PARAMS = sum(w for _, w in PARAMS.values())

A_COLS = {"actp": 0, "in": C, "q": 2 * C, "k": 3 * C, "out": 4 * C}
A_WIDTH = 5 * C


def constants():
    identity = np.eye(P, dtype=np.float32)
    head_of = np.arange(C) // D
    same_head = np.equal.outer(np.arange(P) // D, np.arange(P) // D).astype(np.float32)
    head_rows = np.zeros((P, KC, HQ), np.float32)
    expand = np.zeros((P, KC, P), np.float32)
    for c in range(C):
        head_rows[c % P, c // P, head_of[c]] = 1.0
        for q in range(P // HQ):
            expand[q * HQ + head_of[c], c // P, c % P] = 1.0
    pairs = C // 2
    theta = 1.0 / np.float32(10000.0) ** (np.arange(pairs, dtype=np.float32) / np.float32(pairs))
    cos, sin = np.cos(theta), np.sin(theta)
    rope = np.zeros((P, 2, KC, P), np.float32)
    for j in range(pairs):
        e, chunk = (2 * j) % P, (2 * j) // P
        rot = np.array([[cos[j], -sin[j]], [sin[j], cos[j]]], np.float32)
        rope[e:e + 2, 1, chunk, e:e + 2] = rot
        rope[e:e + 2, 0, chunk, e:e + 2] = rot.T
    return np.concatenate([identity, same_head, head_rows.reshape(P, -1), expand.reshape(P, -1),
                           rope.reshape(P, -1)], axis=1)


CONST_COLS = {"identity": (0, P), "same_head": (P, P), "head_rows": (2 * P, KC * HQ),
              "expand": (2 * P + KC * HQ, KC * P), "rope": (2 * P + KC * HQ + KC * P, 2 * KC * P)}
N_CONST = 2 * P + KC * HQ + 3 * KC * P


def as_tokens(pair):
    return pair[:].rearrange("p a b -> p (a b)").rearrange("p (s c) -> p s c", s=SUB)


def to_channels(e, bank, source, ident):
    for i in range(SUB):
        for k in range(KC):
            last = e.transpose(bank[:, k, i * P:(i + 1) * P], source(i)[:, k * P:(k + 1) * P], ident)
    return last


def to_tokens(e, bank, source, ident):
    for i in range(SUB):
        for k in range(KC):
            last = e.transpose(as_tokens(bank)[:, i, k * P:(k + 1) * P], source(k)[:, i * P:(i + 1) * P], ident)
    return last


def parameter(prm, name, i):
    column, width = PARAMS[name]
    assert i < width
    return prm[:, column + i:column + i + 1]


def split_product(e, out, w_hi, w_lo, x_hi, x_lo, chunks):
    for k in range(chunks):
        for n, (w, v) in enumerate(((w_hi, x_hi), (w_hi, x_lo), (w_lo, x_hi))):
            last = e.matmul(out, w(k), v(k), start=(k == 0 and n == 0), stop=(k == chunks - 1 and n == 2))
    return last


def attention_part(nc, x, params, consts, rows, w_attn, w_fc1, w_fc2, prm, ident, wf, xn_scratch, x1_scratch):
    with ExitStack() as ctx:
        def sb(name, shape, dt=F32):
            return ctx.enter_context(nc.sbuf_tensor(name, shape, dt))

        def sem(name):
            return ctx.enter_context(nc.semaphore(name))

        pairs = [ctx.enter_context(nc.psum_tensor(f"banks{i}", [P, 2, TOK], F32)) for i in range(4)]

        xh = sb("xh", [P, KC, N + 2])
        x0_framed = sb("x0", [P, KC, N + 2])
        x0 = x0_framed[:, :, 1:N + 1]
        act = sb("act", [P, KC, N])
        ph = sb("ph", [P, KC, N + 2])
        vh = sb("vh", [P, KC, N + 2])
        wa_hi, wa_lo = sb("wa_hi", [P, KC, A_WIDTH], F32R), sb("wa_lo", [P, KC, A_WIDTH], F32R)
        cst = sb("cst", [P, N_CONST - P])
        kb = sb("kb", [P, C])
        w1p = sb("w1p", [P, KC])
        small = sb("small", [P, 3, SUB])
        xt = sb("xt", [P, 2, SUB, C])
        xnt = sb("xnt", [P, 2, SUB, C])
        xnf = sb("xnf", [P, 2, KC, TOK])
        p_hi, p_lo = sb("p_hi", [P, 2, KC, TOK], F32R), sb("p_lo", [P, 2, KC, TOK], F32R)
        conv = sb("conv", [P, 2, KC, TOK])
        kt = sb("kt", [P, 2, SUB, C])
        vt = sb("vt", [P, 2, SUB, KC, P + 1])
        st = {x: sb(f"st_{x}", [P, SUB, 6]) for x in "ab"}
        mv = {x: sb(f"mv_{x}", [P, NT, SUB, 2]) for x in "ab"}
        rs = {x: sb(f"rs_{x}", [P, NT, SUB]) for x in "ab"}
        nb = sb("nb", [P, NT, SUB])
        kvs = sb("kvs", [P, KC, P])
        kvr = sb("kvr", [P, KC, P])
        kve = sb("kve", [P, KC, P])
        kden = sb("kden", [P, KC, HQ])
        zi = sb("zi", [P, TOK])
        wf_raw = {"wf1": conv[:].rearrange("p a k n -> p (a k n)").rearrange("p (k n) -> p k n", k=KC),
                  "wf2": kt[:].rearrange("p a s c -> p (a s c)").rearrange("p (k n) -> p k n", k=KH)}
        wa_raw = vh[:].rearrange("p k n -> p (k n)")[:, 0:KC * A_WIDTH].rearrange("p (k n) -> p k n", k=KC)

        def const(name):
            at_, width = CONST_COLS[name]
            return cst[:, at_ - P:at_ - P + width]

        head_rows = const("head_rows").rearrange("p (k h) -> p k h", k=KC)
        expand = const("expand").rearrange("p (k n) -> p k n", k=KC)
        rope = const("rope").rearrange("p (w k n) -> p w k n", w=2, k=KC)

        once = ("params_in", "consts_in", "wa_in", "zeroed", "centre_taps", "wa_hi_done", "wa_lo_done",
                "wf1_in", "wf2_in", "wf1_hi_done", "wf2_hi_done", "wf1_lo_done", "wf2_lo_done",
                "e_masked", "e_rot1", "e_kvr", "e_rot2", "e_kve", "e_den", "e_den_eps", "e_z")
        per_tile = {
            "sync": ("xn_saved",) + tuple(f"x1_saved{t}" for t in range(NT)),
            "gpsimd": ("a_var", "a_rstd", "b_var", "b_rstd", "b_mean", "b_scaled", "b_lo", "d_lo", "f_gated", "f_lo"),
            "scalar": ("xh_written", "b_centre", "b_applied", "b_hi", "c_out", "d_centre", "d_silu", "d_kexp",
                       "d_qparts", "f_centre", "f_z", "f_hi"),
            "vector": ("a_stats", "a_moments", "a_applied", "b_left", "b_taps", "b_stats", "b_moments", "d_left",
                       "d_taps", "d_hi", "d_vcopied", "d_kz", "d_kmin", "d_k", "d_q", "f_left", "f_taps", "f_a",
                       "f_sum", "g_x1"),
            "tensor": ("a_transposed", "b_tokens", "b_back", "c_product", "d_vtokens", "d_kproduct",
                       "d_qproduct", "e_kv", "f_num", "f_zrows", "g_product"),
        }
        s = {name: sem(name) for name in once + sum(per_tile.values(), ())}

        def start_at_one(e, engine):
            for name in per_tile[engine]:
                e.sem_inc(s[name], 1)

        x_in = [sem("x_in0"), sem("x_in1")]

        assert NT == 4

        def done(b, t, per_tile=1):
            return b * (NT * per_tile) + ((t + 1) * per_tile + 1)

        def earlier(b, t, per_tile=1, more=0):
            return b * (NT * per_tile) + (t * per_tile + more + 1)

        def slot_free(b, t, per_tile=1):
            return b * (NT * per_tile) + (max(t - 1, 0) * per_tile + 1)

        def before(b, per_tile=1):
            return b * (NT * per_tile) + 1

        def wait_apart(e, semaphore, value):
            count = e.compute_val(value)
            e.wait_ge(s["params_in"], 32)
            e.wait_ge(semaphore, count)

        def attention(t):
            return kt[:, t % 2].rearrange("p s c -> p (s c)").rearrange("p (k n) -> p k n", k=KC)

        def spread(t):
            return xnt[:, t % 2].rearrange("p s c -> p (s c)").rearrange("p (k n) -> p k n", k=KC)

        def following(b):
            return nc.s_assert_within(b + 1, 0, BATCHES - 1,
                                      skip_runtime_bounds_check_because="the branch excludes the last batch")

        def centre(buf, k, t, shift=0):
            return buf[:, k, 1 + shift + t * TOK:1 + shift + (t + 1) * TOK]

        def centres(buf, t):
            return buf[:, :, 1 + t * TOK:1 + (t + 1) * TOK]

        def tile_of(buf, k, t):
            return buf[:, k, t * TOK:(t + 1) * TOK]

        def par(name, i):
            return parameter(prm, name, i)

        block = ctx.enter_context(nc.Block())

        @block.sync
        def _(sp):
            sp.dma_start(prm[:], params).then_inc(s["params_in"], 16)
            sp.dma_start(ident[:], consts[:, 0:P]).then_inc(s["params_in"], 16)
            start_at_one(sp, "sync")

            def load_x(b, t):
                wait_apart(sp, s["a_transposed"], slot_free(b, t))
                sp.dma_start(xt[:, t % 2], x[b * NT + t]).then_inc(x_in[t % 2], 16)

            def save_xn(b, t):
                wait_apart(sp, s["xh_written"], done(b, t))
                sp.dma_start(xn_scratch[b * NT + t], centres(xh, t)).then_inc(s["xn_saved"], 16)

            def save_x1(b, t):
                wait_apart(sp, s["g_x1"], done(b, t))
                cols = slice(1 + t * TOK - (t == 0), 1 + (t + 1) * TOK + (t == NT - 1))
                sp.dma_start(x1_scratch[b][:, :, cols], x0_framed[:, :, cols]).then_inc(s[f"x1_saved{t}"], 16)

            with sp.Fori(0, BATCHES) as b:
                with sp.If(b < 1):
                    load_x(b, 0)
                    load_x(b, 1)
                    sp.dma_start(wa_raw, w_attn).then_inc(s["wa_in"], 16)
                    for t in range(NT):
                        if t + 2 < NT:
                            load_x(b, t + 2)
                        if t == 1:
                            sp.dma_start(cst[:], consts[:, P:]).then_inc(s["consts_in"], 16)
                            sp.dma_start(kb[:], rows[:, 0:C]).then_inc(s["consts_in"], 16)
                            sp.dma_start(wf_raw["wf1"], w_fc1).then_inc(s["wf1_in"], 16)
                            sp.dma_start(wf_raw["wf2"], w_fc2).then_inc(s["wf2_in"], 16)
                        save_xn(b, t)
                with sp.If(b < BATCHES - 1):
                    for t in range(NT):
                        load_x(following(b), t)
                for t in range(NT):
                    save_x1(b, t)
                    with sp.If(b < BATCHES - 1):
                        save_xn(following(b), t)
            sp.wait_ge(s["xn_saved"], 16 * TILES + 1)
            for t in range(NT):
                sp.wait_ge(s[f"x1_saved{t}"], 16 * BATCHES + 1)

        @block.gpsimd
        def _(pool):
            start_at_one(pool, "gpsimd")
            pool.memset(small[:, 0, :], EPS)
            pool.memset(small[:, 1, :], -0.5)
            pool.memset(small[:, 2, :], -1.0)
            for i in range(2):
                pool.memset(vt[:, i, :, :, P:P + 1], 1.0)
            for buf in (x0_framed, xh, ph):
                pool.memset(buf[:, :, 0:1], 0.0)
                last = pool.memset(buf[:, :, N + 1:N + 2], 0.0)
            last.then_inc(s["zeroed"], 1)

            def inverse_deviation(b, t, x):
                pool.wait_ge(s[f"{x}_applied"], before(b))
                pool.wait_ge(s[f"{x}_moments"], done(b, t))
                pool.tensor_tensor(rs[x][:, t], mv[x][:, t, :, 1], small[:, 0, :], ALU.add).then_inc(s[f"{x}_var"], 1)
                pool.wait_ge(s[f"{x}_var"], done(b, t))
                pool.tensor_tensor(rs[x][:, t], rs[x][:, t], small[:, 1, :], ALU.pow).then_inc(s[f"{x}_rstd"], 1)

            def norm_scalars(b, t):
                inverse_deviation(b, t, "b")
                pool.wait_ge(s["b_rstd"], done(b, t))
                pool.tensor_tensor(nb[:, t], mv["b"][:, t, :, 0], rs["b"][:, t], ALU.mult).then_inc(s["b_mean"], 1)
                pool.wait_ge(s["b_mean"], done(b, t))
                pool.tensor_tensor(nb[:, t], nb[:, t], small[:, 2, :], ALU.mult).then_inc(s["b_scaled"], 1)

            def low_part(b, t, hi, lo, source):
                pool.wait_ge(s[hi], done(b, t))
                pool.tensor_tensor(p_lo[:, t % 2], source, p_hi[:, t % 2].bitcast(F32), ALU.subtract) \
                    .then_inc(s[lo], 1)

            def low_of_mlp_weights(w):
                pool.wait_ge(s[w + "_hi_done"], 1)
                pool.tensor_tensor(wf[w + "_lo"], wf_raw[w], wf[w + "_hi"].bitcast(F32), ALU.subtract) \
                    .then_inc(s[w + "_lo_done"], 1)

            def low_of_norm(b, t):
                low_part(b, t, "b_hi", "b_lo", xnf[:, t % 2])

            def low_of_v(b, t):
                low_part(b, t, "d_hi", "d_lo", centres(vh, t))

            def gate(b, t):
                pool.wait_ge(s["f_sum"], done(b, t))
                gated = act[:, :, t * TOK:(t + 1) * TOK]
                pool.tensor_tensor(gated, gated, attention(t), ALU.mult).then_inc(s["f_gated"], 1)

            def low_of_gated(b, t):
                low_part(b, t, "f_hi", "f_lo", act[:, :, t * TOK:(t + 1) * TOK])

            def split_attn_weights():
                pool.wait_ge(s["wa_hi_done"], 1)
                pool.tensor_tensor(wa_lo[:], wa_raw, wa_hi[:].bitcast(F32), ALU.subtract) \
                    .then_inc(s["wa_lo_done"], 1)
                pool.wait_ge(s["wa_lo_done"], 1)
                pool.memset(vh[:, :, 0:1], 0.0)
                pool.memset(vh[:, :, N + 1:N + 2], 0.0).then_inc(s["zeroed"], 1)

            pool.wait_ge(s["zeroed"], 1)
            with pool.Fori(0, BATCHES) as b:
                with pool.If(b < 1):
                    inverse_deviation(b, 0, "a")
                    inverse_deviation(b, 1, "a")
                    inverse_deviation(b, 2, "a")
                norm_scalars(b, 0)
                with pool.If(b < 1):
                    split_attn_weights()
                    inverse_deviation(b, 3, "a")
                    low_of_mlp_weights("wf1")
                norm_scalars(b, 1)
                low_of_norm(b, 0)
                with pool.If(b < 1):
                    low_of_mlp_weights("wf2")
                norm_scalars(b, 2)
                low_of_norm(b, 1)
                with pool.If(b < BATCHES - 1):
                    inverse_deviation(b + 1, 0, "a")
                low_of_norm(b, 2)
                with pool.If(b < BATCHES - 1):
                    inverse_deviation(b + 1, 1, "a")
                norm_scalars(b, 3)
                low_of_norm(b, 3)
                low_of_v(b, 0)
                low_of_v(b, 1)
                low_of_v(b, 2)
                low_of_v(b, 3)
                with pool.If(b < BATCHES - 1):
                    inverse_deviation(b + 1, 2, "a")
                    inverse_deviation(b + 1, 3, "a")
                gate(b, 0)
                low_of_gated(b, 0)
                gate(b, 1)
                low_of_gated(b, 1)
                gate(b, 2)
                low_of_gated(b, 2)
                gate(b, 3)
                low_of_gated(b, 3)

        @block.scalar
        def _(e):
            start_at_one(e, "scalar")
            e.wait_ge(s["params_in"], 32)
            e.wait_ge(s["centre_taps"], 1)
            e.wait_ge(s["zeroed"], 1)

            def affine(out, in_, scale, bias, func=ACT.Identity):
                return e.activation(out, in_, func, bias=bias, scale=scale)

            def copy_xn(b, t):
                if t == 0:
                    e.wait_ge(s["b_taps"], before(b))
                    e.wait_ge(s["xn_saved"], before(b, 16))
                e.wait_ge(s["a_transposed"], done(b, t))
                e.copy(centres(xh, t), pairs[3][:]).then_inc(s["xh_written"], 1)

            def conv1_centre(b, t):
                e.wait_ge(s["xh_written"], done(b, min(t + 1, NT - 1)))
                e.wait_ge(s[f"x1_saved{t}"], b * 16 + 1)
                for k in range(KC):
                    last = affine(tile_of(x0, k, t), centre(xh, k, t), w1p[:, k:k + 1], par("cpe1_b", k))
                last.then_inc(s["b_centre"], 1)

            def apply_norm(b, t):
                e.wait_ge(s["b_scaled"], done(b, t))
                if t == 0:
                    e.wait_ge(s["f_a"], before(b))
                e.wait_ge(s["b_back"], slot_free(b, t))
                for i in range(SUB):
                    last = affine(xnt[:, t % 2, i, :], as_tokens(pairs[1])[:, i, :], rs["b"][:, t, i:i + 1],
                                  nb[:, t, i:i + 1])
                last.then_inc(s["b_applied"], 1)

            def gain_and_split(b, t):
                e.wait_ge(s["b_back"], done(b, t))
                e.wait_ge(s["b_lo"], slot_free(b, t))
                e.wait_ge(s["c_product"], slot_free(b, t, 2 * KC))
                if t == 0:
                    e.wait_ge(s["g_product"], before(b))
                    e.wait_ge(s["d_q"], before(b))
                for k in range(KC):
                    affine(xnf[:, t % 2, k, :], pairs[2][:, k, :], par("norm1_g", k), par("norm1_b", k))
                for k in range(KC):
                    last = affine(p_hi[:, t % 2, k, :], pairs[2][:, k, :], par("norm1_g", k), par("norm1_b", k))
                last.then_inc(s["b_hi"], 1)

            def projections_out(b, t, js):
                if t == 0:
                    e.wait_ge(s["f_lo"], before(b))
                    e.wait_ge(s["f_num"], before(b))
                for j in js:
                    e.wait_ge(s["c_product"], earlier(b, t, 2 * KC, j + 1))
                    k = j % KC
                    if j < KC:
                        last = e.activation(tile_of(act, k, t), pairs[0][:, j % 2, :], ACT.Silu,
                                            bias=par("actp_b", k))
                    else:
                        last = e.activation(centre(ph, k, t), pairs[0][:, j % 2, :], ACT.Identity,
                                            bias=par("in_b", k))
                    last.then_inc(s["c_out"], 1)

            def gates(b, t):
                projections_out(b, t, range(0, KC))

            def in_proj_out(b, t):
                projections_out(b, t, range(KC, 2 * KC))

            def conv2_centre(b, t):
                e.wait_ge(s["c_out"], done(b, min(t + 1, NT - 1), 2 * KC))
                e.wait_ge(s["d_silu"], slot_free(b, t))
                if t == 0:
                    e.wait_ge(s["f_sum"], before(b))
                    e.wait_ge(s["wf1_lo_done"], 1)
                for k in range(KC):
                    last = affine(conv[:, t % 2, k, :], centre(ph, k, t), par("dwc_w1", k), par("dwc_b", k))
                last.then_inc(s["d_centre"], 1)

            def silu_v(b, t):
                e.wait_ge(s["d_taps"], done(b, t))
                if t == 0:
                    e.wait_ge(s["zeroed"], 2)
                    e.wait_ge(s["f_taps"], before(b))
                e.activation(centres(vh, t), conv[:, t % 2], ACT.Silu).then_inc(s["d_silu"], 1)

            def exp_k(b, t):
                e.wait_ge(s["d_kz"], done(b, t))
                e.wait_ge(s["d_k"], slot_free(b, t))
                if t == 0:
                    e.wait_ge(s["b_back"], done(b, NT - 1))
                e.activation(xnt[:, t % 2], kt[:, t % 2], ACT.Exp).then_inc(s["d_kexp"], 1)

            def exp_q(b, t):
                e.wait_ge(s["d_qproduct"], done(b, t))
                e.wait_ge(s["d_q"], slot_free(b, t))
                if t == 0:
                    e.wait_ge(s["b_lo"], done(b, NT - 1))
                e.wait_ge(s["d_taps"], done(b, min(t + 1, NT - 1)))
                for k in range(KC):
                    e.activation(xnf[:, t % 2, k, :], pairs[2][:, k, :], ACT.Exp, bias=par("q_b", k))
                for k in range(KC):
                    last = e.activation(centre(ph, k, t), pairs[2][:, k, :], ACT.Relu, bias=par("q_b", k))
                last.then_inc(s["d_qparts"], 1)

            def lepe_centre(b, t):
                e.wait_ge(s["f_sum"], slot_free(b, t))
                if t < 2:
                    e.wait_ge(s["d_silu"], done(b, t + 2))
                for k in range(KC):
                    last = affine(conv[:, t % 2, k, :], centre(vh, k, t), par("lepe_w1", k), par("lepe_b", k))
                last.then_inc(s["f_centre"], 1)

            def copy_z(b, t):
                e.wait_ge(s["f_zrows"], done(b, t))
                e.wait_ge(s["f_a"], slot_free(b, t))
                if t == 0:
                    e.wait_ge(s["d_k"], done(b, NT - 1))
                e.copy(spread(t), pairs[1][:]).then_inc(s["f_z"], 1)

            def gated_high(b, t):
                e.wait_ge(s["f_gated"], done(b, t))
                if t < 2:
                    e.wait_ge(s["d_qproduct"], done(b, NT - 1))
                else:
                    e.wait_ge(s["g_product"], slot_free(b, t))
                e.copy(p_hi[:, t % 2], act[:, :, t * TOK:(t + 1) * TOK]).then_inc(s["f_hi"], 1)

            with e.Fori(0, BATCHES) as b:
                with e.If(b < 1):
                    copy_xn(b, 0)
                    copy_xn(b, 1)
                conv1_centre(b, 0)
                with e.If(b < 1):
                    copy_xn(b, 2)
                conv1_centre(b, 1)
                apply_norm(b, 0)
                with e.If(b < 1):
                    e.wait_ge(s["wf1_in"], 16)
                    e.copy(wf["wf1_hi"], wf_raw["wf1"]).then_inc(s["wf1_hi_done"], 1)
                gain_and_split(b, 0)
                with e.If(b < 1):
                    copy_xn(b, 3)
                conv1_centre(b, 2)
                conv1_centre(b, 3)
                apply_norm(b, 1)
                gates(b, 0)
                gain_and_split(b, 1)
                apply_norm(b, 2)
                in_proj_out(b, 0)
                gain_and_split(b, 2)
                gates(b, 1)
                in_proj_out(b, 1)
                conv2_centre(b, 0)
                apply_norm(b, 3)
                gates(b, 2)
                gain_and_split(b, 3)
                silu_v(b, 0)
                in_proj_out(b, 2)
                conv2_centre(b, 1)
                gates(b, 3)
                silu_v(b, 1)
                exp_q(b, 0)
                exp_k(b, 0)
                in_proj_out(b, 3)
                conv2_centre(b, 2)
                conv2_centre(b, 3)
                silu_v(b, 2)
                exp_q(b, 1)
                silu_v(b, 3)
                exp_k(b, 1)
                lepe_centre(b, 0)
                lepe_centre(b, 1)
                exp_q(b, 2)
                exp_k(b, 2)
                exp_q(b, 3)
                exp_k(b, 3)
                with e.If(b < BATCHES - 1):
                    copy_xn(b + 1, 0)
                    copy_xn(b + 1, 1)
                copy_z(b, 0)
                copy_z(b, 1)
                lepe_centre(b, 2)
                gated_high(b, 0)
                copy_z(b, 2)
                lepe_centre(b, 3)
                copy_z(b, 3)
                gated_high(b, 1)
                gated_high(b, 2)
                gated_high(b, 3)
                with e.If(b < BATCHES - 1):
                    copy_xn(b + 1, 2)
                    copy_xn(b + 1, 3)

        @block.vector
        def _(e):
            start_at_one(e, "vector")
            e.wait_ge(s["params_in"], 32)
            at_ = PARAMS["cpe1_w1"][0]
            e.tensor_scalar(w1p[:], prm[:, at_:at_ + KC], 1.0, None, ALU.add).then_inc(s["centre_taps"], 1)

            def moments(b, t, x, source, ready, count):
                wait_apart(e, s[f"{x}_applied"], before(b))
                e.wait_ge(ready, count)
                e.wait_ge(s[f"{x}_moments"], earlier(b, t))
                for i in range(SUB):
                    last = e.bn_stats(st[x][:, i, :], source(i))
                last.then_inc(s[f"{x}_stats"], 1)
                wait_apart(e, s[f"{x}_stats"], done(b, t))
                for i in range(SUB):
                    last = e.bn_aggr(mv[x][:, t, i, :], st[x][:, i, :])
                last.then_inc(s[f"{x}_moments"], 1)

            def xn_moments(b, t):
                moments(b, t, "a", lambda i: xt[:, t % 2, i, :], x_in[t % 2],
                        b * (16 * NT // 2) + 16 * (t // 2 + 1))

            def apply_xn(b, t):
                e.wait_ge(s["a_rstd"], done(b, t))
                for i in range(SUB):
                    last = e.tensor_scalar(xt[:, t % 2, i], xt[:, t % 2, i], mv["a"][:, t, i, 0:1],
                                           rs["a"][:, t, i:i + 1], ALU.subtract, ALU.mult)
                last.then_inc(s["a_applied"], 1)

            def side_taps(b, t, x, source, out, taps):
                e.wait_ge(s[f"{x}_centre"], done(b, t))
                for k in range(KC):
                    last = e.scalar_tensor_tensor(out=out(k), in0=centre(source, k, t, -1), scalar=par(taps + "_w0", k),
                                                  in1=out(k), op0=ALU.mult, op1=ALU.add)
                last.then_inc(s[f"{x}_left"], 1)
                e.wait_ge(s[f"{x}_left"], done(b, t))
                for k in range(KC):
                    last = e.scalar_tensor_tensor(out=out(k), in0=centre(source, k, t, 1), scalar=par(taps + "_w2", k),
                                                  in1=out(k), op0=ALU.mult, op1=ALU.add)
                last.then_inc(s[f"{x}_taps"], 1)

            def conv1_sides(b, t):
                side_taps(b, t, "b", xh, lambda k: tile_of(x0, k, t), "cpe1")

            def norm_moments(b, t):
                moments(b, t, "b", lambda i: as_tokens(pairs[1])[:, i, :], s["b_tokens"], done(b, t))

            def conv2_sides(b, t):
                side_taps(b, t, "d", ph, lambda k: conv[:, t % 2, k, :], "dwc")

            def v_high(b, t):
                e.wait_ge(s["d_silu"], done(b, t))
                if t < 2:
                    e.wait_ge(s["c_product"], done(b, NT - 2 + t, 2 * KC))
                else:
                    e.wait_ge(s["d_qproduct"], slot_free(b, t))
                e.tensor_copy(p_hi[:, t % 2], centres(vh, t)).then_inc(s["d_hi"], 1)

            def copy_v(b, t):
                e.wait_ge(s["d_vtokens"], done(b, t))
                e.wait_ge(s["e_kv"], slot_free(b, t))
                e.tensor_copy(vt[:, t % 2, :, :, 0:P], as_tokens(pairs[0]).rearrange("p s (k n) -> p s k n", k=KC)) \
                    .then_inc(s["d_vcopied"], 1)

            def bias_k(b, t):
                e.wait_ge(s["d_kproduct"], done(b, t))
                e.wait_ge(s["e_kv"], slot_free(b, t))
                if t == 0:
                    e.wait_ge(s["f_gated"], before(b))
                    e.wait_ge(s["wf2_lo_done"], 1)
                    e.wait_ge(s["consts_in"], 32)
                e.tensor_tensor(kt[:, t % 2], as_tokens(pairs[1]), kb[:].unsqueeze(1).to_broadcast([P, SUB, C]),
                                ALU.add).then_inc(s["d_kz"], 1)

            def elu_k(b, t):
                e.wait_ge(s["d_kexp"], done(b, t))
                e.tensor_scalar(xnt[:, t % 2], xnt[:, t % 2], 1.0, None, ALU.min).then_inc(s["d_kmin"], 1)
                e.wait_ge(s["d_kmin"], done(b, t))
                e.scalar_tensor_tensor(out=kt[:, t % 2], in0=kt[:, t % 2], scalar=0.0, in1=xnt[:, t % 2],
                                       op0=ALU.max, op1=ALU.add).then_inc(s["d_k"], 1)

            def elu_q(b, t):
                e.wait_ge(s["d_qparts"], done(b, t))
                q = centres(ph, t)
                e.scalar_tensor_tensor(out=q, in0=xnf[:, t % 2], scalar=1.0, in1=q, op0=ALU.min, op1=ALU.add) \
                    .then_inc(s["d_q"], 1)

            def mask_kv(b):
                e.wait_ge(s["e_kv"], done(b, NT - 1))
                kvp = pairs[3][:, 0, 0:KC * (P + 1)].rearrange("p (k n) -> p k n", k=KC)
                for k in range(KC):
                    e.scalar_tensor_tensor(out=kvs[:, k, :], in0=kvp[:, k, 0:P], scalar=1.0 / N,
                                           in1=const("same_head"), op0=ALU.mult, op1=ALU.mult)
                    last = e.tensor_scalar(kden[:, k, :], head_rows[:, k, :], kvp[:, k, P:P + 1], 1.0 / N,
                                           ALU.mult, ALU.mult)
                last.then_inc(s["e_masked"], 1)

            rotated = pairs[3][:, 1, 0:KC * P].rearrange("p (k n) -> p k n", k=KC)

            def rotated_once(b):
                e.wait_ge(s["e_rot1"], b + 1)
                e.tensor_copy(kvr[:], rotated).then_inc(s["e_kvr"], 1)

            def rotated_twice(b):
                e.wait_ge(s["e_rot2"], b + 1)
                e.tensor_copy(kve[:], rotated).then_inc(s["e_kve"], 1)

            def shift_denominators(b):
                e.wait_ge(s["e_den"], b + 1)
                e.tensor_scalar(zi[:], pairs[3][:, 0, :], Z_EPS, None, ALU.add).then_inc(s["e_den_eps"], 1)

            def invert_denominators(b):
                e.wait_ge(s["e_den_eps"], b + 1)
                e.reciprocal(zi[:], zi[:]).then_inc(s["e_z"], 1)

            def lepe(b, t):
                side_taps(b, t, "f", vh, lambda k: conv[:, t % 2, k, :], "lepe")

            def attention_out(b, t):
                e.wait_ge(s["f_z"], done(b, t))
                e.wait_ge(s["f_num"], done(b, t))
                e.wait_ge(s["f_gated"], slot_free(b, t))
                if t == 0:
                    e.wait_ge(s["e_kv"], done(b, NT - 1))
                e.tensor_tensor(attention(t), pairs[0][:], spread(t), ALU.mult).then_inc(s["f_a"], 1)

            def add_lepe(b, t):
                e.wait_ge(s["f_a"], done(b, t))
                e.wait_ge(s["f_taps"], done(b, t))
                e.tensor_tensor(attention(t), attention(t), conv[:, t % 2], ALU.add).then_inc(s["f_sum"], 1)

            def x1(b, t):
                e.wait_ge(s["g_product"], done(b, t))
                for k in range(KC):
                    last = e.scalar_tensor_tensor(out=tile_of(x0, k, t), in0=pairs[2][:, k, :], scalar=par("out_b", k),
                                                  in1=tile_of(x0, k, t), op0=ALU.add, op1=ALU.add)
                last.then_inc(s["g_x1"], 1)

            with e.Fori(0, BATCHES) as b:
                with e.If(b < 1):
                    xn_moments(b, 0)
                    xn_moments(b, 1)
                    apply_xn(b, 0)
                    apply_xn(b, 1)
                conv1_sides(b, 0)
                with e.If(b < 1):
                    xn_moments(b, 2)
                norm_moments(b, 0)
                with e.If(b < 1):
                    apply_xn(b, 2)
                    e.wait_ge(s["wa_in"], 16)
                    e.tensor_copy(wa_hi[:], wa_raw).then_inc(s["wa_hi_done"], 1)
                    xn_moments(b, 3)
                conv1_sides(b, 1)
                with e.If(b < 1):
                    e.wait_ge(s["wf2_in"], 16)
                    e.tensor_copy(wf["wf2_hi"], wf_raw["wf2"]).then_inc(s["wf2_hi_done"], 1)
                    apply_xn(b, 3)
                norm_moments(b, 1)
                conv1_sides(b, 2)
                conv1_sides(b, 3)
                norm_moments(b, 2)
                with e.If(b < BATCHES - 1):
                    xn_moments(b + 1, 0)
                    xn_moments(b + 1, 1)
                    apply_xn(b + 1, 0)
                norm_moments(b, 3)
                with e.If(b < BATCHES - 1):
                    apply_xn(b + 1, 1)
                conv2_sides(b, 0)
                v_high(b, 0)
                conv2_sides(b, 1)
                bias_k(b, 0)
                v_high(b, 1)
                elu_q(b, 0)
                elu_k(b, 0)
                copy_v(b, 0)
                conv2_sides(b, 2)
                conv2_sides(b, 3)
                v_high(b, 2)
                copy_v(b, 1)
                bias_k(b, 1)
                copy_v(b, 2)
                elu_q(b, 1)
                v_high(b, 3)
                elu_k(b, 1)
                bias_k(b, 2)
                lepe(b, 0)
                elu_q(b, 2)
                lepe(b, 1)
                copy_v(b, 3)
                elu_k(b, 2)
                bias_k(b, 3)
                elu_q(b, 3)
                elu_k(b, 3)
                mask_kv(b)
                rotated_once(b)
                shift_denominators(b)
                rotated_twice(b)
                invert_denominators(b)
                with e.If(b < BATCHES - 1):
                    xn_moments(b + 1, 2)
                    xn_moments(b + 1, 3)
                    apply_xn(b + 1, 2)
                attention_out(b, 0)
                add_lepe(b, 0)
                with e.If(b < BATCHES - 1):
                    apply_xn(b + 1, 3)
                attention_out(b, 1)
                add_lepe(b, 1)
                lepe(b, 2)
                attention_out(b, 2)
                lepe(b, 3)
                add_lepe(b, 2)
                x1(b, 0)
                attention_out(b, 3)
                add_lepe(b, 3)
                x1(b, 1)
                x1(b, 2)
                x1(b, 3)

        @block.tensor
        def _(e):
            start_at_one(e, "tensor")
            e.wait_ge(s["params_in"], 32)

            def attn_w(w, name, m):
                at_ = A_COLS[name] + m * P
                return lambda k: w[:, k, at_:at_ + P]

            def part(buf, t):
                return lambda k: buf[:, t % 2, k, :]

            def a_channels(b, t):
                e.wait_ge(s["a_applied"], done(b, t))
                e.wait_ge(s["xh_written"], earlier(b, t))
                to_channels(e, pairs[3], lambda i: xt[:, t % 2, i, :], ident[:]).then_inc(s["a_transposed"], 1)

            def norm_tokens(b, t):
                e.wait_ge(s["b_taps"], done(b, t))
                e.wait_ge(s["b_applied"], earlier(b, t))
                if t == 0:
                    e.wait_ge(s["f_z"], before(b))
                to_tokens(e, pairs[1], lambda k: tile_of(x0, k, t), ident[:]).then_inc(s["b_tokens"], 1)

            def norm_back(b, t):
                e.wait_ge(s["b_applied"], done(b, t))
                e.wait_ge(s["b_hi"], earlier(b, t))
                if t == 0:
                    e.wait_ge(s["g_x1"], before(b))
                to_channels(e, pairs[2], lambda i: xnt[:, t % 2, i, :], ident[:]).then_inc(s["b_back"], 1)

            def projections(b, t, js):
                if t == 0:
                    e.wait_ge(s["wa_lo_done"], 1)
                    e.wait_ge(s["f_a"], before(b))
                e.wait_ge(s["b_lo"], done(b, t))
                for j in js:
                    m, name = j % KC, "actp" if j < KC else "in"
                    e.wait_ge(s["c_out"], earlier(b, t, 2 * KC, max(j - 1, 0)))
                    split_product(e, pairs[0][:, j % 2, :], attn_w(wa_hi, name, m), attn_w(wa_lo, name, m),
                                  part(p_hi, t), part(p_lo, t), KC).then_inc(s["c_product"], 1)

            def act_proj(b, t):
                projections(b, t, range(0, KC))

            def in_proj(b, t):
                projections(b, t, range(KC, 2 * KC))

            def v_tokens(b, t):
                e.wait_ge(s["d_silu"], done(b, t))
                e.wait_ge(s["d_vcopied"], earlier(b, t))
                if t == 0:
                    e.wait_ge(s["c_out"], done(b, NT - 1, 2 * KC))
                to_tokens(e, pairs[0], lambda k: centre(vh, k, t), ident[:]).then_inc(s["d_vtokens"], 1)

            def k_and_q(b, t):
                e.wait_ge(s["d_lo"], done(b, t))
                e.wait_ge(s["d_kz"], earlier(b, t))
                if t == 0:
                    e.wait_ge(s["b_applied"], done(b, NT - 1))
                kc = A_COLS["k"]
                for i in range(SUB):
                    cols = slice(i * P, (i + 1) * P)
                    last = split_product(e, as_tokens(pairs[1])[:, i, :],
                                         lambda k: p_hi[:, t % 2, k, cols], lambda k: p_lo[:, t % 2, k, cols],
                                         lambda k: wa_hi[:, k, kc:kc + C], lambda k: wa_lo[:, k, kc:kc + C], KC)
                last.then_inc(s["d_kproduct"], 1)
                e.wait_ge(s["d_qparts"], earlier(b, t))
                if t == 0:
                    e.wait_ge(s["b_hi"], done(b, NT - 1))
                for m in range(KC):
                    last = split_product(e, pairs[2][:, m, :], attn_w(wa_hi, "q", m), attn_w(wa_lo, "q", m),
                                         part(p_hi, t), part(p_lo, t), KC)
                last.then_inc(s["d_qproduct"], 1)

            def add_kv(b, t):
                e.wait_ge(s["d_k"], done(b, t))
                e.wait_ge(s["d_vcopied"], done(b, t))
                kvp = pairs[3][:, 0, 0:KC * (P + 1)].rearrange("p (k n) -> p k n", k=KC)
                for i in range(SUB):
                    for k in range(KC):
                        last = e.matmul(kvp[:, k, :], kt[:, t % 2, i, k * P:(k + 1) * P], vt[:, t % 2, i, k, :],
                                        start=(t == 0 and i == 0 and k == 0), stop=(t == NT - 1 and i == SUB - 1),
                                        skip_group_check=True)
                last.then_inc(s["e_kv"], 1)

            def rotate_kv(b, n):
                rotated = pairs[3][:, 1, 0:KC * P].rearrange("p (k n) -> p k n", k=KC)
                before_, source, after = (("e_masked", kvs, "e_rot1"), ("e_kvr", kvr, "e_rot2"))[n]
                e.wait_ge(s["consts_in"], 32)
                e.wait_ge(s[before_], b + 1)
                for k in range(KC):
                    last = e.matmul(rotated[:, k, :], rope[:, n, k, :], source[:, k, :], start=True, stop=True)
                last.then_inc(s[after], 1)

            def denominators(b):
                e.wait_ge(s["d_q"], done(b, NT - 1))
                e.wait_ge(s["e_masked"], b + 1)
                for t in range(NT):
                    for k in range(KC):
                        last = e.matmul(pairs[3][t * HQ:(t + 1) * HQ, 0, :], kden[:, k, :], centre(ph, k, t),
                                        start=(k == 0), stop=(k == KC - 1))
                last.then_inc(s["e_den"], 1)

            def numerators(b, t):
                e.wait_ge(s["e_kve"], b + 1)
                if t == 0:
                    e.wait_ge(s["d_vcopied"], done(b, NT - 1))
                e.wait_ge(s["f_a"], earlier(b, t))
                for k in range(KC):
                    last = e.matmul(pairs[0][:, k, :], kve[:, k, :], centre(ph, k, t), start=True, stop=True)
                last.then_inc(s["f_num"], 1)

            def spread_z(b, t):
                e.wait_ge(s["e_z"], b + 1)
                if t == 0:
                    e.wait_ge(s["d_kz"], done(b, NT - 1))
                e.wait_ge(s["f_z"], earlier(b, t))
                rows = slice(t * HQ, (t + 1) * HQ)
                for k in range(KC):
                    last = e.matmul(pairs[1][:, k, :], expand[rows, k, :], zi[rows, :], start=True, stop=True)
                last.then_inc(s["f_zrows"], 1)

            def out_proj(b, t):
                e.wait_ge(s["f_lo"], done(b, t))
                if t == 0:
                    e.wait_ge(s["d_qparts"], done(b, NT - 1))
                e.wait_ge(s["g_x1"], earlier(b, t))
                for m in range(KC):
                    last = split_product(e, pairs[2][:, m, :], attn_w(wa_hi, "out", m), attn_w(wa_lo, "out", m),
                                         part(p_hi, t), part(p_lo, t), KC)
                last.then_inc(s["g_product"], 1)

            with e.Fori(0, BATCHES) as b:
                with e.If(b < 1):
                    a_channels(b, 0)
                    a_channels(b, 1)
                norm_tokens(b, 0)
                with e.If(b < 1):
                    a_channels(b, 2)
                norm_back(b, 0)
                norm_tokens(b, 1)
                with e.If(b < 1):
                    a_channels(b, 3)
                norm_tokens(b, 2)
                act_proj(b, 0)
                norm_back(b, 1)
                in_proj(b, 0)
                norm_back(b, 2)
                act_proj(b, 1)
                norm_tokens(b, 3)
                in_proj(b, 1)
                act_proj(b, 2)
                norm_back(b, 3)
                in_proj(b, 2)
                act_proj(b, 3)
                k_and_q(b, 0)
                in_proj(b, 3)
                v_tokens(b, 0)
                k_and_q(b, 1)
                v_tokens(b, 1)
                add_kv(b, 0)
                v_tokens(b, 2)
                k_and_q(b, 2)
                v_tokens(b, 3)
                add_kv(b, 1)
                k_and_q(b, 3)
                add_kv(b, 2)
                add_kv(b, 3)
                rotate_kv(b, 0)
                denominators(b)
                rotate_kv(b, 1)
                with e.If(b < BATCHES - 1):
                    e.wait_ge(s["e_den_eps"], b + 1)
                    e.wait_ge(s["e_kve"], b + 1)
                    a_channels(b + 1, 0)
                numerators(b, 0)
                with e.If(b < BATCHES - 1):
                    a_channels(b + 1, 1)
                spread_z(b, 0)
                spread_z(b, 1)
                numerators(b, 1)
                spread_z(b, 2)
                numerators(b, 2)
                spread_z(b, 3)
                out_proj(b, 0)
                numerators(b, 3)
                out_proj(b, 1)
                with e.If(b < BATCHES - 1):
                    a_channels(b + 1, 2)
                out_proj(b, 2)
                with e.If(b < BATCHES - 1):
                    a_channels(b + 1, 3)
                out_proj(b, 3)


def mlp_part(nc, x, rows, w_gated, x1_scratch, xn_scratch, y_scratch, prm, ident, wf, weights, wide_flag, x_hi, x_lo):
    with ExitStack() as ctx:
        def sb(name, shape, dt=F32):
            return ctx.enter_context(nc.sbuf_tensor(name, shape, dt))

        def sem(name):
            return ctx.enter_context(nc.semaphore(name))

        token_banks, back_banks, fc1_banks, fc2_banks = (
            ctx.enter_context(nc.psum_tensor(f"m_banks{i}", [P, 2, TOK], F32)) for i in range(4))

        stage = sb("stage", [P, PIECE])
        low_bits = sb("low_bits", [P, PIECE // 2], I32)
        ones = sb("m_ones", [P, 1])
        small = sb("m_small", [P, 3, SUB])
        w1p = sb("m_w1p", [P, KC])
        xw = sb("xw", [P, KC, TOK + 2])
        x2 = sb("x2", [P, KC, TOK])
        y = sb("m_y", [P, 2, SUB, C])
        fc2_bias = sb("fc2_bias", [P, C])
        xnt = sb("m_xnt", [P, SUB, C])
        xnf = sb("m_xnf", [P, KC, TOK])
        p_hi, p_lo = x_hi, x_lo
        hf = sb("hf", [P, 2, TOK])
        h_hi, h_lo = sb("h_hi", [P, KH, TOK], F32R), sb("h_lo", [P, KH, TOK], F32R)
        st = sb("m_st", [P, SUB, 6])
        mv = sb("m_mv", [P, SUB, 2])
        rs = sb("m_rs", [P, SUB])
        nb = sb("m_nb", [P, SUB])
        bits = sb("bits", [P, 1])
        once = ("bias_in", "xn_in", "xn_split", "ones_set", "centre_taps", "bits_zeroed", "bits_max", "bits_sum",
                "flag_set")
        per_tile = {
            "sync": ("xw_in", "x_in", "w_staged", "w_in", "y_saved"),
            "gpsimd": ("h_var", "h_rstd", "h_mean", "h_scaled", "h_split", "x_biased"),
            "scalar": ("h_centre", "h_applied", "h_hi", "i_gelu"),
            "vector": ("h_left", "h_taps", "h_stats", "h_moments", "h_x2", "i_lo", "i_y", "w_checked"),
            "tensor": ("h_tokens", "h_back", "i_fc1", "i_fc2"),
        }
        s = {name: sem(f"m_{name}") for name in once + sum(per_tile.values(), ())}

        def start_at_one(e, engine):
            for name in per_tile[engine]:
                e.sem_inc(s[name], 1)

        def count(b, t, per_tile=1, more=0):
            return b * (NT * per_tile) + (t * per_tile + more + 1)

        def wait_apart(e, semaphore, value):
            value = e.compute_val(value)
            e.wait_ge(s["bias_in"], 16)
            e.wait_ge(semaphore, value)

        def par(name, i):
            return parameter(prm, name, i)

        block = ctx.enter_context(nc.Block())

        @block.sync
        def _(sp):
            start_at_one(sp, "sync")

            def load_window(b, t):
                sp.dma_start(xw[:], x1_scratch[b][:, :, t * TOK:(t + 1) * TOK + 2]).then_inc(s["xw_in"], 16)

            def following(b, step, records):
                return nc.s_assert_within(b + step, 0, records - 1,
                                          skip_runtime_bounds_check_because="the branch excludes the last batch")

            def load_x(g, slot):
                sp.dma_start(y[:, slot], x[g]).then_inc(s["x_in"], 16)

            load_window(0, 0)
            sp.dma_start(fc2_bias[:], rows[:, C:2 * C]).then_inc(s["bias_in"], 16)
            load_x(0, 0)
            sp.dma_start(stage[:], w_gated[0]).then_inc(s["w_staged"], 16)
            sp.wait_ge(s["h_taps"], 2)
            load_window(0, 1)

            with sp.Fori(0, BATCHES) as b:
                for t in range(NT):
                    wait_apart(sp, s["x_biased"], count(b, t + 1))
                    wait_apart(sp, s["y_saved"], count(b, t, 16))
                    if t + 1 < NT:
                        load_x(b * NT + (t + 1), (t + 1) % 2)
                    else:
                        with sp.If(b < BATCHES - 1):
                            load_x(following(b * NT, NT, TILES), 0)
                    if t + 2 < NT:
                        wait_apart(sp, s["h_taps"], count(b, t + 2))
                        load_window(b, t + 2)
                    else:
                        with sp.If(b < BATCHES - 1):
                            wait_apart(sp, s["h_taps"], count(b, t + 2))
                            load_window(following(b, 1, BATCHES), t + 2 - NT)
                        if t + 1 == NT:
                            with sp.Else():
                                sp.wait_ge(s["h_split"], TILES + 1)
                                sp.dma_start(xnf[:], xn_scratch[0]).then_inc(s["xn_in"], 16)
                    wait_apart(sp, s["w_staged"], count(b, t, 16, 16))
                    sp.dma_start(weights[:, b * NT + t, :].bitcast(F32), stage[:]).then_inc(s["w_in"], 16)
                    wait_apart(sp, s["w_in"], count(b, t, 16, 16))
                    if t + 1 < NT:
                        sp.dma_start(stage[:], w_gated[b * NT + (t + 1)]).then_inc(s["w_staged"], 16)
                    else:
                        with sp.If(b < BATCHES - 1):
                            sp.dma_start(stage[:], w_gated[following(b * NT, NT, TILES)]).then_inc(s["w_staged"], 16)
                    wait_apart(sp, s["i_y"], count(b, t + 1))
                    sp.dma_start(y_scratch[b * NT + t], y[:, t % 2]).then_inc(s["y_saved"], 16)
            sp.wait_ge(s["y_saved"], 16 * TILES + 1)

        @block.gpsimd
        def _(pool):
            start_at_one(pool, "gpsimd")
            pool.memset(small[:, 0, :], EPS)
            pool.memset(small[:, 1, :], -0.5)
            pool.memset(small[:, 2, :], -1.0)
            pool.memset(ones[:], 1.0).then_inc(s["ones_set"], 1)

            def scalars(n):
                pool.wait_ge(s["ones_set"], 1)
                pool.wait_ge(s["h_moments"], n)
                pool.wait_ge(s["h_applied"], n - 1)
                pool.tensor_tensor(rs[:], mv[:, :, 1], small[:, 0, :], ALU.add).then_inc(s["h_var"], 1)
                pool.wait_ge(s["h_var"], n)
                pool.tensor_tensor(rs[:], rs[:], small[:, 1, :], ALU.pow).then_inc(s["h_rstd"], 1)
                pool.wait_ge(s["h_rstd"], n)
                pool.tensor_tensor(nb[:], mv[:, :, 0], rs[:], ALU.mult).then_inc(s["h_mean"], 1)
                pool.wait_ge(s["h_mean"], n)
                pool.tensor_tensor(nb[:], nb[:], small[:, 2, :], ALU.mult).then_inc(s["h_scaled"], 1)

            def bias(n, slot):
                pool.wait_ge(s["bias_in"], 16)
                pool.wait_ge(s["x_in"], n * 16 - 15)
                pool.tensor_tensor(y[:, slot], y[:, slot], fc2_bias[:].unsqueeze(1).to_broadcast([P, SUB, C]),
                                   ALU.add).then_inc(s["x_biased"], 1)

            def low_part(n):
                pool.wait_ge(s["h_hi"], n)
                pool.tensor_tensor(p_lo[:], xnf[:], p_hi[:].bitcast(F32), ALU.subtract).then_inc(s["h_split"], 1)

            def norm(n, slot):
                scalars(n)
                bias(n, slot)
                low_part(n)

            norm(2, 0)
            with pool.Fori(0, BATCHES) as b:
                for t in range(NT):
                    if t + 1 < NT:
                        norm(count(b, t + 2), (t + 1) % 2)
                    else:
                        with pool.If(b < BATCHES - 1):
                            norm(count(b, t + 2), (t + 1) % 2)
                        with pool.Else():
                            pool.wait_ge(s["h_hi"], TILES + 2)
                            pool.tensor_tensor(x_lo[:], xnf[:], x_hi[:].bitcast(F32), ALU.subtract) \
                                .then_inc(s["xn_split"], 1)

        @block.scalar
        def _(e):
            start_at_one(e, "scalar")
            e.wait_ge(s["centre_taps"], 1)

            def centre(n):
                e.wait_ge(s["xw_in"], n * 16 - 15)
                e.wait_ge(s["h_tokens"], n - 1)
                for k in range(KC):
                    last = e.activation(x2[:, k, :], xw[:, k, 1:TOK + 1], ACT.Identity,
                                        bias=par("cpe2_b", k), scale=w1p[:, k:k + 1])
                last.then_inc(s["h_centre"], 1)

            def apply_norm(n):
                e.wait_ge(s["h_scaled"], n)
                e.wait_ge(s["h_back"], n - 1)
                tokens = as_tokens(token_banks)
                for i in range(SUB):
                    last = e.activation(xnt[:, i, :], tokens[:, i, :], ACT.Identity, bias=nb[:, i:i + 1],
                                        scale=rs[:, i:i + 1])
                last.then_inc(s["h_applied"], 1)

            def gain_and_split(n):
                e.wait_ge(s["h_back"], n)
                e.wait_ge(s["h_split"], n - 1)
                for buf in (xnf, p_hi):
                    for k in range(KC):
                        last = e.activation(buf[:, k, :], back_banks[:, k, :], ACT.Identity,
                                            bias=par("norm2_b", k), scale=par("norm2_g", k))
                last.then_inc(s["h_hi"], 1)

            def gelu(b, t, m):
                e.wait_ge(s["i_fc1"], count(b, t, KH, m + 1))
                e.wait_ge(s["i_lo"], count(b, t, KH, max(m - 1, 0)))
                if m == 0:
                    e.wait_ge(s["i_fc2"], count(b, t))
                for out in (hf[:, m % 2, :], h_hi[:, m, :]):
                    last = e.activation(out, fc1_banks[:, m % 2, :], ACT.Gelu, bias=par("fc1_b", m))
                last.then_inc(s["i_gelu"], 1)

            centre(2)
            apply_norm(2)
            gain_and_split(2)
            centre(3)
            with e.Fori(0, BATCHES) as b:
                for t in range(NT):
                    for m in range(KH):
                        gelu(b, t, m)
                        if m == 5:
                            if t + 1 < NT:
                                apply_norm(count(b, t + 2))
                            else:
                                with e.If(b < BATCHES - 1):
                                    apply_norm(count(b, t + 2))
                    if t + 2 < NT:
                        gain_and_split(count(b, t + 2))
                        centre(count(b, t + 3))
                    elif t + 2 == NT:
                        gain_and_split(count(b, t + 2))
                        with e.If(b < BATCHES - 1):
                            centre(count(b, t + 3))
                    else:
                        with e.If(b < BATCHES - 1):
                            gain_and_split(count(b, t + 2))
                            centre(count(b, t + 3))
                        with e.Else():
                            e.wait_ge(s["xn_in"], 16)
                            e.wait_ge(s["i_fc1"], TILES * KH + 1)
                            e.copy(x_hi[:], xnf[:]).then_inc(s["h_hi"], 1)

        @block.vector
        def _(e):
            start_at_one(e, "vector")
            at_ = PARAMS["cpe2_w1"][0]
            e.tensor_scalar(w1p[:], prm[:, at_:at_ + KC], 1.0, None, ALU.add).then_inc(s["centre_taps"], 1)
            e.memset(low_bits[:], 0).then_inc(s["bits_zeroed"], 1)

            def side_taps(n):
                e.wait_ge(s["h_centre"], n)
                for tap, name, signal in ((0, "cpe2_w0", "h_left"), (2, "cpe2_w2", "h_taps")):
                    if tap == 2:
                        e.wait_ge(s["h_left"], n)
                    for k in range(KC):
                        last = e.scalar_tensor_tensor(out=x2[:, k, :], in0=xw[:, k, tap:tap + TOK],
                                                      scalar=par(name, k), in1=x2[:, k, :],
                                                      op0=ALU.mult, op1=ALU.add)
                    last.then_inc(s[signal], 1)

            def moments(n):
                wait_apart(e, s["h_tokens"], n)
                e.wait_ge(s["h_moments"], n - 1)
                for i in range(SUB):
                    last = e.bn_stats(st[:, i, :], as_tokens(token_banks)[:, i, :])
                last.then_inc(s["h_stats"], 1)
                wait_apart(e, s["h_scaled"], n - 1)
                e.wait_ge(s["h_stats"], n)
                for i in range(SUB):
                    last = e.bn_aggr(mv[:, i, :], st[:, i, :])
                last.then_inc(s["h_moments"], 1)

            def add_x2(n, slot):
                e.wait_ge(s["x_biased"], n)
                e.wait_ge(s["h_applied"], n)
                e.tensor_tensor(y[:, slot], as_tokens(token_banks), y[:, slot], ALU.add).then_inc(s["h_x2"], 1)

            def check(piece, n):
                e.wait_ge(s["w_in"], n * 16 + 1)
                for half in range(2):
                    columns_ = weights[:, piece, half * (PIECE // 2):(half + 1) * (PIECE // 2)].bitcast(I32)
                    e.wait_ge(s["w_checked"], n * 2 + (half - 1))
                    e.scalar_tensor_tensor(out=low_bits[:], in0=columns_, scalar=0xFFF, in1=low_bits[:],
                                           op0=ALU.bitwise_and, op1=ALU.bitwise_or).then_inc(s["w_checked"], 1)

            side_taps(2)
            moments(2)
            add_x2(2, 0)
            side_taps(3)
            with e.Fori(0, BATCHES) as b:
                for t in range(NT):
                    for m in range(KH):
                        e.wait_ge(s["i_gelu"], count(b, t, KH, m + 1))
                        if m == 0:
                            e.wait_ge(s["i_fc2"], count(b, t))
                        e.tensor_tensor(h_lo[:, m, :], hf[:, m % 2, :], h_hi[:, m, :].bitcast(F32), ALU.subtract) \
                            .then_inc(s["i_lo"], 1)
                        if m == 2:
                            if t + 1 < NT:
                                moments(count(b, t + 2))
                            else:
                                with e.If(b < BATCHES - 1):
                                    moments(count(b, t + 2))
                    if t + 1 < NT:
                        add_x2(count(b, t + 2), (t + 1) % 2)
                    else:
                        with e.If(b < BATCHES - 1):
                            add_x2(count(b, t + 2), (t + 1) % 2)
                    check(b * NT + t, b * NT + (t + 1))
                    if t + 2 < NT:
                        side_taps(count(b, t + 3))
                    else:
                        with e.If(b < BATCHES - 1):
                            side_taps(count(b, t + 3))
                    e.wait_ge(s["i_fc2"], count(b, t + 1))
                    e.wait_ge(s["h_x2"], count(b, t + 1))
                    e.tensor_tensor(y[:, t % 2], as_tokens(fc2_banks), y[:, t % 2], ALU.add).then_inc(s["i_y"], 1)
            e.wait_ge(s["w_checked"], 2 * TILES + 1)
            e.tensor_reduce(bits[:], low_bits[:], AX_X, ALU.max).then_inc(s["bits_max"], 1)
            e.wait_ge(s["bits_sum"], 1)
            e.tensor_reduce(wide_flag[:], token_banks[0:1, 0, 0:1], AX_X, ALU.max).then_inc(s["flag_set"], 1)

        @block.tensor
        def _(e):
            start_at_one(e, "tensor")

            def norm_tokens(n):
                e.wait_ge(s["h_taps"], n)
                e.wait_ge(s["h_applied"], n - 1)
                e.wait_ge(s["h_x2"], n - 1)
                to_tokens(e, token_banks, lambda k: x2[:, k, :], ident[:]).then_inc(s["h_tokens"], 1)

            def norm_back(n):
                e.wait_ge(s["h_applied"], n)
                e.wait_ge(s["h_hi"], n - 1)
                to_channels(e, back_banks, lambda i: xnt[:, i, :], ident[:]).then_inc(s["h_back"], 1)

            norm_tokens(2)
            norm_back(2)
            with e.Fori(0, BATCHES) as b:
                for t in range(NT):
                    e.wait_ge(s["h_split"], count(b, t + 1))
                    for m in range(KH):
                        e.wait_ge(s["i_gelu"], count(b, t, KH, max(m - 1, 0)))
                        split_product(e, fc1_banks[:, m % 2, :], lambda k: wf["wf1_hi"][:, k, m * P:(m + 1) * P],
                                      lambda k: wf["wf1_lo"][:, k, m * P:(m + 1) * P], lambda k: p_hi[:, k, :],
                                      lambda k: p_lo[:, k, :], KC).then_inc(s["i_fc1"], 1)
                        if m == 1:
                            if t + 1 < NT:
                                norm_tokens(count(b, t + 2))
                            else:
                                with e.If(b < BATCHES - 1):
                                    norm_tokens(count(b, t + 2))
                    if t + 1 < NT:
                        norm_back(count(b, t + 2))
                    else:
                        with e.If(b < BATCHES - 1):
                            norm_back(count(b, t + 2))
                    e.wait_ge(s["i_y"], count(b, t))
                    for i in range(SUB):
                        cols = slice(i * P, (i + 1) * P)
                        for k in range(KH):
                            if i == 0:
                                e.wait_ge(s["i_lo"], count(b, t, KH, k + 1))
                            for n, (v, w) in enumerate(((h_hi, "wf2_hi"), (h_lo, "wf2_hi"), (h_hi, "wf2_lo"))):
                                last = e.matmul(as_tokens(fc2_banks)[:, i, :], v[:, k, cols], wf[w][:, k, :],
                                                start=(k == 0 and n == 0), stop=(k == KH - 1 and n == 2))
                    last.then_inc(s["i_fc2"], 1)
            e.wait_ge(s["h_applied"], TILES + 1)
            e.wait_ge(s["h_x2"], TILES + 1)
            e.wait_ge(s["bits_max"], 1)
            e.matmul(token_banks[0:1, 0, 0:1], ones[:], bits[:], start=True, stop=True).then_inc(s["bits_sum"], 1)


def gated_part(nc, rows, prm, wf, weights, wide_flag, x_hi, x_lo, xn_scratch, y_scratch, out):
    with ExitStack() as ctx:
        def sb(name, shape, dt=F32):
            return ctx.enter_context(nc.sbuf_tensor(name, shape, dt))

        def sem(name):
            return ctx.enter_context(nc.semaphore(name))

        banks = [ctx.enter_context(nc.psum_tensor(f"g_banks{i}", [P, 2, TOK], F32)) for i in range(4)]
        gate_banks, up_banks, layer_banks, down_banks = banks
        hidden_banks = [layer_banks[:, 0, :], layer_banks[:, 1, :], gate_banks[:, 0, :], gate_banks[:, 1, :]]

        flat = weights[:].rearrange("p t n -> p (t n)")
        W, at_column = {}, 0
        for name, k, width in GATED_LAYERS:
            W[name] = flat[:, at_column:at_column + k * width].rearrange("p (k n) -> p k n", k=k)
            at_column += k * width
        down_scale = sb("down_scale", [P, C])
        xn = sb("g_xn", [P, KC, TOK])
        a_hi, a_lo = (part_.rearrange("p (k n) -> p k n", k=KH) for part_ in (wf["all"][:, 0], wf["all"][:, 1]))
        b_hi, b_lo = sb("b_hi", [P, KH, TOK], F32R), sb("b_lo", [P, KH, TOK], F32R)
        silu = sb("g_silu", [P, 2, TOK])
        full = sb("full", [P, 2, TOK])
        y = sb("y", [P, SUB, C])
        ot = sb("g_ot", [P, SUB, C])

        once = ("scale_in",)
        per_tile = {
            "sync": ("xn_in", "y_in", "out_stored"),
            "gpsimd": ("x_split",),
            "scalar": ("x_hi_done", "silu_done", "u_hi", "h1_gelu", "h2_gelu"),
            "vector": ("gated", "u_lo", "h1_lo", "h2_lo", "scaled", "out_sum"),
            "tensor": ("gate_mm", "up_mm", "h1_mm", "h2_mm", "down_mm"),
        }
        s = {name: sem(f"g_{name}") for name in once + sum(per_tile.values(), ())}

        def start_at_one(e, engine):
            for name in per_tile[engine]:
                e.sem_inc(s[name], 1)

        def count(g, per_tile, more=0):
            return g * per_tile + (more + 1)

        def wait_apart(e, semaphore, value):
            count = e.compute_val(value)
            e.wait_ge(s["scale_in"], 16)
            e.wait_ge(semaphore, count)

        def par(name, i):
            return parameter(prm, name, i)

        block = ctx.enter_context(nc.Block())

        @block.sync
        def _(sp):
            start_at_one(sp, "sync")
            sp.sem_inc(s["xn_in"], 16)
            sp.dma_start(down_scale[:], rows[:, 2 * C:3 * C]).then_inc(s["scale_in"], 16)
            with sp.Fori(0, TILES) as g:
                wait_apart(sp, s["x_split"], count(g, 1, 1))
                with sp.If(g < TILES - 1):
                    next_ = nc.s_assert_within(g + 1, 0, TILES - 1,
                                               skip_runtime_bounds_check_because="the branch excludes the last tile")
                    sp.dma_start(xn[:], xn_scratch[next_]).then_inc(s["xn_in"], 16)
                wait_apart(sp, s["out_sum"], count(g, 1))
                sp.dma_start(y[:], y_scratch[g]).then_inc(s["y_in"], 16)
                wait_apart(sp, s["out_sum"], count(g, 1, 1))
                sp.dma_start(out[g], ot[:]).then_inc(s["out_stored"], 16)
            sp.wait_ge(s["out_stored"], 16 * TILES + 1)

        @block.gpsimd
        def _(pool):
            start_at_one(pool, "gpsimd")

            def low_of_x(n):
                pool.wait_ge(s["x_hi_done"], n)
                pool.tensor_tensor(x_lo[:], xn[:], x_hi[:].bitcast(F32), ALU.subtract).then_inc(s["x_split"], 1)

            pool.sem_inc(s["x_split"], 1)
            with pool.Fori(0, TILES - 1) as g:
                low_of_x(g + 3)

        @block.scalar
        def _(e):
            start_at_one(e, "scalar")

            def high_of_x(n):
                e.wait_ge(s["xn_in"], n * 16 - 15)
                e.wait_ge(s["up_mm"], n * KH - (2 * KH - 1))
                e.copy(x_hi[:], xn[:]).then_inc(s["x_hi_done"], 1)

            def gelu(g, m, mm, done, low, out_hi, scale):
                e.wait_ge(s[mm], count(g, KH, m + 1))
                e.wait_ge(s[low], count(g, KH, max(m - 1, 0)))
                for out_ in (full[:, m % 2, :], out_hi[:, m, :]):
                    last = e.activation(out_, hidden_banks[m % 4], ACT.Gelu, scale=par(scale, m))
                last.then_inc(s[done], 1)

            def high_of_gated(g, m):
                e.wait_ge(s["gated"], count(g, KH, m + 1))
                if m == 0:
                    e.wait_ge(s["down_mm"], count(g, 1))
                e.copy(a_hi[:, m, :], full[:, m % 2, :]).then_inc(s["u_hi"], 1)

            e.sem_inc(s["x_hi_done"], 1)
            with e.Fori(0, TILES) as g:
                for m in range(KH):
                    e.wait_ge(s["gate_mm"], count(g, KH, m + 1))
                    e.wait_ge(s["gated"], count(g, KH, max(m - 1, 0)))
                    e.activation(silu[:, m % 2, :], gate_banks[:, m % 2, :], ACT.Silu, scale=par("w1_s", m)) \
                        .then_inc(s["silu_done"], 1)
                    if m >= 1:
                        high_of_gated(g, m - 1)
                high_of_gated(g, KH - 1)
                e.wait_ge(s["h2_mm"], count(g, KH))
                e.wait_ge(s["u_lo"], count(g, KH, KH))
                for m in range(KH):
                    gelu(g, m, "h1_mm", "h1_gelu", "h1_lo", b_hi, "h1_s")
                    if m == 3:
                        with e.If(g < TILES - 1):
                            high_of_x(g + 3)
                e.wait_ge(s["h1_mm"], count(g, KH, KH))
                e.wait_ge(s["h1_lo"], count(g, KH, KH))
                for m in range(KH):
                    gelu(g, m, "h2_mm", "h2_gelu", "h2_lo", a_hi, "h2_s")

        @block.vector
        def _(e):
            start_at_one(e, "vector")
            def low(g, m, out_lo, out_hi, ready, after):
                e.wait_ge(s[ready], count(g, KH, m + 1))
                e.tensor_tensor(out_lo[:, m, :], full[:, m % 2, :], out_hi[:, m, :].bitcast(F32), ALU.subtract) \
                    .then_inc(s[after], 1)

            with e.Fori(0, TILES) as g:
                for m in range(KH):
                    e.wait_ge(s["up_mm"], count(g, KH, m + 1))
                    e.wait_ge(s["silu_done"], count(g, KH, m + 1))
                    if m == 0:
                        e.wait_ge(s["h2_lo"], count(g, KH))
                        e.wait_ge(s["down_mm"], count(g, 1))
                    else:
                        e.wait_ge(s["u_lo"], count(g, KH, max(m - 1, 0)))
                        e.wait_ge(s["u_hi"], count(g, KH, max(m - 1, 0)))
                    e.scalar_tensor_tensor(out=full[:, m % 2, :], in0=up_banks[:, m % 2, :], scalar=par("w2_s", m),
                                           in1=silu[:, m % 2, :], op0=ALU.mult, op1=ALU.mult).then_inc(s["gated"], 1)
                    if m >= 1:
                        low(g, m - 1, a_lo, a_hi, "u_hi", "u_lo")
                low(g, KH - 1, a_lo, a_hi, "u_hi", "u_lo")
                e.wait_ge(s["h2_mm"], count(g, KH))
                for m in range(KH):
                    low(g, m, b_lo, b_hi, "h1_gelu", "h1_lo")
                for m in range(KH):
                    low(g, m, a_lo, a_hi, "h2_gelu", "h2_lo")
                e.wait_ge(s["out_stored"], count(g, 16))
                e.wait_ge(s["down_mm"], count(g, 1, 1))
                e.tensor_tensor(ot[:], as_tokens(down_banks), down_scale[:].unsqueeze(1).to_broadcast([P, SUB, C]),
                                ALU.mult).then_inc(s["scaled"], 1)
                e.wait_ge(s["y_in"], count(g, 16, 16))
                e.wait_ge(s["scaled"], count(g, 1, 1))
                e.tensor_tensor(ot[:], ot[:], y[:], ALU.add).then_inc(s["out_sum"], 1)

        @block.tensor
        def _(e):
            start_at_one(e, "tensor")

            def add(bank, w, v, wide, first, last):
                dt = F32 if wide else F32R
                return e.matmul(bank, w.bitcast(dt), v.bitcast(dt), start=first, stop=last)

            def first_layer(g, wide):
                e.wait_ge(s["x_split"], count(g, 1, 1))
                e.wait_ge(s["h2_gelu"], count(g, KH))
                for m in range(KH):
                    cols = slice(m * P, (m + 1) * P)
                    for name, bank, reader, signal in (("gate", gate_banks, "silu_done", "gate_mm"),
                                                       ("up", up_banks, "gated", "up_mm")):
                        e.wait_ge(s[reader], count(g, KH, max(m - 1, 0)))
                        for k in range(KC):
                            for n, v in enumerate((x_hi, x_lo)):
                                last = add(bank[:, m % 2, :], W[name][:, k, cols], v[:, k, :], wide,
                                           k == 0 and n == 0, k == KC - 1 and n == 1)
                        last.then_inc(s[signal], 1)

            def hidden_layer(g, wide, w, hi, lo, inputs, gelu, mm):
                for ms in [(0, 1)] + [(m,) for m in range(2, KH)]:
                    e.wait_ge(s[gelu], count(g, KH, max(ms[-1] - 3, 0)))
                    for k in range(KH):
                        if ms[0] == 0:
                            e.wait_ge(s[inputs], count(g, KH, k + 1))
                        for m in ms:
                            for n, v in enumerate((hi, lo)):
                                last = add(hidden_banks[m % 4], w[:, k, m * P:(m + 1) * P], v[:, k, :], wide,
                                           k == 0 and n == 0, k == KH - 1 and n == 1)
                            if k == KH - 1:
                                last.then_inc(s[mm], 1)

            def last_layer(g, wide):
                e.wait_ge(s["scaled"], count(g, 1))
                for groups in ((0, 2), (1, 3)):
                    for k in range(KH):
                        if groups[0] == 0:
                            e.wait_ge(s["h2_lo"], count(g, KH, k + 1))
                        for i in groups:
                            for n, v in enumerate((a_hi, a_lo)):
                                last = add(as_tokens(down_banks)[:, i, :], v[:, k, i * P:(i + 1) * P], W["down"][:, k, :],
                                           wide, k == 0 and n == 0, k == KH - 1 and n == 1)
                last.then_inc(s["down_mm"], 1)

            def all_tiles(wide):
                with e.Fori(0, TILES) as g:
                    first_layer(g, wide)
                    e.wait_ge(s["silu_done"], count(g, KH, KH))
                    hidden_layer(g, wide, W["h1"], a_hi, a_lo, "u_lo", "h1_gelu", "h1_mm")
                    e.wait_ge(s["h1_gelu"], count(g, KH, KH - 2))
                    hidden_layer(g, wide, W["h2"], b_hi, b_lo, "h1_lo", "h2_gelu", "h2_mm")
                    last_layer(g, wide)

            flag = e.value_load(wide_flag[0:1, 0:1])
            with e.If(flag > 0):
                all_tiles(True)
            with e.Else():
                all_tiles(False)


def build(nc, t):
    x = t["x"].rearrange("g (s p) c -> g p s c", p=P)
    out = t["out"].rearrange("g (s p) c -> g p s c", p=P)
    xn_scratch = nc.dram_tensor("xn_scratch", (TILES, P, KC, TOK), F32, kind="Internal").ap()
    x1_scratch = nc.dram_tensor("x1_scratch", (BATCHES, P, KC, N + 2), F32, kind="Internal").ap()
    y_scratch = nc.dram_tensor("y_scratch", (TILES, P, SUB, C), F32, kind="Internal").ap()
    with nc.sbuf_tensor("prm", [P, N_PARAMS], F32) as prm, nc.sbuf_tensor("identity", [P, P], F32) as ident, \
            nc.sbuf_tensor("mlp_weights", [P, 2, 2 * KC * HID], F32R) as mlp_weights:
        wf = {"all": mlp_weights}
        for i, part_ in enumerate(("hi", "lo")):
            wf["wf1_" + part_] = mlp_weights[:, i, 0:KC * HID].rearrange("p (k n) -> p k n", k=KC)
            wf["wf2_" + part_] = mlp_weights[:, i, KC * HID:].rearrange("p (k n) -> p k n", k=KH)
        attention_part(nc, x, t["params"], t["consts"], t["rows"], t["w_attn"], t["w_fc1"], t["w_fc2"], prm, ident, wf,
                       xn_scratch, x1_scratch)
        with nc.sbuf_tensor("gated_weights", [P, TILES, PIECE], F32R) as weights, \
                nc.sbuf_tensor("wide_flag", [1, 1], I32) as wide_flag, \
                nc.sbuf_tensor("x_hi", [P, KC, TOK], F32R) as x_hi, nc.sbuf_tensor("x_lo", [P, KC, TOK], F32R) as x_lo:
            mlp_part(nc, x, t["rows"], t["w_gated"], x1_scratch, xn_scratch, y_scratch, prm, ident, wf, weights,
                     wide_flag, x_hi, x_lo)
            gated_part(nc, t["rows"], prm, wf, weights, wide_flag, x_hi, x_lo, xn_scratch, y_scratch, out)


def chunked(w):
    w = np.asarray(w)
    return np.ascontiguousarray(w.reshape(w.shape[0] // P, P, w.shape[1]).transpose(1, 0, 2))


def columns(v):
    v = np.asarray(v)
    return v.reshape(-1, P).T


def kernel(**inputs):
    import concourse.bacc as bacc
    from concourse.bass_utils import run_bass_kernel_spmd as run

    a = {k.removeprefix("L0_attn_"): np.asarray(v) for k, v in inputs.items() if k.startswith("L0_attn_")}
    f = {k.removeprefix("L0_ffn_"): np.asarray(v) for k, v in inputs.items() if k.startswith("L0_ffn_")}
    vectors = {}
    for conv in ("cpe1", "dwc", "lepe", "cpe2"):
        for tap in range(3):
            vectors[f"{conv}_w{tap}"] = a[f"{conv}_w"][:, 0, tap]
        vectors[f"{conv}_b"] = a[f"{conv}_b"]
    for name in ("norm1_g", "norm1_b", "in_b", "actp_b", "out_b", "norm2_g", "norm2_b", "fc1_b"):
        vectors[name] = a[name]
    vectors["q_b"] = a["qk_b"][:C]
    for name in ("w1_s", "w2_s", "h1_s", "h2_s"):
        vectors[name] = f[name]
    arrays = {
        "x": a["x"].reshape(TILES, TOK, C),
        "params": np.concatenate([columns(vectors[name]) for name in PARAMS], axis=1),
        "consts": constants(),
        "rows": np.concatenate([np.tile(v[None, :], (P, 1)) for v in (a["qk_b"][C:], a["fc2_b"], f["w3_s"])], axis=1),
        "w_attn": chunked(np.concatenate([a["actp_w"], a["in_w"], a["qk_w"], a["out_w"]], axis=1)),
        "w_fc1": chunked(a["fc1_w"]),
        "w_fc2": chunked(a["fc2_w"]),
        "w_gated": np.concatenate(
            [chunked(f[f"{w}_w"].T).reshape(P, -1) for w in ("w1", "w2", "h1", "h2", "w3")], axis=1)
        .reshape(P, TILES, PIECE).transpose(1, 0, 2),
    }
    arrays = {k: np.ascontiguousarray(v) for k, v in arrays.items()}
    nc = bacc.Bacc("TRN2", target_bir_lowering=False, num_devices=1)
    t = {k: nc.dram_tensor(k, v.shape, mybir.dt.from_np(v.dtype), kind="ExternalInput").ap()
         for k, v in arrays.items()}
    t["out"] = nc.dram_tensor("out", (TILES, TOK, C), F32, kind="ExternalOutput").ap()
    build(nc, t)
    r = run(nc, [arrays], core_ids=[0])
    return r.results[0]["out"].reshape(BATCHES, N, C)
```
